# Optimizing a Trainium2 kernel written in Bass

```python
import numpy as np
import jax
import jax.numpy as jnp

def _softmax(x, axis=-1):
    return jax.nn.softmax(x, axis=axis)

def _gelu(x):
    return jax.nn.gelu(x, approximate=True)

def _silu(x):
    return jax.nn.silu(x)

def _sigmoid(x):
    return jax.nn.sigmoid(x)

def _layernorm(x, axis=-1, eps=1e-05):
    m = jnp.mean(x, axis=axis, keepdims=True)
    v = jnp.var(x, axis=axis, keepdims=True)
    return (x - m) / jnp.sqrt(v + eps)

def _scatter_add(tgt, idx, src, axis=0):
    return tgt.at[idx].add(src)

def _segment_sum(src, seg, n):
    return jax.ops.segment_sum(src, seg, n)
kernel_name = 'mk_gnn_preln_d2_gnn_r8_d529f2'

def setup_inputs(seed: int=0):
    np.random.seed(seed)
    _w = jnp.asarray

    def _rec_inputs():
        import jax
        import jax.numpy as jnp
        _gk = jax.random.key(seed)
        x = -0.0002117 + 1 * jax.random.normal(jax.random.fold_in(_gk, 1), (6250, 512), jnp.float32)
        src = jax.random.randint(jax.random.fold_in(_gk, 2), (100000,), 0, 6250, jnp.int32)
        dst = jnp.minimum((6250 * jax.random.uniform(jax.random.fold_in(_gk, 3), (100000,)) ** 2.0).astype(jnp.int32), 49999)
        _o = jnp.argsort(dst, stable=True)
        src = src[_o]
        dst = dst[_o]
        return (x, src, dst)
    x, src, dst = _rec_inputs()

    def _L0_gnn_setup():
        import jax, jax.numpy as jnp
        import numpy as np
        N_NODES = 6250
        N_EDGES = 200000
        N_HEADS = 8
        IN_DIM = 512
        OUT_DIM = 64
        LRELU_ALPHA = 0.2
        key = jax.random.key(seed)
        k1, k2, k3, k4, k5 = jax.random.split(key, 5)
        x = jax.random.normal(k1, (N_NODES, IN_DIM), dtype=jnp.float32)
        W = jax.random.normal(k2, (N_HEADS, IN_DIM, OUT_DIM), dtype=jnp.float32) * (1.0 / np.sqrt(IN_DIM))
        att_w = jax.random.normal(k3, (N_HEADS, 2 * OUT_DIM), dtype=jnp.float32) * (1.0 / np.sqrt(2 * OUT_DIM))
        src = jax.random.randint(k4, (N_EDGES,), 0, N_NODES, dtype=jnp.int64 if jax.config.read('jax_enable_x64') else jnp.int32).astype(jnp.int32)
        dst = jax.random.randint(k5, (N_EDGES,), 0, N_NODES, dtype=jnp.int32)
        return {'x': x, 'W': W, 'att_w': att_w, 'src': src, 'dst': dst}
    _L0_gnn_all = _L0_gnn_setup()
    _L0_gnn_in = {k: v for k, v in _L0_gnn_all.items() if k in ('W', 'att_w')}
    del _L0_gnn_all

    def _L1_gnn_setup():
        import jax, jax.numpy as jnp
        import numpy as np
        B = 32
        MAXN = 256
        HEADS = 8
        DH = 64
        M = 256
        D = 512
        EPS = 1e-05
        KEPS = 1e-06

        def _batchnorm(x, g, b):
            mu = jnp.mean(x, axis=0)
            var = jnp.mean((x - mu) ** 2, axis=0)
            return (x - mu) * jax.lax.rsqrt(var + EPS) * g + b

        def _forward(x, batch, edge_index, norm1_g, norm1_b, norm2_g, norm2_b, W_conv, b_conv, Wq, Wk, Wv, Wo, proj):
            N = x.shape[0]
            E = edge_index.shape[1]
            h = x
            xn = _batchnorm(x, norm1_g, norm1_b)
            msg = xn[edge_index[0]]
            agg = jax.ops.segment_sum(msg, edge_index[1], num_segments=N)
            deg = jax.ops.segment_sum(jnp.ones((E,), x.dtype), edge_index[1], num_segments=N)
            agg = agg / jnp.maximum(deg, 1.0)[:, None]
            conv_out = jax.nn.relu(agg @ W_conv + b_conv)
            counts = jax.ops.segment_sum(jnp.ones((N,), jnp.int32), batch, num_segments=B)
            offsets = jnp.concatenate([jnp.zeros((1,), jnp.int32), jnp.cumsum(counts)[:-1]])
            pos = jnp.arange(N, dtype=jnp.int32) - offsets[batch]
            h_dense = jnp.zeros((B, MAXN, D), x.dtype).at[batch, pos].set(h)
            mask = jnp.zeros((B, MAXN), bool).at[batch, pos].set(True)

            def heads(t, W):
                return (t @ W).reshape(B, MAXN, HEADS, DH).transpose(0, 2, 1, 3)
            q, k, v = (heads(h_dense, Wq), heads(h_dense, Wk), heads(h_dense, Wv))
            scale = DH ** (-0.25)

            def phi(t, is_query):
                t = t * scale
                u = jnp.einsum('bhnd,md->bhnm', t, proj)
                diag = 0.5 * jnp.sum(t * t, axis=-1, keepdims=True)
                if is_query:
                    m_ = jnp.max(u, axis=-1, keepdims=True)
                else:
                    m_ = jnp.max(u, axis=(-2, -1), keepdims=True)
                return jnp.exp(u - diag - jax.lax.stop_gradient(m_)) / np.sqrt(M) + KEPS
            qf = phi(q, True)
            kf = phi(k, False) * mask[:, None, :, None]
            vm = v * mask[:, None, :, None]
            kv = jnp.einsum('bhnm,bhnd->bhmd', kf, vm)
            z = 1.0 / (jnp.einsum('bhnm,bhm->bhn', qf, kf.sum(axis=2)) + KEPS)
            attn = jnp.einsum('bhnm,bhmd->bhnd', qf, kv) * z[..., None]
            attn = attn.transpose(0, 2, 1, 3).reshape(B, MAXN, D) @ Wo
            h_attn = attn[batch, pos]
            return _batchnorm(conv_out + h_attn + h, norm2_g, norm2_b)
        key = jax.random.key(seed)
        ks = jax.random.split(key, 10)
        sizes = 1024 + np.arange(B) * 131 % 1025
        N = int(sizes.sum())
        E = N * 8
        batch = jnp.asarray(np.repeat(np.arange(B), sizes), dtype=jnp.int32)
        edge_index = jax.random.randint(ks[0], (2, E), 0, N, dtype=jnp.int32)
        s = 1.0 / np.sqrt(D)
        return {'x': jax.random.normal(ks[1], (N, D), jnp.float32), 'batch': batch, 'edge_index': edge_index, 'norm1_g': jnp.ones((D,), jnp.float32), 'norm1_b': jnp.zeros((D,), jnp.float32), 'norm2_g': jnp.ones((D,), jnp.float32), 'norm2_b': jnp.zeros((D,), jnp.float32), 'W_conv': jax.random.normal(ks[2], (D, D), jnp.float32) * s, 'b_conv': jnp.zeros((D,), jnp.float32), 'Wq': jax.random.normal(ks[3], (D, D), jnp.float32) * s, 'Wk': jax.random.normal(ks[4], (D, D), jnp.float32) * s, 'Wv': jax.random.normal(ks[5], (D, D), jnp.float32) * s, 'Wo': jax.random.normal(ks[6], (D, D), jnp.float32) * s, 'proj': jax.random.normal(ks[7], (M, DH), jnp.float32)}
    _L1_gnn_all = _L1_gnn_setup()
    _L1_gnn_in = {k: v for k, v in _L1_gnn_all.items() if k in ('norm1_g', 'norm1_b', 'norm2_g', 'norm2_b', 'W_conv', 'b_conv', 'Wq', 'Wk', 'Wv', 'Wo', 'proj')}
    del _L1_gnn_all
    return {'x': x, 'src': src, 'dst': dst, 'L0_gnn_W': _L0_gnn_in['W'], 'L0_gnn_att_w': _L0_gnn_in['att_w'], 'L1_gnn_norm1_g': _L1_gnn_in['norm1_g'], 'L1_gnn_norm1_b': _L1_gnn_in['norm1_b'], 'L1_gnn_norm2_g': _L1_gnn_in['norm2_g'], 'L1_gnn_norm2_b': _L1_gnn_in['norm2_b'], 'L1_gnn_W_conv': _L1_gnn_in['W_conv'], 'L1_gnn_b_conv': _L1_gnn_in['b_conv'], 'L1_gnn_Wq': _L1_gnn_in['Wq'], 'L1_gnn_Wk': _L1_gnn_in['Wk'], 'L1_gnn_Wv': _L1_gnn_in['Wv'], 'L1_gnn_Wo': _L1_gnn_in['Wo'], 'L1_gnn_proj': _L1_gnn_in['proj']}

def reference(x, src, dst, L0_gnn_W, L0_gnn_att_w, L1_gnn_norm1_g, L1_gnn_norm1_b, L1_gnn_norm2_g, L1_gnn_norm2_b, L1_gnn_W_conv, L1_gnn_b_conv, L1_gnn_Wq, L1_gnn_Wk, L1_gnn_Wv, L1_gnn_Wo, L1_gnn_proj):
    import jax
    import jax.numpy as jnp

    def _L0_gnn_ref(x, W, att_w, src, dst):
        import jax, jax.numpy as jnp
        import numpy as np
        N_NODES = 6250
        N_EDGES = 200000
        N_HEADS = 8
        IN_DIM = 512
        OUT_DIM = 64
        LRELU_ALPHA = 0.2
        outs = []
        for h in range(N_HEADS):
            feat = x @ W[h]
            a1 = att_w[h, :OUT_DIM]
            a2 = att_w[h, OUT_DIM:]
            alpha_s = feat @ a1
            alpha_d = feat @ a2
            logit = jax.nn.leaky_relu(alpha_s[src] + alpha_d[dst], LRELU_ALPHA)
            m = jax.ops.segment_max(logit, src, num_segments=N_NODES)
            e = jnp.exp(logit - m[src])
            denom = jax.ops.segment_sum(e, src, num_segments=N_NODES)
            att = e / denom[src]
            agg = jax.ops.segment_sum(att[:, None] * feat[dst], src, num_segments=N_NODES)
            outs.append(jax.nn.relu(agg))
        return jnp.concatenate(outs, axis=1)

    def _L1_gnn_ref(x, batch, edge_index, norm1_g, norm1_b, norm2_g, norm2_b, W_conv, b_conv, Wq, Wk, Wv, Wo, proj):
        import jax, jax.numpy as jnp
        import numpy as np
        B = 32
        MAXN = 256
        HEADS = 8
        DH = 64
        M = 256
        D = 512
        EPS = 1e-05
        KEPS = 1e-06

        def _batchnorm(x, g, b):
            mu = jnp.mean(x, axis=0)
            var = jnp.mean((x - mu) ** 2, axis=0)
            return (x - mu) * jax.lax.rsqrt(var + EPS) * g + b

        def _forward(x, batch, edge_index, norm1_g, norm1_b, norm2_g, norm2_b, W_conv, b_conv, Wq, Wk, Wv, Wo, proj):
            N = x.shape[0]
            E = edge_index.shape[1]
            h = x
            xn = _batchnorm(x, norm1_g, norm1_b)
            msg = xn[edge_index[0]]
            agg = jax.ops.segment_sum(msg, edge_index[1], num_segments=N)
            deg = jax.ops.segment_sum(jnp.ones((E,), x.dtype), edge_index[1], num_segments=N)
            agg = agg / jnp.maximum(deg, 1.0)[:, None]
            conv_out = jax.nn.relu(agg @ W_conv + b_conv)
            counts = jax.ops.segment_sum(jnp.ones((N,), jnp.int32), batch, num_segments=B)
            offsets = jnp.concatenate([jnp.zeros((1,), jnp.int32), jnp.cumsum(counts)[:-1]])
            pos = jnp.arange(N, dtype=jnp.int32) - offsets[batch]
            h_dense = jnp.zeros((B, MAXN, D), x.dtype).at[batch, pos].set(h)
            mask = jnp.zeros((B, MAXN), bool).at[batch, pos].set(True)

            def heads(t, W):
                return (t @ W).reshape(B, MAXN, HEADS, DH).transpose(0, 2, 1, 3)
            q, k, v = (heads(h_dense, Wq), heads(h_dense, Wk), heads(h_dense, Wv))
            scale = DH ** (-0.25)

            def phi(t, is_query):
                t = t * scale
                u = jnp.einsum('bhnd,md->bhnm', t, proj)
                diag = 0.5 * jnp.sum(t * t, axis=-1, keepdims=True)
                if is_query:
                    m_ = jnp.max(u, axis=-1, keepdims=True)
                else:
                    m_ = jnp.max(u, axis=(-2, -1), keepdims=True)
                return jnp.exp(u - diag - jax.lax.stop_gradient(m_)) / np.sqrt(M) + KEPS
            qf = phi(q, True)
            kf = phi(k, False) * mask[:, None, :, None]
            vm = v * mask[:, None, :, None]
            kv = jnp.einsum('bhnm,bhnd->bhmd', kf, vm)
            z = 1.0 / (jnp.einsum('bhnm,bhm->bhn', qf, kf.sum(axis=2)) + KEPS)
            attn = jnp.einsum('bhnm,bhmd->bhnd', qf, kv) * z[..., None]
            attn = attn.transpose(0, 2, 1, 3).reshape(B, MAXN, D) @ Wo
            h_attn = attn[batch, pos]
            return _batchnorm(conv_out + h_attn + h, norm2_g, norm2_b)
        return _forward(x, batch, edge_index, norm1_g, norm1_b, norm2_g, norm2_b, W_conv, b_conv, Wq, Wk, Wv, Wo, proj)
    edge_index = jnp.stack([src, dst])
    batch0 = jnp.zeros((6250,), jnp.int32)
    h = jnp.maximum(_layernorm(x, axis=-1), 0.0)
    x = x + _L0_gnn_ref(h, L0_gnn_W, L0_gnn_att_w, src, dst)
    h = jnp.maximum(_layernorm(x, axis=-1), 0.0)
    x = x + _L1_gnn_ref(h, batch0, edge_index, L1_gnn_norm1_g, L1_gnn_norm1_b, L1_gnn_norm2_g, L1_gnn_norm2_b, L1_gnn_W_conv, L1_gnn_b_conv, L1_gnn_Wq, L1_gnn_Wk, L1_gnn_Wv, L1_gnn_Wo, L1_gnn_proj)
    return x

_drawn_inputs = setup_inputs


def setup_inputs(seed=0):
    import zlib

    import numpy as np

    out = dict(_drawn_inputs(seed))
    spreads = {'L1_gnn_norm1_g': (1.0, 0.2),
     'L1_gnn_norm1_b': (0.0, 0.1),
     'L1_gnn_norm2_g': (1.0, 0.2),
     'L1_gnn_norm2_b': (0.0, 0.1),
     'L1_gnn_b_conv': (0.0, 0.1)}
    factors = {'L1_gnn_Wq': 6.865,
     'L1_gnn_Wk': 7.09,
     'L1_gnn_Wv': 6.741,
     'L1_gnn_Wo': 7.141,
     'L1_gnn_proj': 8.0}
    for name, (base, spread) in spreads.items():
        noise = np.random.default_rng([zlib.crc32(name.encode()), seed]).standard_normal(out[name].shape)
        drawn = base * np.exp(spread * noise) if base else spread * noise
        out[name] = jnp.asarray(drawn.astype(out[name].dtype))
    for name, factor in factors.items():
        out[name] = (out[name] * factor).astype(out[name].dtype)
    return out
```

```python
from contextlib import ExitStack

import concourse.bass as bass
from concourse import mybir

P = 128
F32 = mybir.dt.float32
BF16 = mybir.dt.bfloat16
I32 = mybir.dt.int32
ALU = mybir.AluOpType
ACT = mybir.ActivationFunctionType
AX_X = mybir.AxisListType.X

N = 6250
E = 100000
D = 512
KD = D // P
H, O = 8, 64
TILES = (N + P - 1) // P
LAST = N - (TILES - 1) * P
ACC_W = D + H
LN_EPS = 1e-5
BN_EPS = 1e-5
KEPS = 1e-6
SLOPE = 0.2
BIG = 1e30

COLS = 1024
ROW_BITS = 10
ALL_BITS = 17
EDGE_ROWS, EDGE_COLS = 125, 800
PAD_COLS = COLS - EDGE_COLS
LOT = 256
SHIFT = 13
MINOR_MASK = (1 << SHIFT) - 1
KEY_BASE = 0x20000000
NO_NODE = TILES * P + P - 1
assert EDGE_ROWS * EDGE_COLS == E and 2 * PAD_COLS >= LOT - 1 and 2 * TILES <= P and P * COLS == 1 << ALL_BITS

SB = COLS // P
LOTS = SB // 2
ROWS = -(-(E + TILES * (LOT - 1)) // COLS)
GROUP = 16
GROUPS = -(-ROWS // GROUP)
ROWS_G = GROUPS * GROUP
OFF = 128.0
SHADOW = 2
assert ROWS % SHADOW == 0

MAXN = 256
NT = MAXN // P
M = 256
MT = M // P
DH = 64
SCALE = DH ** -0.25


class Steps:

    def __init__(self, sem, names):
        self.sem, self.names, self.n = sem, list(names), 0
        self.at = {name: i + 1 for i, name in enumerate(self.names)}
        assert len(self.at) == len(self.names)

    def done(self, instruction, name):
        assert self.names[self.n] == name, (self.names[self.n], name)
        self.n += 1
        instruction.then_inc(self.sem, 1)

    def wait(self, engine, name):
        engine.wait_ge(self.sem, self.at[name])


def build(nc, x, src, dst, W0, att_w, norm1_g, norm1_b, norm2_g, norm2_b, W_conv, b_conv, Wq, Wk, Wv, Wo, proj, out):
    with ExitStack() as ctx:
        def sb(name, shape, dt):
            return ctx.enter_context(nc.sbuf_tensor(name, shape, dt))

        def pb(name, shape, dt):
            return ctx.enter_context(nc.psum_tensor(name, shape, dt))

        def sem(name):
            return ctx.enter_context(nc.semaphore(name))

        v, s, g, pet = nc.vector, nc.scalar, nc.gpsimd, nc.tensor

        feat_table = nc.dram_tensor("feat_table", (TILES * P, D), F32).ap()
        ad_table = nc.dram_tensor("ad_table", (TILES * P, H), F32).ap()
        slot_nodes = nc.dram_tensor("slot_nodes", (P, COLS), BF16).ap()
        x1_table = nc.dram_tensor("x1_table", (TILES * P, D), F32).ap()
        ind_table = nc.dram_tensor("ind_table", (TILES, P), BF16).ap()
        bias_table = nc.dram_tensor("bias_table", (6, D), BF16).ap()
        h1_table = nc.dram_tensor("h1_table", (TILES * P, D), F32).ap()

        acc = sb("acc", [P, TILES, ACC_W], F32)
        gathered_ad = sb("gathered_ad", [P, SB, ROWS_G, H], F32)
        keys = sb("keys", [P, 2, COLS], F32)
        wk = sb("wk", [P, 2, COLS], F32)
        minorA = sb("minorA", [P, SB, P], I32)
        minorB = sb("minorB", [P, SB, P], I32)
        nodeA = sb("nodeA", [P, SB, P], F32)
        nodeB = sb("nodeB", [P, SB, P], F32)
        lastA = sb("lastA", [P, SB, P], F32)
        tileA = sb("tileA", [1, LOTS, P], I32)
        tileB = sb("tileB", [1, LOTS, P], I32)
        rows = sb("rows", [P, SB, D], F32)
        onehot = sb("onehot", [P, 2, SB, P], F32)
        ident = sb("ident", [P, P], F32)
        iota_row = sb("iota_row", [P, P], F32)
        iota_col = sb("iota_col", [P, 1], F32)
        iota_pad = sb("iota_pad", [P, PAD_COLS], F32)
        ones = sb("ones", [P, 1], F32)
        half = sb("half", [P, 2], F32)
        onesb = sb("onesb", [1, P], BF16)
        part = sb("part", [P, 4], I32)
        padc = sb("padc", [P, 4], F32)
        padi = sb("padi", [P, 2], I32)
        signi = sb("signi", [P, 8], I32)
        signs = sb("signs", [P, 8], F32)
        count = sb("count", [P, P // 2, 2], F32)
        look = sb("look", [P, TILES, 3, 2 * H], BF16)
        alphas = sb("alphas", [P, TILES, 2 * H], F32)
        maxd = sb("maxd", [P, TILES, H], F32)
        Wa = sb("Wa", [P, KD, 2 * H], F32)
        stat = sb("stat", [P, 4, TILES], F32)
        idx = sb("idx", [P, SB], I32)
        staged_ad = sb("staged_ad", [P, SB, H], F32)
        wts = sb("wts", [P, 2, SB, H], F32)
        small = sb("small", [P, 96], F32)

        keyX, keyY = keys[:, 0, :], keys[:, 1, :]
        wk1, wk2 = wk[:, 0, :], wk[:, 1, :]
        acc_flat = acc[:, :, :].rearrange("p t w -> p (t w)")
        look_flat = look[:, :, :, :].rearrange("p t a b -> p (t a b)")
        spread = look_flat[:, 0:P * H]
        same = look_flat[:, P * H:P * H + COLS + 2]
        ad_flat = gathered_ad[:, :, :, :].rearrange("p a b c -> p (a b c)")
        rows_flat = rows[:, :, :].rearrange("p a b -> p (a b)")
        oh_flat = onehot[:, :, :, :].rearrange("p a b c -> p (a b c)")
        W4 = rows_flat[:, 0:KD * D].rearrange("p (k h o) -> p k h o", k=KD, h=H)
        Wprod = rows_flat[:, KD * D:2 * KD * D].rearrange("p (k h o) -> p k h o", k=KD, h=H)
        attb = oh_flat[:, 0:H * 2 * O].rearrange("p (h a o) -> p h a o", h=H, a=2)
        hbuf = ad_flat[:, 0:2 * D].rearrange("p (a d) -> p a d", a=2)
        hTbuf = ad_flat[:, 2 * D:4 * D].rearrange("p (a d) -> p a d", a=2)
        fbuf = ad_flat[:, 4 * D:6 * D].rearrange("p (a d) -> p a d", a=2)
        junk = ad_flat[:, 6 * D:8 * D].rearrange("p (a d) -> p a d", a=2)
        mask = rows_flat[:, 0:COLS]
        runmax = rows_flat[:, COLS:2 * COLS]
        runmaxE = rows_flat[:, 2 * COLS:2 * COLS + SB * GROUP * (H + 1)].rearrange("p (b r h) -> p b r h", b=SB, r=GROUP)
        bcast_row = keyX.bitcast(BF16).rearrange("p (q c) -> p q c", q=2)
        zbuf = keyY[:, 0:6 * SB * H].rearrange("p (a b h) -> p a b h", a=6, b=SB)
        nodes_all = wk1.bitcast(BF16).rearrange("p (q c) -> p q c", q=2)
        onehotT = wk2.bitcast(BF16).rearrange("p (q c) -> p q c", q=2)

        psA = pb("psA", [P, COLS], F32)
        psB = pb("psB", [P, COLS], F32)
        psC = pb("psC", [P, COLS], F32)
        psD = pb("psD", [P, 512], F32)
        psE = pb("psE", [P, 512], F32)

        consts = sem("consts")
        keys_loaded = sem("keys_loaded")
        keys_loaded2 = sem("keys_loaded2")
        w0_loaded = sem("w0_loaded")
        x_loaded = sem("x_loaded")
        sort_step = sem("sort_step")
        turned = sem("turned")
        dve_link = sem("dve_link")
        act_link = sem("act_link")
        pool_link = sem("pool_link")
        counted = sem("counted")
        pads_known = sem("pads_known")
        Wa_ready = sem("Wa_ready")
        var_ready = sem("var_ready")
        rstd_ready = sem("rstd_ready")
        h_ready = sem("h_ready")
        hT_ps = sem("hT_ps")
        hT_ready = sem("hT_ready")
        feat_ps = sem("feat_ps")
        feat_ready = sem("feat_ready")
        feat_stored = [sem("feat_stored0"), sem("feat_stored1")]
        ad_stored = sem("ad_stored")
        fields = sem("fields")
        fieldsT = sem("fieldsT")
        slotsA = sem("slotsA")
        slots_stored = sem("slots_stored")
        keysB_free = sem("keysB_free")
        sortB_done = sem("sortB_done")
        hold = sem("hold")
        idx1 = sem("idx1")
        ad_arrived = [sem("ad_arrived0"), sem("ad_arrived1")]
        ad_kept = sem("ad_kept")
        adT = sem("adT")
        scanned = sem("scanned")
        scanT = sem("scanT")
        last_ready = sem("last_ready")
        slotmax = sem("slotmax")
        taken = sem("taken")
        look_ready = sem("look_ready")
        done = sem("done")

        DENSE_PAIRS = TILES // 2
        CROSSINGS = 2 * (ALL_BITS - ROW_BITS)
        share = [DENSE_PAIRS * (c + 1) // CROSSINGS for c in range(CROSSINGS)]

        def sort_plan(start):
            n, at, plan = start + 1, 1, []
            n += 2 * sum(range(1, ROW_BITS + 1))
            at ^= sum(range(1, ROW_BITS + 1)) & 1
            for m in range(ROW_BITS + 1, ALL_BITS + 1):
                n, at = n + 1, at ^ 1
                for js in (m - ROW_BITS, ROW_BITS):
                    plan.append((n, at))
                    n, at = n + 1 + 2 * js, at ^ (js & 1)
            return plan, n, at

        planA, stepsA, atA = sort_plan(0)
        planB, stepsB, atB = sort_plan(stepsA)

        block = ctx.enter_context(nc.Block())

        def zbuf_small(q):
            return rows_flat[:, 3500 + 64 * q:3564 + 64 * q].rearrange("p (b h) -> p b h", h=H)

        row_loaded = [sem("row_loaded0"), sem("row_loaded1")]
        spread_ps = sem("spread_ps")
        nodes_ready = sem("nodes_ready")
        onehotT_ready = sem("onehotT_ready")
        look_ps = sem("look_ps")
        zstep = sem("zstep")
        w_ready = sem("w_ready")
        idx2 = sem("idx2")
        rows_arrived = [sem("rows_arrived0"), sem("rows_arrived1")]
        onehot_ready = sem("onehot_ready")
        weighted = sem("weighted")
        lot_ps = sem("lot_ps")
        lot_added = sem("lot_added")
        LOT_CREDIT, ADD_CREDIT = LOTS, 2
        x_in = [sem("x_in0"), sem("x_in1")]
        x_last = sem("x_last")
        zeroed = sem("zeroed")
        normed = sem("normed")
        moments = sem("moments")
        x1_ready = sem("x1_ready")
        x1_stored = sem("x1_stored")
        var1_ready = sem("var1_ready")
        rstd1_ready = sem("rstd1_ready")
        h1_ready = sem("h1_ready")
        h1_stored = [sem("h1_stored0"), sem("h1_stored1")]
        colsum_ps = sem("colsum_ps")
        xin = rows[:, 0:2, :]
        xlast = rows[:, 2, :]
        hout = ad_flat[:, 0:4 * D].rearrange("p (q a d) -> p q a d", q=2, a=2)
        bnst = keyX[:, 0:6 * TILES].rearrange("p (t c) -> p t c", c=6)
        mean1, var1, dif1 = (keyX[:, 512 + 64 * n:512 + 64 * n + TILES] for n in range(3))
        zeros8 = small[:, 8:16]

        def tail_sync(sp):
            sp.wait_ge(look_ready, 1)
            for q in range(2):
                sp.dma_start(bcast_row[0:1, q, :], slot_nodes[q:q + 1, :]).then_inc(row_loaded[q], 16)
            with sp.Fori(0, ROWS // 2) as i:
                for q in range(2):
                    sp.wait_ge(spread_ps, i * 2 + (q + 1))
                    sp.dma_start(bcast_row[0:1, q, :], slot_nodes[bass.ds(i * 2 + (q + 2), 1), :]).then_inc(row_loaded[q], 16)
            for q in range(2):
                sp.wait_ge(row_loaded[q], 16 * (1 + ROWS // 2))
            sp.wait_ge(lot_added, ADD_CREDIT + ROWS * LOTS)
            sp.wait_ge(zeroed, 1)
            sp.dma_start(xlast[0:LAST, :], x[(TILES - 1) * P:N, :]).then_inc(x_last, 16)
            for q in range(2):
                sp.dma_start(xin[:, q, :], x[q * P:(q + 1) * P, :]).then_inc(x_in[q], 16)
            def store_x1(i, q):
                sp.wait_ge(x1_ready, i * 2 + (q + 1))
                sp.dma_start(x1_table[bass.ds(i * (2 * P) + q * P, P), :],
                             acc[:, bass.ds(i * 2 + q, 1), 0:D].rearrange("p a d -> p (a d)")).then_inc(x1_stored, 16)
            with sp.Fori(0, DENSE_PAIRS - 1) as i:
                for q in range(2):
                    store_x1(i, q)
                    sp.dma_start(xin[:, q, :], x[bass.ds(i * (2 * P) + (2 + q) * P, P), :]).then_inc(x_in[q], 16)
            for q in range(2):
                store_x1(DENSE_PAIRS - 1, q)
            sp.wait_ge(x1_ready, TILES)
            sp.dma_start(x1_table[(TILES - 1) * P:TILES * P, :], acc[:, TILES - 1, 0:D]).then_inc(x1_stored, 16)
            with sp.Fori(0, DENSE_PAIRS) as i:
                for q in range(2):
                    sp.wait_ge(h1_ready, i * 4 + (2 * q + 1))
                    sp.dma_start(h1_table[bass.ds(i * (2 * P) + q * P, P), :], hout[:, q, 0, :]).then_inc(h1_stored[q], 16)
            sp.wait_ge(h1_ready, 2 * TILES - 1)
            sp.dma_start(h1_table[(TILES - 1) * P:TILES * P, :], hout[:, 0, 0, :]).then_inc(h1_stored[0], 16)
            tail2_sync(sp)

        def tail_gpsimd(pool):
            pool.wait_ge(look_ready, 1)
            pool.sem_inc(hold, 1)
            with pool.Fori(0, ROWS) as r:
                for hf in range(2):
                    pool.wait_ge(lot_ps, r * LOTS + (LOT_CREDIT - LOTS + 2 * hf + 2))
                    pool.wait_ge(idx2, r * 2 + (hf + 1))
                    pool.sem_inc(hold, 1)
                    for b in range(4 * hf, 4 * hf + 4):
                        g.indirect_dma_start(rows[:, b, :], None, feat_table,
                                             bass.IndirectOffsetOnAxis(ap=idx[:, b:b + 1], axis=0),
                                             bounds_check=N - 1, oob_is_err=False).then_inc(rows_arrived[hf], 16)
            tail2_gpsimd(pool)

        def tail_scalar(act, link, links):
            def put_indices(minor_t, r, hf, signal):
                bs = slice(4 * hf, 4 * hf + 4)
                s.copy(idx[:, bs], minor_t[:, bs, bass.ds(r, 1)].rearrange("p b a -> p (b a)")).then_inc(signal, 1)

            def nodes(q):
                s.copy(nodes_all[:, q, :], psC[:, :]).then_inc(nodes_ready, 1)

            def weights(q):
                s.activation(wts[:, q, :, :], zbuf[:, 3 * q + 2, :, :], ACT.Exp).then_inc(w_ready, 1)

            act.wait_ge(look_ready, 1)
            act.wait_ge(idx1, 2 + 2 * ROWS_G)
            put_indices(minorA, 0, 0, idx2)
            put_indices(minorA, 0, 1, idx2)
            act.wait_ge(spread_ps, 1)
            nodes(0)
            act.wait_ge(zstep, 4)
            weights(0)
            with act.Fori(0, ROWS // 2) as i:
                for q in range(2):
                    act.wait_ge(rows_arrived[0], i * 128 + (64 * q + 64))
                    act.sem_inc(hold, 1)
                    put_indices(minorA, i * 2 + (q + 1), 0, idx2)
                    act.wait_ge(spread_ps, i * 2 + (q + 2))
                    act.wait_ge(onehotT_ready, i * 2 + (q + 1))
                    nodes(1 - q)
                    act.wait_ge(rows_arrived[1], i * 128 + (64 * q + 64))
                    act.sem_inc(hold, 1)
                    put_indices(minorA, i * 2 + (q + 1), 1, idx2)
                    act.wait_ge(zstep, i * 8 + (4 * q + 8))
                    act.wait_ge(lot_ps, i * 8 + (4 * q + LOT_CREDIT))
                    weights(1 - q)
            act.wait_ge(moments, 1)
            s.activation(stat[:, 2, :], var1, ACT.Sqrt, bias=small[:, 0:1]).then_inc(var1_ready, 1)
            act.wait_ge(rstd1_ready, 1)

            def make_h1(t, q):
                s.activation(hout[:, q, 0, :], acc[:, bass.ds(t, 1), 0:D].rearrange("p a d -> p (a d)"), ACT.Relu,
                             scale=stat[:, 3, bass.ds(t, 1)], bias=stat[:, 1, bass.ds(t, 1)]).then_inc(h1_ready, 1)
                act.wait_ge(h1_ready, t * 2 + 1)
                s.activation(hout[:, q, 1, :], hout[:, q, 0, :], ACT.Square).then_inc(h1_ready, 1)
            make_h1(0, 0)
            make_h1(1, 1)
            with act.Fori(1, DENSE_PAIRS) as i:
                for q in range(2):
                    act.wait_ge(colsum_ps, i * 2 + (q - 1))
                    act.wait_ge(h1_stored[q], i * 16)
                    act.sem_inc(hold, 1)
                    make_h1(i * 2 + q, q)
            act.wait_ge(colsum_ps, TILES - 2)
            act.wait_ge(h1_stored[0], 16 * DENSE_PAIRS)
            make_h1(TILES - 1, 0)
            tail2_scalar(act, link, links, put_indices)

        def tail_vector(dve, link, links):
            def make_onehotT(q):
                v.tensor_scalar(onehotT[:, q, :], nodes_all[:, q, :], iota_col[:, 0:1], None,
                                ALU.is_equal).then_inc(onehotT_ready, 1)

            def make_onehot(node_t, r, q, signal):
                v.tensor_tensor(onehot[:, q, :, :], iota_row[:, :].unsqueeze(1).broadcast_to([P, SB, P]),
                                node_t[:, :, bass.ds(r, 1)].broadcast_to([P, SB, P]), ALU.is_equal).then_inc(signal, 1)

            def zops(k, r, q, zbase):
                ps = (psD, psE)[q][:, 0:SB * 2 * H].rearrange("p (b c) -> p b c", c=2 * H)
                z = [zbuf[:, 3 * q + n, :, :] for n in range(3)]
                if k > 0:
                    dve.wait_ge(zstep, zbase + k)
                if k == 0:
                    v.tensor_tensor(z[0], ps[:, :, 0:H],
                                    gathered_ad[:, :, bass.ds(r, 1), :].rearrange("p b a h -> p b (a h)"),
                                    ALU.add).then_inc(zstep, 1)
                elif k == 1:
                    v.scalar_tensor_tensor(z[1], z[0], SLOPE, z[0], ALU.mult, ALU.max).then_inc(zstep, 1)
                elif k == 2:
                    v.tensor_tensor(z[0], z[1], ps[:, :, H:2 * H], ALU.subtract).then_inc(zstep, 1)
                else:
                    v.tensor_scalar(z[2], z[0], 0.0, None, ALU.min).then_inc(zstep, 1)

            def weigh(b, q):
                row = rows[:, b, :].rearrange("p (h o) -> p h o", h=H)
                v.tensor_tensor(row, row, wts[:, q, b, :].unsqueeze(2).broadcast_to([P, H, O]),
                                ALU.mult).then_inc(weighted, 1)

            def add_lot(a, tile, psum, width):
                d = acc[:, bass.ds(tile, 1), 0:width].rearrange("p a d -> p (a d)")
                v.tensor_tensor(d, d, psum[:, 0:width], ALU.add).then_inc(lot_added, 1)

            dve.sem_inc(lot_added, ADD_CREDIT)
            dve.wait_ge(nodes_ready, 1)
            make_onehotT(0)
            dve.wait_ge(look_ps, 1)
            for k in range(4):
                zops(k, 0, 0, 0)
            make_onehot(nodeA, 0, 0, onehot_ready)
            with dve.Fori(0, ROWS // 2) as i:
                for q in range(2):
                    r1, q1 = i * 2 + (q + 1), 1 - q
                    tiles = [dve.value_load(tileA[0:1, a, bass.ds(i * 2 + q, 1)], min_val=0, max_val=TILES - 1)
                             for a in range(LOTS)]

                    def add(a):
                        dve.wait_ge(lot_added, i * 8 + (4 * q + a + ADD_CREDIT))
                        dve.wait_ge(lot_ps, i * 8 + (4 * q + a + 1 + LOT_CREDIT))
                        add_lot(a, tiles[a], (psA, psB)[a % 2], ACC_W)
                    dve.wait_ge(w_ready, i * 2 + (q + 1))
                    dve.wait_ge(rows_arrived[0], i * 128 + (64 * q + 64))
                    weigh(0, q)
                    weigh(1, q)
                    dve.wait_ge(nodes_ready, i * 2 + (q + 2))
                    dve.wait_ge(look_ps, i * 2 + (q + 1))
                    make_onehotT(q1)
                    weigh(2, q)
                    weigh(3, q)
                    add(0)
                    dve.wait_ge(look_ps, i * 2 + (q + 2))
                    zb = i * 8 + (4 * q + 4)
                    zops(0, r1, q1, zb)
                    dve.wait_ge(rows_arrived[1], i * 128 + (64 * q + 64))
                    weigh(4, q)
                    weigh(5, q)
                    zops(1, r1, q1, zb)
                    add(1)
                    zops(2, r1, q1, zb)
                    weigh(6, q)
                    weigh(7, q)
                    zops(3, r1, q1, zb)
                    add(2)
                    dve.wait_ge(lot_ps, i * 8 + (4 * q + LOT_CREDIT))
                    make_onehot(nodeA, r1, q1, onehot_ready)
                    add(3)
            dve.wait_ge(lot_added, ADD_CREDIT + ROWS * LOTS)
            v.memset(xlast, 0.0).then_inc(zeroed, 1)
            link(v.memset(zeros8, 0.0))
            link(v.tensor_scalar(maxd[:, :, :], acc[:, :, D:ACC_W], 1e-30, None, ALU.max))
            link(v.reciprocal(maxd[:, :, :], maxd[:, :, :]))

            def make_x1(t, q, xt, base):
                row = acc[:, bass.ds(t, 1), 0:D].rearrange("p a (h o) -> p (a h) o", h=H)
                row_flat = acc[:, bass.ds(t, 1), 0:D].rearrange("p a d -> p (a d)")
                v.tensor_tensor(row, row, maxd[:, bass.ds(t, 1), :].rearrange("p a h -> p (a h)").unsqueeze(2)
                                .broadcast_to([P, H, O]), ALU.mult).then_inc(dve_link, 1)
                dve.wait_ge(dve_link, base + 1)
                v.scalar_tensor_tensor(row_flat, row_flat, 0.0, xt, ALU.max, ALU.add).then_inc(x1_ready, 1)
                dve.wait_ge(x1_ready, t + 1)
                dve.sem_inc(hold, 1)
                v.bn_stats(bnst[:, bass.ds(t, 1), :].rearrange("p a c -> p (a c)"), row_flat).then_inc(normed, 1)

            start = links[0]
            with dve.Fori(0, DENSE_PAIRS) as i:
                for q in range(2):
                    dve.wait_ge(x_in[q], i * 16 + 16)
                    make_x1(i * 2 + q, q, xin[:, q, :], i * 2 + (q + start))
            links[0] += 2 * DENSE_PAIRS
            dve.wait_ge(x_last, 16)
            make_x1(TILES - 1, 0, xlast, links[0])
            links[0] += 1
            dve.wait_ge(normed, TILES)
            link(v.tensor_tensor(mean1, bnst[:, :, 1], bnst[:, :, 4], ALU.add))
            link(v.tensor_tensor(dif1, bnst[:, :, 1], bnst[:, :, 4], ALU.subtract))
            link(v.tensor_tensor(dif1, dif1, dif1, ALU.mult))
            link(v.tensor_tensor(var1, bnst[:, :, 2], bnst[:, :, 5], ALU.add))
            link(v.tensor_scalar(var1, var1, 1.0 / D, None, ALU.mult))
            v.scalar_tensor_tensor(var1, dif1, 0.25, var1, ALU.mult, ALU.add).then_inc(moments, 1)
            dve.wait_ge(var1_ready, 1)
            link(v.reciprocal(stat[:, 3, :], stat[:, 2, :]))
            v.scalar_tensor_tensor(stat[:, 1, :], mean1, -0.5, stat[:, 3, :], ALU.mult, ALU.mult).then_inc(rstd1_ready, 1)
            tail2_vector(dve, link, links, make_onehot, add_lot)

        def tail_tensor(pe):
            def spread_nodes(q, count):
                for c in range(2):
                    ins = pet.matmul(psC[:, c * 512:(c + 1) * 512], onesb[0:1, :], bcast_row[0:1, q, c * 512:(c + 1) * 512],
                                     start=True, stop=True)
                ins.then_inc(spread_ps, 1)

            def look_up(r, q):
                for a in range(LOTS):
                    t = pe.value_load(tileA[0:1, a, bass.ds(r, 1)], min_val=0, max_val=TILES - 1)
                    for b in (2 * a, 2 * a + 1):
                        for n in range(3):
                            ins = pet.matmul((psD, psE)[q][:, b * 2 * H:(b + 1) * 2 * H], onehotT[:, q, b * P:(b + 1) * P],
                                             look[:, bass.ds(t, 1), n, :].rearrange("p a c -> p (a c)"),
                                             start=(n == 0), stop=(n == 2))
                ins.then_inc(look_ps, 1)

            def lot(a, q, r):
                psum = (psA, psB)[a % 2]
                for b in (2 * a, 2 * a + 1):
                    pet.matmul(psum[:, 0:D], onehot[:, q, b, :], rows[:, b, :], start=(b % 2 == 0), stop=(b % 2 == 1))
                for b in (2 * a, 2 * a + 1):
                    ins = pet.matmul(psum[:, D:ACC_W], onehot[:, q, b, :], wts[:, q, b, :],
                                     start=(b % 2 == 0), stop=(b % 2 == 1))
                ins.then_inc(lot_ps, 1)

            pe.sem_inc(lot_ps, LOT_CREDIT)
            pe.wait_ge(row_loaded[0], 16)
            spread_nodes(0, 0)
            pe.wait_ge(onehotT_ready, 1)
            look_up(0, 0)
            with pe.Fori(0, ROWS // 2) as i:
                for q in range(2):
                    pe.wait_ge(row_loaded[1 - q], i * 16 + 16 * (q + 1))
                    pe.wait_ge(nodes_ready, i * 2 + (q + 1))
                    spread_nodes(1 - q, None)
                    pe.wait_ge(onehot_ready, i * 2 + (q + 1))
                    for a in range(LOTS):
                        if a == 2:
                            pe.wait_ge(onehotT_ready, i * 2 + (q + 2))
                            pe.wait_ge(zstep, i * 8 + (4 * q + 4))
                            look_up(i * 2 + (q + 1), 1 - q)
                        pe.wait_ge(weighted, i * 16 + (8 * q + 2 * a + 2))
                        pe.wait_ge(lot_added, i * 8 + (4 * q + a + ADD_CREDIT - 1))
                        lot(a, q, None)
            pe.wait_ge(h1_ready, 2)
            pet.matmul(psD[:, 0:8], ident[:, :], zeros8, start=True, stop=False, skip_group_check=True)

            def colsums(q, last=False):
                for k in range(2 * KD):
                    ins = pet.matmul(psD[:, k:k + 1], hout[:, q, k // KD, (k % KD) * P:(k % KD + 1) * P], ones[:, :],
                                     start=False, stop=last, skip_group_check=True)
                ins.then_inc(colsum_ps, 1)
            with pe.Fori(0, DENSE_PAIRS) as i:
                for q in range(2):
                    pe.wait_ge(h1_ready, i * 4 + (2 * q + 2))
                    colsums(q)
            pe.wait_ge(h1_ready, 2 * TILES)
            colsums(0, True)
            tail2_tensor(pe)

        def blocks(flat_view):
            return flat_view.rearrange("p (k d) -> p k d", k=KD)
        Wc_s = blocks(ad_flat[:, 0:KD * D])
        Wq_s = blocks(ad_flat[:, 4 * D:8 * D])
        Wk_s = blocks(ad_flat[:, 8 * D:12 * D])
        Wv_s = blocks(wk[:, :, :].rearrange("p a c -> p (a c)"))
        Wo_s = blocks(keys[:, :, :].rearrange("p a c -> p (a c)"))
        lastA_flat = lastA[:, :, :].rearrange("p b r -> p (b r)")
        nodeA_flat = nodeA[:, :, :].rearrange("p b r -> p (b r)")
        minorA_flat = minorA[:, :, :].rearrange("p b r -> p (b r)").bitcast(F32)
        proj_s = lastA_flat[:, 0:2 * MT * DH].rearrange("p (t u d) -> p t u d", t=MT, u=2)
        projT = lastA_flat[:, 256:256 + M]
        select_last = lastA_flat[:, 512:512 + P]
        ones_mat = lastA_flat[:, 640:640 + P]
        SCRATCH = 28 * ACC_W
        at = [SCRATCH]

        def scratch(width):
            at[0] += width
            assert at[0] <= TILES * ACC_W
            return acc_flat[:, at[0] - width:at[0]]
        hT = scratch(KD * MAXN).rearrange("p (k n) -> p k n", k=KD)
        qT = scratch(KD * MAXN).rearrange("p (j n) -> p j n", j=KD)
        kT = scratch(KD * MAXN).rearrange("p (j n) -> p j n", j=KD)
        values = scratch(NT * H * (DH + 1)).rearrange("p (t h d) -> p t h d", t=NT, h=H)
        uk = scratch(H * NT * M).rearrange("p (h t m) -> p h t m", h=H, t=NT)
        squares = scratch(2 * KD * MAXN)
        kvs = scratch(2 * MT * (DH + 1)).rearrange("p (q t d) -> p q t d", q=2, t=MT)
        qf = nodeA_flat.rearrange("p (q t m) -> p q t m", q=2, t=NT)
        qfT = squares[:, 0:2 * MT * MAXN].rearrange("p (q t n) -> p q t n", q=2, t=MT)
        attn = minorA_flat.rearrange("p (t d) -> p t d", t=NT)
        look_f32 = look_flat.bitcast(F32)
        hA = look_f32[:, 0:NT * D].rearrange("p (t d) -> p t d", t=NT)
        hattn = hA
        dg = small[:, 16:48]
        mxk = small[:, 48:56]
        mxq = small[:, 56:72]
        bias_k = stat[:, 0, 0:16]
        bias_q = stat[:, 0, 16:32]
        km8 = stat[:, 2, 0:1]
        kmd = stat[:, 2, 8:16]
        zden = stat[:, 2, 16:20]

        hA_loaded = sem("hA_loaded")
        Wqkv_loaded = sem("Wqkv_loaded")
        proj_loaded = sem("proj_loaded")
        Wo_loaded = sem("Wo_loaded")
        Wc_loaded = sem("Wc_loaded")
        vec_loaded = sem("vec_loaded")
        hs = range(H)
        SPE = Steps(sem("att_pe"), ["hT", "projT", "qT", "kT", "v0", "v1", "diag"] + [f"uk{h}" for h in hs] +
                    ["kmT", "kmB", "uq0"] + [n for h in hs for n in ([f"uq{h + 1}"] if h < H - 1 else []) +
                                             [f"kv{h}", f"qfT{h}", f"at{h}"]] + ["aT", "wo", "last"])
        SACT = Steps(sem("att_act"), ["hT", "projT", "qT", "kT", "sq"] + [f"uk{h}" for h in hs] + [f"ek{h}" for h in hs] +
                     ["eq0"] + [n for h in hs for n in ([f"eq{h + 1}"] if h < H - 1 else []) + [f"qfT{h}"]] + ["aT", "wo"])
        SDVE = Steps(sem("att_dve"), ["cleared", "sums", "sel", "ones_mat", "ones", "v0", "v1", "diag"] + [f"mk{h}" for h in hs] +
                     ["km", "kmd", "bk", "mq0", "bq0"] +
                     [n for h in hs for n in [f"kf{h}", f"kv{h}"] + ([f"mq{h + 1}", f"bq{h + 1}"] if h < H - 1 else []) +
                      [f"qf{h}", f"zd{h}", f"zr{h}", f"at{h}"]] + ["hat0", "hat1"])

        colsum = stat[:, 1, 0:8]
        vecs = alphas[:, :, :].rearrange("p t c -> p (t c)")
        g1c, b1c = vecs[:, 0:KD], vecs[:, 4:4 + KD]
        mean_c, var_c, scale_c, shift_c, sd_c = (vecs[:, 8 + 4 * n:12 + 4 * n] for n in range(5))
        shrow = ad_flat[0:1, 4 * D:5 * D]
        bcrow = ad_flat[0:1, 5 * D:6 * D]
        parts1 = ad_flat[0:1, 6 * D:9 * D].bitcast(BF16).rearrange("p (n d) -> p n d", n=6)
        keys_flat = keys[:, :, :].rearrange("p a c -> p (a c)")
        bias_rows = keys_flat[0:6, 2 * D:2 * D + D // 2].bitcast(BF16)
        indT = wk1[0:TILES, 0:P // 2].bitcast(BF16)
        ind_rows = ad_flat[0:6, SB * ROWS_G * H - TILES * P // 2:].bitcast(BF16)
        bn1_sd = sem("bn1_sd")
        bn1_step = sem("bn1_step")
        bn1_shift = sem("bn1_shift")
        bn1_ps = sem("bn1_ps")
        parts_ready = sem("parts_ready")
        bias_stored = sem("bias_stored")
        acc_cleared = sem("acc_cleared")
        attended = sem("attended")

        idx3 = sem("idx3")
        h_arrived = [sem("h_arrived0"), sem("h_arrived1")]
        onehot1_ready = sem("onehot1_ready")
        lot1_ps = sem("lot1_ps")
        lot1_added = sem("lot1_added")

        rowsf = rows_flat
        h_in = rowsf[:, 0:2 * D].rearrange("p (q d) -> p q d", q=2)
        aggn = rowsf[:, 2 * D:4 * D].rearrange("p (q d) -> p q d", q=2)
        aggT = rowsf[:, 4 * D:6 * D].rearrange("p (q d) -> p q d", q=2)
        ybuf = rowsf[:, 6 * D:8 * D].rearrange("p (q d) -> p q d", q=2)
        ysq = oh_flat[:, 0:2 * D].rearrange("p (q d) -> p q d", q=2)
        ysum, ysum2 = oh_flat[:, 2 * D:3 * D], oh_flat[:, 3 * D:4 * D]
        rdeg = stat[:, 3, :]
        indc = stat[:, 1, :]
        deg_ready = sem("deg_ready")
        ind_ps = sem("ind_ps")
        ind_ready = sem("ind_ready")
        ind_spread = sem("ind_spread")
        hc_in = [sem("hc_in0"), sem("hc_in1")]
        aggn_ready = sem("aggn_ready")
        aggT_ps = sem("aggT_ps")
        aggT_ready = sem("aggT_ready")
        conv_ps = sem("conv_ps")
        y_ready = sem("y_ready")
        y_kept = sem("y_kept")
        y_summed = sem("y_summed")
        g2_loaded = sem("g2_loaded")
        total_ps = sem("total_ps")
        bn2_step = sem("bn2_step")
        bn2_sd = sem("bn2_sd")
        bn2_ready = sem("bn2_ready")
        x1_in = [sem(f"x1_in{n}") for n in range(4)]
        shifted = sem("shifted")
        scaled = sem("scaled")
        out_ready = sem("out_ready")
        out_stored = [sem(f"out_stored{n}") for n in range(4)]
        QUADS = TILES // 4
        scale2, shift2, mean2, sd2 = (ad_flat[:, (6 + n) * D:(7 + n) * D] for n in range(4))
        g2row, b2row = keys_flat[:, 0:D], keys_flat[:, D:2 * D]
        x1buf = rowsf[:, 0:4 * D].rearrange("p (q d) -> p q d", q=4)
        obuf = rowsf[:, 4 * D:8 * D].rearrange("p (q d) -> p q d", q=4)
        tbuf = oh_flat[:, 0:4 * D].rearrange("p (q d) -> p q d", q=4)

        def w_by_block(w):
            return w.rearrange("(k p) d -> p k d", p=P)

        def row_of(vector):
            return vector.rearrange("(u c) -> u c", u=1)

        def tail2_sync(sp):
            sp.wait_ge(lot_added, ADD_CREDIT + ROWS * LOTS)
            sp.wait_ge(w_ready, ROWS + 1)
            for w, place in ((Wq, Wq_s), (Wk, Wk_s), (Wv, Wv_s)):
                sp.dma_start(place, w_by_block(w)).then_inc(Wqkv_loaded, 16)
            for u in range(2):
                sp.dma_start(proj_s[:, :, u, :], proj.rearrange("(t p) d -> p t d", p=P)).then_inc(proj_loaded, 16)
            sp.wait_ge(rstd1_ready, 1)
            sp.dma_start(Wo_s, w_by_block(Wo)).then_inc(Wo_loaded, 16)
            for q in range(2):
                sp.wait_ge(h1_stored[q], 16 * (DENSE_PAIRS + 1 - q))
            sp.wait_ge(x1_stored, 16 * TILES)
            sp.dma_start(hA, h1_table[0:MAXN, :].rearrange("(t p) d -> p t d", p=P)).then_inc(hA_loaded, 16)
            sp.wait_ge(colsum_ps, TILES)
            sp.dma_start(Wc_s, w_by_block(W_conv)).then_inc(Wc_loaded, 16)
            sp.wait_ge(rstd1_ready, 1)
            for vector, place in ((norm1_g, g1c), (norm1_b, b1c)):
                sp.dma_start(place, vector.rearrange("(k p) -> p k", p=P), allow_slow_non_contiguous=True).then_inc(vec_loaded, 16)
            SDVE.wait(sp, "hat1")
            sp.dma_start(bcrow, row_of(b_conv)).then_inc(vec_loaded, 16)
            sp.wait_ge(parts_ready, 1)
            sp.dma_start(bias_table.rearrange("n d -> (n d)").rearrange("(u c) -> u c", u=1),
                         parts1.rearrange("p n d -> p (n d)")).then_inc(bias_stored, 16)
            sp.wait_ge(bias_stored, 16)
            sp.dma_start(bias_rows, bias_table).then_inc(bias_stored, 16)
            for vector, place in ((norm2_g, g2row), (norm2_b, b2row)):
                sp.dma_start(place, row_of(vector).broadcast_to([P, D])).then_inc(g2_loaded, 16)
            sp.wait_ge(lot1_added, ADD_CREDIT + ROWS * LOTS)
            for q in range(2):
                sp.dma_start(h_in[:, q, :], h1_table[q * P:(q + 1) * P, :]).then_inc(hc_in[q], 16)
            sp.wait_ge(ind_ready, 2)
            sp.dma_start(ind_table, indT).then_inc(ind_spread, 16)
            sp.wait_ge(ind_spread, 16)
            sp.dma_start(ind_rows[0:3, :], row_of(ind_table.rearrange("t n -> (t n)")).broadcast_to([3, TILES * P])
                         ).then_inc(ind_spread, 16)
            with sp.Fori(0, DENSE_PAIRS - 1) as i:
                for q in range(2):
                    sp.wait_ge(y_ready, i * 2 + (q + 1))
                    sp.dma_start(h_in[:, q, :], h1_table[bass.ds(i * (2 * P) + (2 + q) * P, P), :]).then_inc(hc_in[q], 16)
            sp.wait_ge(y_ready, TILES - 2)
            sp.dma_start(h_in[:, 0, :], h1_table[(TILES - 1) * P:TILES * P, :]).then_inc(hc_in[0], 16)
            sp.wait_ge(y_ready, TILES)
            sp.wait_ge(y_kept, 2 * TILES)
            sp.wait_ge(y_summed, 2 * TILES)
            for q in range(4):
                sp.dma_start(x1buf[:, q, :], x1_table[q * P:(q + 1) * P, :]).then_inc(x1_in[q], 16)

            with sp.Fori(0, QUADS - 1) as i:
                for q in range(4):
                    sp.wait_ge(out_ready, i * 4 + (q + 1))
                    sp.dma_start(out[bass.ds(i * (4 * P) + q * P, P), :], obuf[:, q, :]).then_inc(out_stored[q], 16)
                    sp.dma_start(x1buf[:, q, :], x1_table[bass.ds(i * (4 * P) + (4 + q) * P, P), :]).then_inc(x1_in[q], 16)
            for q in range(4):
                t = 4 * (QUADS - 1) + q
                sp.wait_ge(out_ready, t + 1)
                sp.dma_start(out[t * P:(t + 1) * P, :], obuf[:, q, :]).then_inc(out_stored[q], 16)
                if q == 0:
                    sp.dma_start(x1buf[:, 0, :], x1_table[(TILES - 1) * P:TILES * P, :]).then_inc(x1_in[0], 16)
            sp.wait_ge(out_ready, TILES)
            sp.dma_start(out[(TILES - 1) * P:N, :], obuf[0:LAST, 0, :]).then_inc(out_stored[0], 16)
            for q in range(4):
                sp.wait_ge(out_stored[q], 16 * (QUADS + (q == 0)))

        def tail2_gpsimd(pool):
            for q in range(2):
                pool.wait_ge(h1_stored[q], 16 * (DENSE_PAIRS + 1 - q))
            pool.sem_inc(hold, 1)
            with pool.Fori(0, ROWS) as r:
                for hf in range(2):
                    pool.wait_ge(lot1_ps, r * LOTS + (LOT_CREDIT - LOTS + 2 * hf + 2))
                    pool.wait_ge(idx3, r * 2 + (hf + 1))
                    pool.sem_inc(hold, 1)
                    for b in range(4 * hf, 4 * hf + 4):
                        g.indirect_dma_start(rows[:, b, :], None, h1_table,
                                             bass.IndirectOffsetOnAxis(ap=idx[:, b:b + 1], axis=0),
                                             bounds_check=N - 1, oob_is_err=False).then_inc(h_arrived[hf], 16)
            pool.wait_ge(lot1_added, ADD_CREDIT + ROWS * LOTS)
            g.memset(ysum, 0.0).then_inc(pool_link, 1)
            g.memset(ysum2, 0.0).then_inc(pool_link, 1)
            pool.wait_ge(pool_link, 2)

            def add_y(q, n=P):
                g.tensor_tensor(ysum[0:n, :], ysum[0:n, :], ybuf[0:n, q, :], ALU.add).then_inc(y_summed, 1)
                g.tensor_tensor(ysum2[0:n, :], ysum2[0:n, :], ysq[0:n, q, :], ALU.add).then_inc(y_summed, 1)
            with pool.Fori(0, DENSE_PAIRS) as i:
                for q in range(2):
                    pool.wait_ge(y_kept, i * 4 + (2 * q + 2))
                    pool.sem_inc(hold, 1)
                    add_y(q)
                    pool.wait_ge(y_summed, i * 4 + (2 * q + 2))
                    pool.sem_inc(hold, 1)
            pool.wait_ge(y_kept, 2 * TILES)
            add_y(0, LAST)
            pool.wait_ge(bn2_ready, 1)

            def shift_x1(q, loads):
                pool.wait_ge(x1_in[q], loads)
                pool.sem_inc(hold, 1)
                g.tensor_tensor(x1buf[:, q, :], x1buf[:, q, :], shift2, ALU.add).then_inc(shifted, 1)
            with pool.Fori(0, QUADS) as i:
                for q in range(4):
                    shift_x1(q, i * 16 + 16)
            shift_x1(0, 16 * (QUADS + 1))

        def tail2_scalar(act, link, links, put_indices):
            act.wait_ge(idx2, 2 + 2 * ROWS)
            put_indices(minorB, 0, 0, idx3)
            put_indices(minorB, 0, 1, idx3)
            done = SACT.done
            SPE.wait(act, "hT")
            done(s.copy(hT.rearrange("p k n -> p (k n)"), psA[:, :]), "hT")
            SPE.wait(act, "projT")
            done(s.copy(projT, psE[:, 0:M]), "projT")
            SPE.wait(act, "qT")
            done(s.mul(qT.rearrange("p k n -> p (k n)"), psB[:, :], SCALE), "qT")
            SPE.wait(act, "kT")
            done(s.mul(kT.rearrange("p k n -> p (k n)"), psC[:, :], SCALE), "kT")
            SACT.wait(act, "kT")
            s.activation(squares[:, 0:KD * MAXN], qT.rearrange("p k n -> p (k n)"), ACT.Square)
            done(s.activation(squares[:, KD * MAXN:], kT.rearrange("p k n -> p (k n)"), ACT.Square), "sq")
            for h in hs:
                SPE.wait(act, f"uk{h}")
                done(s.copy(uk[:, h, :, :].rearrange("p t m -> p (t m)"), (psA, psB)[h // 2 % 2][:, h % 2 * 512:h % 2 * 512 + 512]), f"uk{h}")
            SDVE.wait(act, "bk")
            SACT.wait(act, f"uk{H - 1}")
            for h in hs:
                for t in range(NT):
                    ins = s.activation(uk[:, h, t, :], uk[:, h, t, :], ACT.Exp, bias=bias_k[:, 2 * h + t:2 * h + t + 1])
                done(ins, f"ek{h}")

            def exp_q(h):
                SDVE.wait(act, f"bq{h}")
                if h >= 2:
                    SPE.wait(act, f"qfT{h - 2}")
                for t in range(NT):
                    ins = s.activation(qf[:, h % 2, t, :], (psA, psB)[h // 2 % 2][:, h % 2 * 512 + t * M:h % 2 * 512 + (t + 1) * M],
                                       ACT.Exp, bias=bias_q[:, 2 * h + t:2 * h + t + 1])
                done(ins, f"eq{h}")
            exp_q(0)
            for h in hs:
                if h < H - 1:
                    exp_q(h + 1)
                SPE.wait(act, f"qfT{h}")
                if h >= 2:
                    SPE.wait(act, f"at{h - 2}")
                done(s.copy(qfT[:, h % 2, :, :].rearrange("p t n -> p (t n)"), psC[:, h % 2 * 512:h % 2 * 512 + 512]), f"qfT{h}")
            SPE.wait(act, "aT")
            done(s.copy(hT.rearrange("p k n -> p (k n)"), psA[:, :]), "aT")
            SPE.wait(act, "wo")
            done(s.copy(hattn.rearrange("p t d -> p (t d)"), psB[:, :]), "wo")
            act.wait_ge(bn1_step, 4)
            s.activation(sd_c, var_c, ACT.Sqrt, bias=small[:, 0:1]).then_inc(bn1_sd, 1)
            with act.Fori(0, ROWS) as r:
                for hf in range(2):
                    act.wait_ge(h_arrived[hf], r * 64 + 64)
                    act.sem_inc(hold, 1)
                    put_indices(minorB, r + 1, hf, idx3)

            def turn_out(t, q, first=False):
                act.wait_ge(aggT_ps, t + 1)
                if not first:
                    act.wait_ge(conv_ps, t - 1)
                s.copy(aggT[:, q, :], psC[:, q * 512:(q + 1) * 512]).then_inc(aggT_ready, 1)

            def keep_y(t, q, first=False):
                act.wait_ge(y_ready, t + 1)
                act.sem_inc(hold, 1)
                s.copy(acc[:, bass.ds(t, 1), 0:D].rearrange("p a d -> p (a d)"), ybuf[:, q, :]).then_inc(y_kept, 1)
                if not first:
                    act.wait_ge(y_summed, t * 2 - 2)
                s.activation(ysq[:, q, :], ybuf[:, q, :], ACT.Square).then_inc(y_kept, 1)
            turn_out(0, 0, True)
            turn_out(1, 1, True)
            keep_y(0, 0, True)
            turn_out(2, 0)
            keep_y(1, 1, True)
            with act.Fori(1, DENSE_PAIRS) as i:
                for q in range(2):
                    turn_out(i * 2 + (q + 1), 1 - q)
                    keep_y(i * 2 + q, q)
            keep_y(TILES - 1, 0)
            act.wait_ge(bn2_step, 4)
            s.activation(sd2, scale2, ACT.Sqrt, bias=small[:, 0:1]).then_inc(bn2_sd, 1)

        def tail2_vector(dve, link, links, make_onehot, add_lot):
            done = SDVE.done
            dve.wait_ge(h1_ready, 2 * TILES - 1)
            dve.wait_ge(x1_stored, 16 * TILES)
            done(v.memset(acc_flat[:, 0:SCRATCH], 0.0), "cleared")
            dve.wait_ge(colsum_ps, TILES)
            done(v.tensor_copy(colsum, psD[:, 0:8]), "sums")
            done(v.tensor_copy(select_last, ident[:, P - 1:P].broadcast_to([P, P])), "sel")
            done(v.memset(ones_mat, 1.0), "ones_mat")
            done(v.memset(values, 1.0), "ones")
            SDVE.wait(dve, "ones")
            for t, ps in enumerate((psD, psE)):
                SPE.wait(dve, f"v{t}")
                done(v.tensor_copy(values[:, t, :, 0:DH], ps[:, :].rearrange("p (h d) -> p h d", h=H)), f"v{t}")
            SPE.wait(dve, "diag")
            done(v.tensor_copy(dg, psD[:, 0:32]), "diag")

            def half_bank(h):
                return (psA, psB)[h // 2 % 2][:, h % 2 * 512:h % 2 * 512 + 512]
            for h in hs:
                SACT.wait(dve, f"uk{h}")
                done(v.tensor_reduce(mxk[:, h:h + 1], uk[:, h, :, :].rearrange("p t m -> p (t m)"), AX_X, ALU.max), f"mk{h}")
            SPE.wait(dve, "kmT")
            done(v.tensor_reduce(km8[0:H, :], psC[0:H, 0:P], AX_X, ALU.max), "km")
            SDVE.wait(dve, "km")
            done(v.tensor_scalar(kmd[0:H, :], ident[0:H, 0:H], km8[0:H, :], None, ALU.mult), "kmd")
            SPE.wait(dve, "kmB")
            done(v.scalar_tensor_tensor(bias_k.rearrange("p (h t) -> p h t", t=NT),
                                        psC[:, 512:512 + H].unsqueeze(2).broadcast_to([P, H, NT]), -1.0,
                                        dg[:, 16:32].rearrange("p (h t) -> p h t", t=NT), ALU.mult, ALU.subtract), "bk")

            def max_q(h):
                SPE.wait(dve, f"uq{h}")
                m = mxq[:, 2 * h:2 * h + 2]
                done(v.tensor_reduce(m, half_bank(h).rearrange("p (t m) -> p t m", t=NT), AX_X, ALU.max), f"mq{h}")
                SDVE.wait(dve, f"mq{h}")
                done(v.scalar_tensor_tensor(bias_q[:, 2 * h:2 * h + 2], m, -1.0, dg[:, 2 * h:2 * h + 2],
                                            ALU.mult, ALU.subtract), f"bq{h}")
            max_q(0)
            for h in hs:
                SACT.wait(dve, f"ek{h}")
                done(v.tensor_scalar(uk[:, h, :, :], uk[:, h, :, :], M ** -0.5, KEPS, ALU.mult, ALU.add), f"kf{h}")
                SPE.wait(dve, f"kv{h}")
                if h >= 2:
                    SPE.wait(dve, f"at{h - 2}")
                done(v.tensor_copy(kvs[:, h % 2, :, :], psD[:, h % 2 * 256:h % 2 * 256 + MT * (DH + 1)]
                                   .rearrange("p (t d) -> p t d", t=MT)), f"kv{h}")
                if h < H - 1:
                    max_q(h + 1)
                SACT.wait(dve, f"eq{h}")
                done(v.tensor_scalar(qf[:, h % 2, :, :], qf[:, h % 2, :, :], M ** -0.5, KEPS, ALU.mult, ALU.add), f"qf{h}")
                SPE.wait(dve, f"at{h}")
                av = psE[:, h % 2 * 256:h % 2 * 256 + NT * (DH + 1)].rearrange("p (t d) -> p t d", t=NT)
                z = zden[:, 2 * (h % 2):2 * (h % 2) + 2]
                done(v.tensor_scalar(z, av[:, :, DH], KEPS, None, ALU.add), f"zd{h}")
                SDVE.wait(dve, f"zd{h}")
                done(v.reciprocal(z, z), f"zr{h}")
                SDVE.wait(dve, f"zr{h}")
                done(v.tensor_tensor(attn[:, :, h * DH:(h + 1) * DH], av[:, :, 0:DH],
                                     z.unsqueeze(2).broadcast_to([P, NT, DH]), ALU.mult), f"at{h}")
            for t in range(NT):
                if t == 0:
                    SPE.wait(dve, "last")
                    SACT.wait(dve, "wo")
                done(v.tensor_tensor(hattn[:, t, :], hattn[:, t, :], psD[:, :], ALU.subtract), f"hat{t}")
            dve.wait_ge(vec_loaded, 48)
            k = [0]

            def step(ins, wait=True):
                k[0] += 1
                ins.then_inc(bn1_step, 1)
                if wait:
                    dve.wait_ge(bn1_step, k[0])
            step(v.tensor_scalar(mean_c, colsum[:, 0:KD], 1.0 / N, None, ALU.mult))
            step(v.tensor_scalar(var_c, colsum[:, KD:2 * KD], 1.0 / N, None, ALU.mult))
            step(v.tensor_tensor(shift_c, mean_c, mean_c, ALU.mult))
            step(v.tensor_tensor(var_c, var_c, shift_c, ALU.subtract))
            dve.wait_ge(bn1_sd, 1)
            step(v.reciprocal(sd_c, sd_c))
            step(v.tensor_tensor(scale_c, g1c, sd_c, ALU.mult))
            step(v.tensor_tensor(shift_c, mean_c, scale_c, ALU.mult))
            v.tensor_tensor(shift_c, b1c, shift_c, ALU.subtract).then_inc(bn1_shift, 1)
            dve.wait_ge(bn1_ps, 1)
            step(v.tensor_copy(shrow, psE[0:1, :]))
            for n, row in enumerate((shrow, bcrow)):
                for m in range(3):
                    last = n == 1 and m == 2
                    ins = v.tensor_copy(parts1[:, 3 * n + m, :], row)
                    if last:
                        ins.then_inc(parts_ready, 1)
                    else:
                        step(ins)
                    if m < 2:
                        step(v.tensor_tensor(row, row, parts1[:, 3 * n + m, :], ALU.subtract))
            dve.wait_ge(Wc_loaded, 16)
            for kk in range(KD):
                step(v.tensor_scalar(Wc_s[:, kk, :], Wc_s[:, kk, :], scale_c[:, kk:kk + 1], None, ALU.mult))
            step(v.memset(acc_flat[:, SCRATCH:], 0.0))
            dve.sem_inc(lot1_added, ADD_CREDIT)
            make_onehot(nodeB, 0, 0, onehot1_ready)
            with dve.Fori(0, ROWS // 2) as i:
                for q in range(2):
                    tiles = [dve.value_load(tileB[0:1, a, bass.ds(i * 2 + q, 1)], min_val=0, max_val=TILES - 1)
                             for a in range(LOTS)]
                    for a in range(LOTS):
                        if a == 1:
                            dve.wait_ge(lot1_ps, i * 8 + (4 * q + LOT_CREDIT))
                            make_onehot(nodeB, i * 2 + (q + 1), 1 - q, onehot1_ready)
                        dve.wait_ge(lot1_added, i * 8 + (4 * q + a + ADD_CREDIT))
                        dve.wait_ge(lot1_ps, i * 8 + (4 * q + a + 1 + LOT_CREDIT))
                        d = acc[:, bass.ds(tiles[a], 1), 0:D + 1].rearrange("p a d -> p (a d)")
                        v.tensor_tensor(d, d, (psA, psB)[a % 2][:, 0:D + 1], ALU.add).then_inc(lot1_added, 1)
            dve.wait_ge(lot1_added, ADD_CREDIT + ROWS * LOTS)
            v.tensor_scalar(indc, acc[:, :, D], 1.0, None, ALU.min).then_inc(deg_ready, 1)
            link(v.tensor_scalar(rdeg, acc[:, :, D], 1.0, None, ALU.max))
            link(v.reciprocal(rdeg, rdeg))
            dve.wait_ge(bias_stored, 32)
            dve.wait_ge(ind_ps, 1)
            v.memset(ind_rows, 1.0).then_inc(ind_ready, 1)
            v.tensor_copy(indT, psD[0:TILES, 0:P]).then_inc(ind_ready, 1)

            def average(t, q, first=False):
                if not first:
                    dve.wait_ge(aggT_ps, t - 1)
                v.tensor_scalar(aggn[:, q, :], acc[:, bass.ds(t, 1), 0:D].rearrange("p a d -> p (a d)"),
                                rdeg[:, bass.ds(t, 1)], None, ALU.mult).then_inc(aggn_ready, 1)

            def make_y(t, q, loads, first=False):
                dve.wait_ge(conv_ps, t + 1)
                dve.wait_ge(hc_in[q], loads)
                if not first:
                    dve.wait_ge(y_kept, t * 2 - 2)
                    dve.wait_ge(y_summed, t * 2 - 2)
                return v.scalar_tensor_tensor(ybuf[:, q, :], psA[:, q * 512:(q + 1) * 512], 0.0, h_in[:, q, :],
                                              ALU.max, ALU.add)
            average(0, 0, True)
            average(1, 1, True)
            for t in range(NT):
                link(make_y(t, t, 16, True))
                v.tensor_tensor(ybuf[:, t, :], ybuf[:, t, :], hattn[:, t, :], ALU.add).then_inc(y_ready, 1)
                average(t + 2, t)
            with dve.Fori(1, DENSE_PAIRS - 1) as i:
                for q in range(2):
                    make_y(i * 2 + q, q, i * 16 + 16).then_inc(y_ready, 1)
                    average(i * 2 + (q + 2), q)
            for q in range(2):
                make_y(TILES - 3 + q, q, 16 * DENSE_PAIRS).then_inc(y_ready, 1)
                if q == 0:
                    average(TILES - 1, 0)
            make_y(TILES - 1, 0, 16 * (DENSE_PAIRS + 1)).then_inc(y_ready, 1)
            dve.wait_ge(g2_loaded, 32)
            dve.wait_ge(total_ps, 1)
            n2 = [0]

            def step2(ins, signal=bn2_step):
                n2[0] += 1
                ins.then_inc(signal, 1)
                dve.wait_ge(signal, n2[0])
            step2(v.tensor_scalar(mean2, psA[:, 0:D], 1.0 / N, None, ALU.mult))
            step2(v.tensor_tensor(shift2, mean2, mean2, ALU.mult))
            step2(v.tensor_scalar(scale2, psA[:, D:2 * D], 1.0 / N, None, ALU.mult))
            step2(v.tensor_tensor(scale2, scale2, shift2, ALU.subtract))
            dve.wait_ge(bn2_sd, 1)
            step2(v.reciprocal(sd2, sd2))
            step2(v.tensor_tensor(scale2, g2row, sd2, ALU.mult))
            step2(v.tensor_tensor(shift2, mean2, scale2, ALU.mult))
            v.tensor_tensor(shift2, b2row, shift2, ALU.subtract).then_inc(bn2_ready, 1)

            def finish(t, q, stores):
                dve.sem_inc(hold, 1)
                v.tensor_tensor(tbuf[:, q, :], acc[:, bass.ds(t, 1), 0:D].rearrange("p a d -> p (a d)"), scale2,
                                ALU.mult).then_inc(scaled, 1)
                dve.wait_ge(scaled, t + 1)
                dve.wait_ge(shifted, t + 1)
                if stores is not None:
                    dve.wait_ge(out_stored[q], stores)
                v.tensor_tensor(obuf[:, q, :], tbuf[:, q, :], x1buf[:, q, :], ALU.add).then_inc(out_ready, 1)
            for q in range(4):
                finish(q, q, None)
            with dve.Fori(1, QUADS) as i:
                for q in range(4):
                    finish(i * 4 + q, q, i * 16)
            finish(TILES - 1, 0, 16 * QUADS)

        def tail2_tensor(pe):
            done = SPE.done
            pe.wait_ge(hA_loaded, 16)
            for k in range(KD):
                for t in range(NT):
                    ins = pet.transpose(psA[:, k * MAXN + t * P:k * MAXN + (t + 1) * P], hA[:, t, k * P:(k + 1) * P], ident[:, :])
            done(ins, "hT")
            pe.wait_ge(proj_loaded, 32)
            for t in range(MT):
                ins = pet.transpose(psE[:, t * P:(t + 1) * P], proj_s[:, t, :, :].rearrange("p u d -> p (u d)"), ident[:, :])
            done(ins, "projT")
            SACT.wait(pe, "hT")
            pe.wait_ge(Wqkv_loaded, 48)
            for w, ps, name in ((Wq_s, psB, "qT"), (Wk_s, psC, "kT")):
                for j in range(KD):
                    for k in range(KD):
                        ins = pet.matmul(ps[:, j * MAXN:(j + 1) * MAXN], w[:, k, j * P:(j + 1) * P], hT[:, k, :],
                                         start=(k == 0), stop=(k == KD - 1))
                done(ins, name)
            SDVE.wait(pe, "sums")
            for t, ps in enumerate((psD, psE)):
                if t == 1:
                    SACT.wait(pe, "projT")
                for k in range(KD):
                    ins = pet.matmul(ps[:, :], hT[:, k, t * P:(t + 1) * P], Wv_s[:, k, :], start=(k == 0), stop=(k == KD - 1))
                done(ins, f"v{t}")
            SACT.wait(pe, "sq")
            SDVE.wait(pe, "v0")
            for n in range(2):
                for j in range(KD):
                    for t in range(NT):
                        c = n * 16 + 4 * j + t
                        at = n * KD * MAXN + j * MAXN + t * P
                        ins = pet.matmul(psD[:, c:c + 3:2], squares[:, at:at + P], half[:, :], start=True, stop=True)
            done(ins, "diag")

            def half_bank(h):
                return (psA, psB)[h // 2 % 2][:, h % 2 * 512:h % 2 * 512 + 512]

            def features(tT, h, name):
                j, o = h // 2, DH * (h % 2)
                for t in range(NT):
                    ins = pet.matmul(half_bank(h)[:, t * M:(t + 1) * M], tT[o:o + DH, j, t * P:(t + 1) * P],
                                     projT[o:o + DH, :], start=True, stop=True)
                done(ins, f"{name}{h}")
            SACT.wait(pe, "kT")
            for h in hs:
                if h >= 4:
                    SACT.wait(pe, f"uk{h - 4}")
                features(kT, h, "uk")
            SDVE.wait(pe, f"mk{H - 1}")
            done(pet.transpose(psC[0:H, 0:P], mxk, ident[:, :]), "kmT")
            SDVE.wait(pe, "kmd")
            done(pet.matmul(psC[:, 512:512 + H], ones_mat[0:H, :], kmd[0:H, :], start=True, stop=True), "kmB")
            SACT.wait(pe, f"uk{H - 1}")
            features(qT, 0, "uq")
            for h in hs:
                if h < H - 1:
                    if h + 1 >= 4:
                        SACT.wait(pe, f"eq{h - 3}")
                    features(qT, h + 1, "uq")
                SDVE.wait(pe, f"kf{h}")
                SDVE.wait(pe, f"kv{h - 1}" if h >= 1 else "diag")
                for mt in range(MT):
                    c = h % 2 * 256 + mt * (DH + 1)
                    for t in range(NT):
                        ins = pet.matmul(psD[:, c:c + DH + 1], uk[:, h, t, mt * P:(mt + 1) * P], values[:, t, h, :],
                                         start=(t == 0), stop=(t == NT - 1))
                done(ins, f"kv{h}")
                SDVE.wait(pe, f"qf{h}")
                if h >= 2:
                    SACT.wait(pe, f"qfT{h - 2}")
                else:
                    SDVE.wait(pe, "bk")
                for mt in range(MT):
                    for t in range(NT):
                        c = h % 2 * 512 + mt * MAXN + t * P
                        ins = pet.transpose(psC[:, c:c + P], qf[:, h % 2, t, mt * P:(mt + 1) * P], ident[:, :])
                done(ins, f"qfT{h}")
                SACT.wait(pe, f"qfT{h}")
                SDVE.wait(pe, f"kv{h}")
                SDVE.wait(pe, f"at{h - 1}" if h >= 1 else "v1")
                for t in range(NT):
                    c = h % 2 * 256 + t * (DH + 1)
                    for mt in range(MT):
                        ins = pet.matmul(psE[:, c:c + DH + 1], qfT[:, h % 2, mt, t * P:(t + 1) * P], kvs[:, h % 2, mt, :],
                                         start=(mt == 0), stop=(mt == MT - 1))
                done(ins, f"at{h}")
            SDVE.wait(pe, f"at{H - 1}")
            SACT.wait(pe, f"eq{H - 1}")
            for k in range(KD):
                for t in range(NT):
                    ins = pet.transpose(psA[:, k * MAXN + t * P:k * MAXN + (t + 1) * P], attn[:, t, k * P:(k + 1) * P], ident[:, :])
            done(ins, "aT")
            SACT.wait(pe, "aT")
            pe.wait_ge(Wo_loaded, 16)
            for t in range(NT):
                for k in range(KD):
                    ins = pet.matmul(psB[:, t * 512:(t + 1) * 512], hT[:, k, t * P:(t + 1) * P], Wo_s[:, k, :],
                                     start=(k == 0), stop=(k == KD - 1))
            done(ins, "wo")
            SACT.wait(pe, "wo")
            done(pet.matmul(psD[:, :], select_last, hattn[:, NT - 1, :], start=True, stop=True), "last")
            pe.wait_ge(bn1_shift, 1)
            pe.wait_ge(Wc_loaded, 16)
            for k in range(KD):
                ins = pet.matmul(psE[0:1, :], shift_c[:, k:k + 1], Wc_s[:, k, :], start=(k == 0), stop=(k == KD - 1))
            ins.then_inc(bn1_ps, 1)
            pe.sem_inc(lot1_ps, LOT_CREDIT)
            with pe.Fori(0, ROWS // 2) as i:
                for q in range(2):
                    pe.wait_ge(onehot1_ready, i * 2 + (q + 1))
                    for a in range(LOTS):
                        psum = (psA, psB)[a % 2]
                        if a % 2 == 0:
                            pe.wait_ge(h_arrived[a // 2], i * 128 + (64 * q + 64))
                        pe.wait_ge(lot1_added, i * 8 + (4 * q + a + ADD_CREDIT - 1))
                        for b in (2 * a, 2 * a + 1):
                            pet.matmul(psum[:, 0:D], onehot[:, q, b, :], rows[:, b, :], start=(b % 2 == 0), stop=(b % 2 == 1))
                        for b in (2 * a, 2 * a + 1):
                            ins = pet.matmul(psum[:, D:D + 1], onehot[:, q, b, :], ones[:, :],
                                             start=(b % 2 == 0), stop=(b % 2 == 1))
                        ins.then_inc(lot1_ps, 1)
            pe.wait_ge(deg_ready, 1)
            pet.transpose(psD[0:TILES, 0:P], indc, ident[:, :]).then_inc(ind_ps, 1)

            def turn(t, q, first=False):
                pe.wait_ge(aggn_ready, t + 1)
                if not first:
                    pe.wait_ge(aggT_ready, t - 1)
                for k in range(KD):
                    ins = pet.transpose(psC[:, q * 512 + k * P:q * 512 + (k + 1) * P], aggn[:, q, k * P:(k + 1) * P], ident[:, :])
                ins.then_inc(aggT_ps, 1)

            def convolve(t, q, first=False):
                pe.wait_ge(aggT_ready, t + 1)
                if not first:
                    pe.wait_ge(y_ready, t - 1)
                for k in range(KD):
                    pet.matmul(psA[:, q * 512:(q + 1) * 512], aggT[:, q, k * P:(k + 1) * P], Wc_s[:, k, :],
                               start=(k == 0), stop=False)
                pet.matmul(psA[:, q * 512:(q + 1) * 512],
                           ind_rows.rearrange("p (t n) -> p t n", n=P)[:, bass.ds(t, 1), :].rearrange("p a n -> p (a n)"),
                           bias_rows, start=False, stop=True).then_inc(conv_ps, 1)
            turn(0, 0, True)
            turn(1, 1, True)
            pe.wait_ge(ind_spread, 32)
            pe.wait_ge(bias_stored, 32)
            convolve(0, 0, True)
            turn(2, 0)
            convolve(1, 1, True)
            with pe.Fori(1, DENSE_PAIRS) as i:
                for q in range(2):
                    turn(i * 2 + (q + 1), 1 - q)
                    convolve(i * 2 + q, q)
            convolve(TILES - 1, 0)
            pe.wait_ge(y_summed, 2 * TILES)
            for n, total in enumerate((ysum, ysum2)):
                ins = pet.matmul(psA[:, n * 512:(n + 1) * 512], ones_mat, total, start=True, stop=True)
            ins.then_inc(total_ps, 1)

        N_CONST = 12

        @block.sync
        def _(sp):
            def load_keys(order, signal):
                for edge_end, place in zip(order, (wk1, wk2)):
                    sp.dma_start(place[0:EDGE_ROWS, 0:EDGE_COLS].bitcast(I32),
                                 edge_end.rearrange("(p c) -> p c", c=EDGE_COLS)).then_inc(signal, 16)
            load_keys((src, dst), keys_loaded)
            for a in range(0, TILES - 1, 12):
                sp.dma_start(acc[:, a:a + 12, 0:D],
                             x[a * P:(a + 12) * P, :].rearrange("(t p) d -> p t d", p=P)).then_inc(x_loaded, 16)
            for k in range(KD):
                sp.dma_start(W4[:, k, :, :], W0[:, k * P:(k + 1) * P, :].rearrange("h p o -> p h o")).then_inc(w0_loaded, 16)
            sp.dma_start(attb.rearrange("p h a o -> p (h a o)"),
                         att_w.rearrange("h a -> (h a)").rearrange("(u c) -> u c", u=1).broadcast_to([P, H * 2 * O])
                         ).then_inc(w0_loaded, 16)
            sp.wait_ge(consts, N_CONST)
            sp.dma_start(acc[0:LAST, TILES - 1, 0:D], x[(TILES - 1) * P:N, :]).then_inc(x_loaded, 16)
            with sp.Fori(0, DENSE_PAIRS) as i:
                for q in range(2):
                    sp.wait_ge(feat_ready, i * 2 + (q + 1))
                    sp.dma_start(feat_table[bass.ds(i * (2 * P) + q * P, P), :], fbuf[:, q, :]).then_inc(feat_stored[q], 16)
            sp.wait_ge(feat_ready, TILES)
            sp.dma_start(feat_table[(TILES - 1) * P:TILES * P, :], fbuf[:, 0, :]).then_inc(feat_stored[0], 16)
            sp.dma_start(ad_table.rearrange("(t p) h -> p t h", p=P), alphas[:, :, H:2 * H]).then_inc(ad_stored, 16)
            sp.wait_ge(fields, 1)
            sp.dma_start(slot_nodes, oh_flat.bitcast(BF16)[:, 0:COLS]).then_inc(slots_stored, 16)
            sp.wait_ge(keysB_free, 1)
            load_keys((dst, src), keys_loaded2)
            tail_sync(sp)


        @block.gpsimd
        def _(pool):
            c = [0]

            def const(ins, wait=False):
                ins.then_inc(consts, 1)
                c[0] += 1
                if wait:
                    pool.wait_ge(consts, c[0])
            const(g.memset(acc[:, TILES - 1, 0:D], 0.0))
            const(g.memset(ident[:, :], 0.0))
            const(g.memset(spread, 0.0), wait=True)
            const(g.affine_select(out=ident[:, :], in_=ident[:, :], compare_op=ALU.not_equal, fill=1.0, base=0,
                                  pattern=[[-1, P]], channel_multiplier=1))
            sp3 = spread.rearrange("p (r h) -> p r h", h=H)
            const(g.affine_select(out=sp3, in_=sp3, compare_op=ALU.not_equal, fill=1.0, base=0,
                                  pattern=[[-1, P], [0, H]], channel_multiplier=1))
            const(g.iota(part[:, 0:1], [[0, 1]], base=0, channel_multiplier=1))
            const(g.iota(iota_pad[:, :], [[1, PAD_COLS]], base=0, channel_multiplier=0,
                         allow_small_or_imprecise_dtypes=True))
            const(g.iota(iota_row[:, :], [[1, P]], base=0, channel_multiplier=0, allow_small_or_imprecise_dtypes=True))
            const(g.iota(iota_col[:, :], [[0, 1]], base=0, channel_multiplier=1, allow_small_or_imprecise_dtypes=True))
            const(g.memset(staged_ad[:, :, :], 0.0))
            const(g.memset(onesb[:, :], 1.0))
            const(g.memset(small[:, 0:1], LN_EPS))
            assert c[0] == N_CONST
            pool.wait_ge(ad_stored, 16)
            with pool.Fori(0, ROWS_G) as r:
                for hf in range(2):
                    pool.wait_ge(idx1, r * 2 + (hf + 1))
                    pool.sem_inc(hold, 1)
                    for b in range(4 * hf, 4 * hf + 4):
                        g.indirect_dma_start(staged_ad[:, b, :], None, ad_table,
                                             bass.IndirectOffsetOnAxis(ap=idx[:, b:b + 1], axis=0),
                                             bounds_check=N - 1, oob_is_err=False).then_inc(ad_arrived[hf], 16)
            tail_gpsimd(pool)

        @block.scalar
        def _(act):
            links = [0]

            def link(ins):
                links[0] += 1
                ins.then_inc(act_link, 1)
                act.wait_ge(act_link, links[0])
            act.wait_ge(consts, N_CONST)
            act.wait_ge(x_loaded, 16 * 5)
            def statistics(function, column):
                for t in range(TILES):
                    if t >= 2:
                        act.wait_ge(act_link, links[0] - 1)
                    s.activation(junk[:, t % 2, :], acc[:, t, 0:D], function,
                                 accum_out=stat[:, column, t:t + 1]).then_inc(act_link, 1)
                    links[0] += 1
                act.wait_ge(act_link, links[0])
            statistics(ACT.Identity, 0)
            link(s.mul(stat[:, 1, :], stat[:, 0, :], -1.0 / D))
            for t in range(TILES):
                if t >= 2:
                    act.wait_ge(act_link, links[0] - 1)
                s.activation(junk[:, t % 2, :], acc[:, t, 0:D], ACT.Square, bias=stat[:, 1, t:t + 1],
                             accum_out=stat[:, 2, t:t + 1]).then_inc(act_link, 1)
                links[0] += 1
            act.wait_ge(act_link, links[0])
            s.activation(stat[:, 3, :], stat[:, 2, :], ACT.Sqrt, scale=1.0 / D, bias=small[:, 0:1]).then_inc(var_ready, 1)
            act.wait_ge(rstd_ready, 1)

            def make_h(t, q):
                s.activation(hbuf[:, q, :], acc[:, bass.ds(t, 1), 0:D].rearrange("p a d -> p (a d)"), ACT.Relu,
                             scale=stat[:, 3, bass.ds(t, 1)], bias=stat[:, 1, bass.ds(t, 1)]).then_inc(h_ready, 1)

            def evacuate(t, q, stores):
                act.wait_ge(hT_ps, t + 1)
                s.copy(hTbuf[:, q, :], psC[:, q * D:(q + 1) * D]).then_inc(hT_ready, 1)
                act.wait_ge(feat_ps, t + 1)
                s.copy(alphas[:, bass.ds(t, 1), :], psE[:, 32 * q:32 * q + 16].rearrange("p (a c) -> p a c", a=1))
                if stores is not None:
                    act.wait_ge(feat_stored[q], stores * 16)
                    act.sem_inc(hold, 1)
                s.copy(fbuf[:, q, :], psB[:, q * D:(q + 1) * D]).then_inc(feat_ready, 1)

            make_h(0, 0)
            make_h(1, 1)
            evacuate(0, 0, None)
            act.wait_ge(hT_ps, 1)
            make_h(2, 0)
            evacuate(1, 1, None)
            with act.Fori(1, DENSE_PAIRS) as i:
                for q in range(2):
                    act.wait_ge(hT_ps, i * 2 + q)
                    act.sem_inc(hold, 1)
                    make_h(i * 2 + (q + 1), 1 - q)
                    evacuate(i * 2 + q, q, i)
            evacuate(TILES - 1, 0, DENSE_PAIRS)
            act.wait_ge(slotsA, 1)
            act.wait_ge(feat_stored[0], 16 * (DENSE_PAIRS + 1))
            act.wait_ge(feat_stored[1], 16 * DENSE_PAIRS)
            for hf in range(2):
                s.copy(idx[:, 4 * hf:4 * hf + 4], minorA[:, 4 * hf:4 * hf + 4, 0]).then_inc(idx1, 1)
            with act.Fori(0, ROWS_G) as r:
                for hf in range(2):
                    bs = slice(4 * hf, 4 * hf + 4)
                    act.wait_ge(ad_arrived[hf], r * 64 + 64)
                    act.sem_inc(hold, 1)
                    s.copy(gathered_ad[:, bs, bass.ds(r, 1), :].rearrange("p b a h -> p b (a h)"),
                           staged_ad[:, bs, :]).then_inc(ad_kept, 1)
                    act.wait_ge(ad_kept, r * 2 + (hf + 1))
                    act.sem_inc(hold, 1)
                    s.copy(idx[:, bs], minorA[:, bs, bass.ds(r + 1, 1)].rearrange("p b a -> p (b a)")).then_inc(idx1, 1)
            tail_scalar(act, link, links)

        @block.vector
        def _(dve):
            links = [0]

            def link(ins):
                links[0] += 1
                ins.then_inc(dve_link, 1)
                dve.wait_ge(dve_link, links[0])

            dve.wait_ge(consts, N_CONST)
            v.memset(ones[:, :], 1.0).then_inc(dve_link, 1)
            v.memset(half[:, :], 0.0).then_inc(dve_link, 1)
            links[0] += 2
            dve.wait_ge(dve_link, links[0])
            for u in range(2):
                link(v.memset(half[u * DH:(u + 1) * DH, u:u + 1], 0.5))
            link(v.tensor_scalar(part[:, 2:3], part[:, 0:1], 1, None, ALU.logical_shift_right))
            link(v.tensor_scalar(part[:, 3:4], part[:, 0:1], 1, None, ALU.bitwise_and))
            link(v.tensor_tensor(part[:, 1:2], part[:, 0:1], part[:, 2:3], ALU.bitwise_xor))
            link(v.tensor_scalar(signi[:, 0:1], part[:, 0:1], 1, None, ALU.bitwise_and))
            for k in range(ALL_BITS - ROW_BITS):
                link(v.tensor_scalar(signi[:, k + 1:k + 2], part[:, 1:2], k, 1, ALU.logical_shift_right, ALU.bitwise_and))
            link(v.tensor_scalar(signs[:, :], signi[:, :], -2.0, 1.0, ALU.mult, ALU.add))
            link(v.tensor_scalar(padc[:, 0:1], part[:, 3:4], float(PAD_COLS), None, ALU.mult))
            link(v.tensor_scalar(padc[:, 1:2], part[:, 2:3], float(P), float(P - 1 - NO_NODE), ALU.mult, ALU.add))
            link(v.tensor_scalar(iota_pad[:, :], iota_pad[:, :], padc[:, 0:1], None, ALU.add))

            steps = [0]

            def prepare(turn):
                major = wk1[0:EDGE_ROWS, 0:EDGE_COLS].bitcast(I32)
                minor = wk2[0:EDGE_ROWS, 0:EDGE_COLS].bitcast(I32)
                key = keyX.bitcast(I32)
                edge_key = key[0:EDGE_ROWS, 0:EDGE_COLS]
                link(v.tensor_scalar(edge_key, major, P.bit_length() - 1, None, ALU.logical_shift_right))
                link(v.tensor_copy(keyY[0:EDGE_ROWS, 0:EDGE_COLS], edge_key))
                link(v.memset(count[:, :, :], 0.0))
                thrown = keyX.bitcast(BF16).rearrange("p (a c) -> p a c", a=2)
                for j in range(TILES):
                    if j >= 2:
                        dve.wait_ge(dve_link, links[0] - 1)
                    v.tensor_scalar(thrown[0:EDGE_ROWS, j % 2, 0:EDGE_COLS], keyY[0:EDGE_ROWS, 0:EDGE_COLS], float(j),
                                    None, ALU.is_equal, ALU.add,
                                    accum_out=count[0:EDGE_ROWS, j, 0:1]).then_inc(dve_link, 1)
                    links[0] += 1
                dve.wait_ge(dve_link, links[0])
                v.tensor_copy(count[:, :, 1:2], count[:, :, 0:1]).then_inc(counted, 1)
                link(v.memset(key, (NO_NODE << SHIFT) | MINOR_MASK | KEY_BASE))
                link(v.tensor_scalar(edge_key, major, SHIFT, KEY_BASE, ALU.logical_shift_left, ALU.bitwise_or))
                link(v.tensor_tensor(edge_key, edge_key, minor, ALU.bitwise_or))
                dve.wait_ge(pads_known, turn)
                link(v.tensor_scalar(padi[:, 0:1], psD[:, 0:1], -1.0, float(1 << ALL_BITS), ALU.mult, ALU.add))
                link(v.tensor_scalar(padi[:, 1:2], padi[:, 0:1], LOT - 1, None, ALU.bitwise_and))
                link(v.tensor_copy(padc[:, 2:3], padi[:, 1:2]))
                pads = keyY[:, EDGE_COLS:COLS]
                link(v.tensor_scalar(pads, iota_pad[:, :], padc[:, 2:3], padc[:, 1:2], ALU.is_lt, ALU.mult))
                link(v.tensor_scalar(pads.bitcast(I32), pads, float(NO_NODE), None, ALU.add))
                link(v.tensor_scalar(key[:, EDGE_COLS:COLS], pads.bitcast(I32), SHIFT, MINOR_MASK | KEY_BASE,
                                     ALU.logical_shift_left, ALU.bitwise_or))
                v.tensor_scalar(keyY, keyX, signs[:, 0:1], None, ALU.mult).then_inc(sort_step, 1)
                steps[0] += 1

            def stage(j, mirror, source, target):
                dve.wait_ge(sort_step, steps[0])

                def halves(buf):
                    w = buf.rearrange("p (n two h) -> p n two h", two=2, h=1 << j)
                    return w[:, :, 0, :], (w[:, :, 1, ::-1] if mirror else w[:, :, 1, :])
                (a, b), (low, high) = halves(source), halves(target)
                if source is psA_all:
                    copied = wk1[:, 0:COLS // 2].rearrange("p (n h) -> p n h", h=1 << j)
                    v.tensor_copy(copied, a).then_inc(sort_step, 1)
                    steps[0] += 1
                    dve.wait_ge(sort_step, steps[0])
                    a = copied
                v.tensor_tensor(low, a, b, ALU.min).then_inc(sort_step, 1)
                v.tensor_tensor(high, a, b, ALU.max).then_inc(sort_step, 1)
                steps[0] += 2

            psA_all = psA[:, :]

            def sort(turns, plan, between=None):
                bufs, at = (keyX, keyY), 1
                for m in range(1, ROW_BITS + 1):
                    for j in range(m - 1, -1, -1):
                        stage(j, j == m - 1 and j > 0, bufs[at], bufs[at ^ 1])
                        at ^= 1
                if between:
                    between()
                n = 0
                for m in range(ROW_BITS + 1, ALL_BITS + 1):
                    dve.wait_ge(sort_step, steps[0])
                    v.tensor_scalar(bufs[at ^ 1], bufs[at], signs[:, m - ROW_BITS:m - ROW_BITS + 1], None,
                                    ALU.mult).then_inc(sort_step, 1)
                    steps[0] += 1
                    at ^= 1
                    for js in (range(m - ROW_BITS - 1, -1, -1), range(ROW_BITS - 1, -1, -1)):
                        assert plan[n] == (steps[0], at), (plan[n], steps[0], at)
                        n += 1
                        dve.wait_ge(turned, turns + n)
                        for i, j in enumerate(js):
                            stage(j, False, psA_all if i == 0 else bufs[at], bufs[at ^ 1])
                            at ^= 1
                dve.wait_ge(sort_step, steps[0])
                return bufs[at], bufs[at ^ 1]

            def wait_rstd():
                dve.wait_ge(var_ready, 1)
                link(v.reciprocal(stat[:, 3, :], stat[:, 3, :]))
                v.tensor_tensor(stat[:, 1, :], stat[:, 1, :], stat[:, 3, :], ALU.mult).then_inc(rstd_ready, 1)

            def slot_fields(sorted_keys, other, minor_t, node_t, tile_t, turns, with_last):
                bits = sorted_keys.bitcast(I32)
                seg = wk1.bitcast(I32)
                link(v.tensor_scalar(seg, bits, SHIFT, None, ALU.logical_shift_right))
                link(v.tensor_scalar(seg, seg, P - 1, None, ALU.bitwise_and))
                link(v.tensor_scalar(other.bitcast(I32), bits, MINOR_MASK, None, ALU.bitwise_and))
                link(v.tensor_scalar(other, other.bitcast(I32), float(MINOR_MASK), OFF, ALU.is_equal, ALU.mult))
                link(v.tensor_tensor(wk2, other, seg, ALU.add))
                if with_last:
                    link(v.memset(same, 0.0))
                    link(v.tensor_tensor(same[:, 1:COLS], wk2[:, 1:COLS], wk2[:, 0:COLS - 1], ALU.is_equal))
                    link(v.memset(same[:, 0:COLS:P], 0.0))
                    dve.wait_ge(Wa_ready, 1)
                    v.tensor_copy(oh_flat.bitcast(BF16)[:, 0:COLS], wk2).then_inc(fields, 1)
                    v.scalar_tensor_tensor(wk1, same[:, 1:COLS + 1], OFF, wk2, ALU.mult, ALU.add).then_inc(fields, 1)
                else:
                    v.tensor_copy(small[:, 1:2], small[:, 0:1]).then_inc(fields, 1)
                dve.wait_ge(fieldsT, turns)
                bitsT = psA[:, :].bitcast(I32)
                link(v.tensor_scalar(minor_t[:, :, :].rearrange("p b r -> p (b r)"), bitsT, MINOR_MASK, None,
                                     ALU.bitwise_and))
                link(v.tensor_scalar(tile_t[:, :, :],
                                     bitsT[0:1, :].rearrange("p (a two r) -> p a two r", two=2, r=P)[:, :, 0, :],
                                     SHIFT + 7, 63, ALU.logical_shift_right, ALU.bitwise_and))
                link(v.tensor_scalar(tile_t[:, :, :], tile_t[:, :, :], float(TILES - 1), None, ALU.min))
                link(v.tensor_copy(node_t[:, :, :].rearrange("p b r -> p (b r)"), psB[:, :]))
                if with_last:
                    link(v.tensor_copy(lastA[:, :, :].rearrange("p b r -> p (b r)"), psC[:, :]))

            dve.wait_ge(w0_loaded, 16 * 5)
            for a in range(2):
                link(v.tensor_tensor(Wprod, W4, attb[:, :, a, :].unsqueeze(1).broadcast_to([P, KD, H, O]), ALU.mult))
                ins = v.tensor_reduce(Wa[:, :, a * H:(a + 1) * H], Wprod, AX_X, ALU.add)
                if a == 0:
                    link(ins)
                else:
                    ins.then_inc(Wa_ready, 1)
            dve.wait_ge(keys_loaded, 32)
            prepare(1)
            kA, other = sort(0, planA, wait_rstd)
            slot_fields(kA, other, minorA, nodeA, tileA, 1, True)
            v.memset(small[:, 2:3], 0.0).then_inc(slotsA, 1)

            dve.wait_ge(slots_stored, 16)
            v.memset(small[:, 3:4], 0.0).then_inc(keysB_free, 1)
            dve.wait_ge(keys_loaded2, 32)
            prepare(2)
            kB, other = sort(CROSSINGS, planB)
            slot_fields(kB, other, minorB, nodeB, tileB, 2, False)
            v.memset(small[:, 4:5], 0.0).then_inc(sortB_done, 1)

            dve.wait_ge(feat_ready, TILES)
            link(v.memset(acc_flat, 0.0))
            link(v.memset(maxd[:, :, :], -BIG))
            link(v.memset(runmaxE, 1.0))
            for gr in range(GROUPS):
                dve.wait_ge(adT, 2 * gr + 2)
                link(v.tensor_scalar(mask, psB[:, :], BIG, -BIG, ALU.mult, ALU.add))
                v.tensor_tensor_scan(runmax, mask, psA[:, :], 0.0, ALU.add, ALU.max).then_inc(scanned, 1)
                dve.wait_ge(scanT, gr + 1)
                link(v.tensor_copy(runmaxE[:, :, :, 0:H], psC[:, :].rearrange("p (b r h) -> p b r h", b=SB, r=GROUP)))
                with dve.Fori(0, GROUP // 2) as i:
                    for q in range(2):
                        v.tensor_tensor(onehot[:, q, :, :], iota_row[:, :].unsqueeze(1).broadcast_to([P, SB, P]),
                                        lastA[:, :, bass.ds(i * 2 + (gr * GROUP + q), 1)].broadcast_to([P, SB, P]),
                                        ALU.is_equal).then_inc(last_ready, 1)
                    for q in range(2):
                        ps = (psD, psE)[q][:, 0:SB * (H + 1)].rearrange("p (b h) -> p b h", h=H + 1)
                        pen = small[:, 8 + 8 * q:16 + 8 * q]
                        both = zbuf_small(q)
                        dve.wait_ge(slotmax, i * 2 + (gr * GROUP + q + 1))
                        v.tensor_scalar(pen, ps[:, :, H], BIG, -BIG, ALU.mult, ALU.add).then_inc(taken, 1)
                        base = gr * GROUP * 7 + q * 7
                        dve.wait_ge(taken, i * 14 + (base + 1))
                        v.tensor_tensor(both, ps[:, :, 0:H], pen.unsqueeze(2).broadcast_to([P, SB, H]),
                                        ALU.add).then_inc(taken, 1)
                        dve.wait_ge(taken, i * 14 + (base + 2))
                        pair = both.rearrange("p (a two) h -> p a two h", two=2)
                        lotmax = small[:, 24 + 32 * q:56 + 32 * q].rearrange("p (a h) -> p a h", h=H)
                        v.tensor_tensor(lotmax, pair[:, :, 0, :], pair[:, :, 1, :], ALU.max).then_inc(taken, 1)
                        for a in range(LOTS):
                            t = dve.value_load(tileA[0:1, a, bass.ds(i * 2 + (gr * GROUP + q), 1)],
                                               min_val=0, max_val=TILES - 1)
                            dve.wait_ge(taken, i * 14 + (base + 3 + a))
                            m = maxd[:, bass.ds(t, 1), :].rearrange("p a h -> p (a h)")
                            v.tensor_tensor(m, m, lotmax[:, a, :], ALU.max).then_inc(taken, 1)
            dve.wait_ge(taken, GROUPS * GROUP * 7)
            c_part = alphas[:, :, H:2 * H]
            link(v.tensor_tensor(maxd[:, :, :], alphas[:, :, 0:H], maxd[:, :, :], ALU.add))
            dve.wait_ge(ad_stored, 16)
            link(v.scalar_tensor_tensor(c_part, maxd[:, :, :], SLOPE, maxd[:, :, :], ALU.mult, ALU.max))
            rest = wk2[:, 0:TILES * 2 * H].rearrange("p (t c) -> p t c", c=2 * H)
            link(v.tensor_copy(look[:, :, 0, :], alphas[:, :, :]))
            link(v.tensor_tensor(rest, alphas[:, :, :], look[:, :, 0, :], ALU.subtract))
            link(v.tensor_copy(look[:, :, 1, :], rest))
            link(v.tensor_tensor(rest, rest, look[:, :, 1, :], ALU.subtract))
            v.tensor_copy(look[:, :, 2, :], rest).then_inc(look_ready, 1)
            tail_vector(dve, link, links)

        @block.tensor
        def _(pe):
            pe.wait_ge(consts, N_CONST)

            def cross(plan, n):
                step, at = plan[n]
                pe.wait_ge(sort_step, step)
                for b in range(SB):
                    ins = pet.transpose(psA[:, b * P:(b + 1) * P], keys[:, at, b * P:(b + 1) * P], ident[:, :])
                ins.then_inc(turned, 1)

            def count_pads(turn):
                pe.wait_ge(counted, turn)
                pet.matmul(psD[:, 0:1], count[:, :, :].rearrange("p a b -> p (a b)"), ones[:, :],
                           start=True, stop=True).then_inc(pads_known, 1)

            def dense(t, q, first):
                pe.wait_ge(h_ready, t + 1)
                if not first:
                    pe.wait_ge(hT_ready, t - 1)
                for k in range(KD):
                    ins = pet.transpose(psC[:, q * D + k * P:q * D + (k + 1) * P], hbuf[:, q, k * P:(k + 1) * P],
                                        ident[:, :])
                ins.then_inc(hT_ps, 1)
                pe.wait_ge(hT_ready, t + 1)
                if not first:
                    pe.wait_ge(feat_ready, t - 1)
                for k in range(KD):
                    pet.matmul(psB[:, q * D:(q + 1) * D], hTbuf[:, q, k * P:(k + 1) * P],
                               W4[:, k, :, :].rearrange("p h o -> p (h o)"), start=(k == 0), stop=(k == KD - 1))
                for k in range(KD):
                    ins = pet.matmul(psE[:, 32 * q:32 * q + 16], hTbuf[:, q, k * P:(k + 1) * P], Wa[:, k, :],
                                     start=(k == 0), stop=(k == KD - 1))
                ins.then_inc(feat_ps, 1)

            count_pads(1)
            pe.wait_ge(Wa_ready, 1)
            done_pairs = 0
            for n in range(CROSSINGS):
                cross(planA, n)
                upto = share[n]
                if done_pairs == 0 and upto > 0:
                    dense(0, 0, True)
                    dense(1, 1, True)
                    done_pairs = 1
                if upto > done_pairs:
                    with pe.Fori(done_pairs, upto) as i:
                        for q in range(2):
                            dense(i * 2 + q, q, False)
                    done_pairs = upto
            dense(TILES - 1, 0, False)

            def turn_fields(at, turn, with_last):
                pe.wait_ge(sort_step, (stepsA, stepsB)[turn - 1])
                pe.wait_ge(fields, (2, 3)[turn - 1])
                if with_last:
                    pe.wait_ge(feat_ready, TILES)
                for source, target in ((keys[:, at, :], psA), (wk2, psB)) + (((wk1, psC),) if with_last else ()):
                    for b in range(SB):
                        ins = pet.transpose(target[:, b * P:(b + 1) * P], source[:, b * P:(b + 1) * P], ident[:, :])
                ins.then_inc(fieldsT, 1)

            turn_fields(atA, 1, True)
            count_pads(2)
            pe.wait_ge(slotsA, 1)
            for n in range(CROSSINGS):
                cross(planB, n)
            turn_fields(atB, 2, False)
            pe.wait_ge(sortB_done, 1)

            for gr in range(GROUPS):
                pe.wait_ge(ad_kept, 2 * GROUP * (gr + 1))
                for b in range(SB):
                    ins = pet.transpose(psA[:, b * P:(b + 1) * P],
                                        gathered_ad[:, b, gr * GROUP:(gr + 1) * GROUP, :].rearrange("p r h -> p (r h)"),
                                        ident[:, :])
                ins.then_inc(adT, 1)
                for c in range(2):
                    ins = pet.matmul(psB[:, c * 512:(c + 1) * 512], spread[:, gr * P:(gr + 1) * P],
                                     same[:, c * 512:(c + 1) * 512], start=True, stop=True)
                ins.then_inc(adT, 1)
                pe.wait_ge(scanned, gr + 1)
                for b in range(SB):
                    ins = pet.transpose(psC[:, b * P:(b + 1) * P], runmax[:, b * P:(b + 1) * P], ident[:, :])
                ins.then_inc(scanT, 1)
                with pe.Fori(0, GROUP // 2) as i:
                    for q in range(2):
                        pe.wait_ge(last_ready, i * 2 + (gr * GROUP + q + 1))
                        for b in range(SB):
                            ins = pet.matmul((psD, psE)[q][:, b * (H + 1):(b + 1) * (H + 1)], onehot[:, q, b, :],
                                             runmaxE[:, b, bass.ds(i * 2 + q, 1), :].rearrange("p a h -> p (a h)"),
                                             start=True, stop=True)
                        ins.then_inc(slotmax, 1)
            tail_tensor(pe)



_INS = ['x', 'src', 'dst', 'L0_gnn_W', 'L0_gnn_att_w', 'L1_gnn_norm1_g', 'L1_gnn_norm1_b', 'L1_gnn_norm2_g',
        'L1_gnn_norm2_b', 'L1_gnn_W_conv', 'L1_gnn_b_conv', 'L1_gnn_Wq', 'L1_gnn_Wk', 'L1_gnn_Wv', 'L1_gnn_Wo',
        'L1_gnn_proj']


def kernel(**inputs):
    import numpy as _np
    import concourse.bacc as _bacc
    from concourse import mybir as _mybir
    from concourse.bass_utils import run_bass_kernel_spmd as _run

    nc = _bacc.Bacc("TRN2", target_bir_lowering=False, num_devices=1)
    arrays, args = {}, []
    for name in _INS:
        a = _np.ascontiguousarray(inputs[name])
        arrays[f"in_{name}_dram"] = a
        args.append(nc.dram_tensor(f"in_{name}_dram", a.shape, _mybir.dt.from_np(a.dtype), kind="ExternalInput").ap())
    args.append(nc.dram_tensor("out_0_dram", (N, D), _mybir.dt.float32, kind="ExternalOutput").ap())
    build(nc, *args)
    r = _run(nc, [arrays], core_ids=[0])
    return r.results[0]["out_0_dram"]
```

```python
from contextlib import ExitStack

import concourse.bass as bass
from concourse import mybir

P = 128
F32 = mybir.dt.float32
BF16 = mybir.dt.bfloat16
I32 = mybir.dt.int32
I16 = mybir.dt.int16
ALU = mybir.AluOpType
ACT = mybir.ActivationFunctionType
AX_X = mybir.AxisListType.X

N = 6250
E = 100000
D = 512
KD = D // P
H, O = 8, 64
TILES = (N + P - 1) // P
LAST = N - (TILES - 1) * P
ACC_W = D + H
LN_EPS = 1e-5
KEPS = 1e-6
SLOPE = 0.2
BIG = 1e30

COLS = 1024
ROW_BITS = 10
ALL_BITS = 17
EDGE_ROWS, EDGE_COLS = 125, 800
PAD_COLS = COLS - EDGE_COLS
LOT = 256
SHIFT = 13
MINOR_MASK = (1 << SHIFT) - 1
KEY_BASE = 0x20000000
NO_NODE = TILES * P + P - 1
assert EDGE_ROWS * EDGE_COLS == E and 2 * PAD_COLS >= LOT - 1 and 2 * TILES <= P and P * COLS == 1 << ALL_BITS

SB = COLS // P
LOTS = SB // 2
ROWS = -(-(E + TILES * (LOT - 1)) // COLS)
GROUP = 16
GROUPS = -(-ROWS // GROUP)
ROWS_G = GROUPS * GROUP
OFF = 128.0
assert ROWS % 2 == 0

MAXN = 256
NT = MAXN // P
M = 256
MT = M // P
DH = 64
SCALE = DH ** -0.25


class Steps:

    def __init__(self, sem, names):
        self.sem, self.names, self.n = sem, list(names), 0
        self.at = {name: i + 1 for i, name in enumerate(self.names)}
        assert len(self.at) == len(self.names)

    def done(self, instruction, name):
        assert self.names[self.n] == name, (self.names[self.n], name)
        self.n += 1
        instruction.then_inc(self.sem, 1)

    def wait(self, engine, name):
        engine.wait_ge(self.sem, self.at[name])


def build(nc, x, src, dst, W0, att_w, norm1_g, norm1_b, norm2_g, norm2_b, W_conv, b_conv, Wq, Wk, Wv, Wo, proj, out):
    with ExitStack() as ctx:
        def sb(name, shape, dt):
            return ctx.enter_context(nc.sbuf_tensor(name, shape, dt))

        def pb(name, shape, dt):
            return ctx.enter_context(nc.psum_tensor(name, shape, dt))

        def sem(name):
            return ctx.enter_context(nc.semaphore(name))

        v, s, g, pet = nc.vector, nc.scalar, nc.gpsimd, nc.tensor

        feat_table = nc.dram_tensor("feat_table", (TILES * P, D), F32).ap()
        ad_table = nc.dram_tensor("ad_table", (TILES * P, H), F32).ap()
        slot_nodes = nc.dram_tensor("slot_nodes", (P, COLS), BF16).ap()
        x1_table = nc.dram_tensor("x1_table", (TILES * P, D), F32).ap()
        ind_table = nc.dram_tensor("ind_table", (TILES, P), BF16).ap()
        bias_table = nc.dram_tensor("bias_table", (6, D), BF16).ap()
        h1_table = nc.dram_tensor("h1_table", (TILES * P, D), F32).ap()

        acc = sb("acc", [P, TILES, ACC_W], F32)
        gathered_ad = sb("gathered_ad", [P, SB, ROWS_G, H], F32)
        keys = sb("keys", [P, 2, COLS], F32)
        wk = sb("wk", [P, 2, COLS], F32)
        minorA = sb("minorA", [P, SB, P], I16)
        minorB = sb("minorB", [P, SB, P], I16)
        nodeA = sb("nodeA", [P, SB, P], BF16)
        nodeB = sb("nodeB", [P, SB, P], BF16)
        lastA = sb("lastA", [P, SB, P], BF16)
        tables = sb("tables", [P, 2, LOTS, P], I32)
        tileA = tables[0:1, 0, :, :]
        tileB = tables[0:1, 1, :, :]
        rows = sb("rows", [P, SB, D], F32)
        rows2 = sb("rows2", [P, SB // 2, D], F32)
        onehot = sb("onehot", [P, 2, SB, P], F32)
        ident = sb("ident", [P, P], F32)
        iota_row = sb("iota_row", [P, P], F32)
        iota_col = sb("iota_col", [P, 1], F32)
        iota_pad = sb("iota_pad", [P, PAD_COLS], F32)
        ones = sb("ones", [P, 1], F32)
        half = sb("half", [P, 2], F32)
        one_b = sb("one_b", [P, 1], BF16)
        part = sb("part", [P, 4], I32)
        padc = sb("padc", [P, 4], F32)
        padi = sb("padi", [P, 2], I32)
        signi = sb("signi", [P, 8], I32)
        signs = sb("signs", [P, 8], F32)
        count = sb("count", [P, P // 2, 2], F32)
        look = sb("look", [P, TILES, 3, 2 * H], BF16)
        alphas = sb("alphas", [P, TILES, 2 * H], F32)
        maxd = sb("maxd", [P, TILES, H], F32)
        Wa = sb("Wa", [P, KD, 2 * H], F32)
        stat = sb("stat", [P, 4, TILES], F32)
        idx = sb("idx", [P, 2, SB], I32)
        zbuf = sb("zbuf", [P, 6, SB, H], F32)
        staged_ad = sb("staged_ad", [P, SB, H], F32)
        wts = sb("wts", [P, 2, SB, H], F32)
        wrest = sb("wrest", [P, SB, H], F32)
        ident_bf = sb("ident_bf", [P, P], BF16)
        ident_b = ident_bf[:, :]
        small = sb("small", [P, 96], F32)

        keyX, keyY = keys[:, 0, :], keys[:, 1, :]
        wk1, wk2 = wk[:, 0, :], wk[:, 1, :]
        acc_flat = acc[:, :, :].rearrange("p t w -> p (t w)")
        look_flat = look[:, :, :, :].rearrange("p t a b -> p (t a b)")
        spread = look_flat[:, 0:P * H]
        same = look_flat[:, P * H:P * H + COLS + 2]
        ad_flat = gathered_ad[:, :, :, :].rearrange("p a b c -> p (a b c)")
        rows_flat = rows[:, :, :].rearrange("p a b -> p (a b)")
        oh_flat = onehot[:, :, :, :].rearrange("p a b c -> p (a b c)")
        W4 = rows_flat[:, 0:KD * D].rearrange("p (k h o) -> p k h o", k=KD, h=H)
        Wprod = rows_flat[:, KD * D:2 * KD * D].rearrange("p (k h o) -> p k h o", k=KD, h=H)
        attb = oh_flat[:, 0:H * 2 * O].rearrange("p (h a o) -> p h a o", h=H, a=2)
        hbuf = ad_flat[:, 0:2 * D].rearrange("p (a d) -> p a d", a=2)
        hTbuf = ad_flat[:, 2 * D:4 * D].rearrange("p (a d) -> p a d", a=2)
        fbuf = ad_flat[:, 4 * D:6 * D].rearrange("p (a d) -> p a d", a=2)
        junk = ad_flat[:, 6 * D:8 * D].rearrange("p (a d) -> p a d", a=2)
        mask = rows_flat[:, 0:COLS]
        runmax = rows_flat[:, COLS:2 * COLS]
        runmaxE = rows_flat[:, 2 * COLS:2 * COLS + SB * GROUP * (H + 1)].rearrange("p (b r h) -> p b r h", b=SB, r=GROUP)
        rows2_flat = rows2[:, :, :].rearrange("p a b -> p (a b)")
        keys_flat = keys[:, :, :].rearrange("p a c -> p (a c)")

        def row_bufs(*places):
            pairs = [place[:, 2 * D * n:2 * D * (n + 1)] for place, count in places for n in range(count)]
            assert len(pairs) == 2 * LOTS
            return pairs
        rows_p2 = row_bufs((rows_flat, 4), (keys_flat, 2), (rows2_flat, 2))
        nodes_all = wk1.bitcast(BF16).rearrange("p (q c) -> p q c", q=2)
        onehotT = wk2.bitcast(BF16).rearrange("p (q c) -> p q c", q=2)

        psA = pb("psA", [P, COLS], F32)
        psB = pb("psB", [P, COLS], F32)
        psC = pb("psC", [P, COLS], F32)
        psD = pb("psD", [P, 512], F32)
        psE = pb("psE", [P, 512], F32)

        consts = sem("consts")
        keys_loaded = sem("keys_loaded")
        keys_loaded2 = sem("keys_loaded2")
        w0_loaded = sem("w0_loaded")
        x_loaded = sem("x_loaded")
        sort_step = sem("sort_step")
        turned = sem("turned")
        dve_link = sem("dve_link")
        act_link = sem("act_link")
        pool_link = sem("pool_link")
        counted = sem("counted")
        pads_known = sem("pads_known")
        Wa_ready = sem("Wa_ready")
        var_ready = sem("var_ready")
        rstd_ready = sem("rstd_ready")
        h_ready = sem("h_ready")
        hT_ps = sem("hT_ps")
        hT_ready = sem("hT_ready")
        feat_ps = sem("feat_ps")
        feat_ready = sem("feat_ready")
        feat_stored = [sem("feat_stored0"), sem("feat_stored1")]
        ad_stored = sem("ad_stored")
        fields = sem("fields")
        fieldsT = sem("fieldsT")
        slotsA = sem("slotsA")
        slots_stored = sem("slots_stored")
        keysB_free = sem("keysB_free")
        sortB_done = sem("sortB_done")
        hold = sem("hold")
        idx1 = sem("idx1")
        ad_arrived = [sem("ad_arrived0"), sem("ad_arrived1")]
        ad_kept = sem("ad_kept")
        ad_padded = sem("ad_padded")
        adT = sem("adT")
        scanned = sem("scanned")
        scanT = sem("scanT")
        last_ready = sem("last_ready")
        runs_ready = sem("runs_ready")
        slotmax = sem("slotmax")
        taken = sem("taken")
        look_ready = sem("look_ready")
        done = sem("done")

        DENSE_PAIRS = TILES // 2
        CROSSINGS = 2 * (ALL_BITS - ROW_BITS)
        EARLY = 4
        share = [EARLY + (DENSE_PAIRS - EARLY) * c // (CROSSINGS - 1) for c in range(CROSSINGS)]

        def sort_plan(start):
            n, at, plan = start + 1, 1, []
            n += 2 * sum(range(1, ROW_BITS + 1))
            at ^= sum(range(1, ROW_BITS + 1)) & 1
            for m in range(ROW_BITS + 1, ALL_BITS + 1):
                n, at = n + 1, at ^ 1
                for js in (m - ROW_BITS, ROW_BITS):
                    plan.append((n, at))
                    n, at = n + 1 + 2 * js, at ^ (js & 1)
            return plan, n, at

        planA, stepsA, atA = sort_plan(0)
        planB, stepsB, atB = sort_plan(stepsA)

        block = ctx.enter_context(nc.Block())

        row_loaded = [sem("row_loaded0"), sem("row_loaded1")]
        onehotT_ready = sem("onehotT_ready")
        look_ps = sem("look_ps")
        zstep = sem("zstep")
        w_ready = sem("w_ready")
        idx2 = sem("idx2")
        rows_arrived = [[sem(f"rows_arrived{q}{u}") for u in range(2)] for q in range(2)]
        onehot_ready = sem("onehot_ready")
        weighted = sem("weighted")
        lot_ps = sem("lot_ps")
        turned_ps = sem("turned_ps")
        split = sem("split")
        wparts = alphas[:, :, :].rearrange("p t c -> p (t c)")[:, 0:SB * 3 * H].bitcast(BF16).rearrange(
            "p (q b n h) -> p q b n h", q=2, b=SB, n=3)
        onehot_b = onehot[:, :, :, :].rearrange("p q b n -> p (q b n)").bitcast(BF16)[:, 1::2].rearrange(
            "p (q b n) -> p q b n", q=2, b=SB)
        onehot_ps = psE[:, :].bitcast(BF16)
        lot_added = sem("lot_added")
        LOT_CREDIT, ADD_CREDIT = 2 * LOTS, 2
        x_in = [sem(f"x_in{q}") for q in range(4)]
        x_last = sem("x_last")
        zeroed = sem("zeroed")
        normed = sem("normed")
        moments = sem("moments")
        x1_ready = sem("x1_ready")
        x1_stored = sem("x1_stored")
        var1_ready = sem("var1_ready")
        rstd1_ready = sem("rstd1_ready")
        h1_ready = sem("h1_ready")
        h1_stored = [sem(f"h1_stored{q}") for q in range(4)]
        den_ready = sem("den_ready")
        x_scaled = sem("x_scaled")
        hA_ready = sem("hA_ready")
        squared = sem("squared")
        sums_cleared = sem("sums_cleared")
        h_summed = sem("h_summed")
        sq_summed = sem("sq_summed")
        colsum_ps = sem("colsum_ps")
        xin = rows[:, 0:4, :]
        xlast = rows[:, 4, :]
        hout = ad_flat[:, 0:4 * D].rearrange("p (q d) -> p q d", q=4)
        hsq = rows[:, 4:8, :]
        hsum, hsqsum = rows[:, 0, :], rows[:, 1, :]
        QUADS = TILES // 4
        assert TILES == 4 * QUADS + 1
        bnst = keyX[:, 0:6 * TILES].rearrange("p (t c) -> p t c", c=6)
        mean1, var1, dif1 = (keyX[:, 512 + 64 * n:512 + 64 * n + TILES] for n in range(3))

        def look_of(q):
            return psD[:, 2 * P * q:2 * P * q + SB * 2 * H]

        def layer0_sync(sp):
            sp.wait_ge(look_ready, 1)
            def load_nodes(r, q):
                sp.dma_start(nodes_all[:, q, :], slot_nodes[r, :].broadcast_to([P, COLS])).then_inc(row_loaded[q], 16)
            for q in range(2):
                load_nodes(slice(q, q + 1), q)
            with sp.Fori(0, ROWS // 2) as i:
                for q in range(2):
                    sp.wait_ge(onehotT_ready, i * 2 + (q + 1))
                    load_nodes(bass.ds(i * 2 + (q + 2), 1), q)
            for q in range(2):
                sp.wait_ge(row_loaded[q], 16 * (1 + ROWS // 2))
            sp.wait_ge(lot_ps, LOT_CREDIT + (ROWS - 1) * LOTS)
            for q in range(4):
                sp.dma_start(xin[:, q, :], x[q * P:(q + 1) * P, :]).then_inc(x_in[q], 16)
            sp.wait_ge(lot_added, ADD_CREDIT + ROWS * LOTS)
            sp.wait_ge(zeroed, 1)
            sp.dma_start(xlast[0:LAST, :], x[(TILES - 1) * P:N, :]).then_inc(x_last, 16)

            def store_x1(i, q):
                sp.wait_ge(x1_ready, i * 4 + (q + 1))
                sp.dma_start(x1_table[bass.ds(i * (4 * P) + q * P, P), :],
                             acc[:, bass.ds(i * 4 + q, 1), 0:D].rearrange("p a d -> p (a d)")).then_inc(x1_stored, 16)
            with sp.Fori(0, QUADS - 1) as i:
                for q in range(4):
                    store_x1(i, q)
                    sp.dma_start(xin[:, q, :], x[bass.ds(i * (4 * P) + (4 + q) * P, P), :]).then_inc(x_in[q], 16)
            for q in range(4):
                store_x1(QUADS - 1, q)
            sp.wait_ge(x1_ready, TILES)
            sp.dma_start(x1_table[(TILES - 1) * P:TILES * P, :], acc[:, TILES - 1, 0:D]).then_inc(x1_stored, 16)
            load_attention(sp)
            with sp.Fori(0, QUADS) as i:
                for q in range(4):
                    sp.wait_ge(h1_ready, i * 4 + (q + 1))
                    sp.dma_start(h1_table[bass.ds(i * (4 * P) + q * P, P), :], hout[:, q, :]).then_inc(h1_stored[q], 16)
            sp.wait_ge(h1_ready, TILES)
            sp.dma_start(h1_table[(TILES - 1) * P:TILES * P, :], hout[:, 0, :]).then_inc(h1_stored[0], 16)
            layer1_sync(sp)

        def gather_rows(pool, table, bufs, idx_sem, lot_sem, arrived):
            with pool.Fori(0, ROWS // 2) as i:
                for q in range(2):
                    pool.wait_ge(idx_sem, i * 2 + (q + 1))
                    for hf in range(2):
                        pool.wait_ge(lot_sem, i * 8 + (4 * q + 2 * hf + 2 + LOT_CREDIT - 2 * LOTS))
                        pool.sem_inc(hold, 1)
                        for b in range(4 * hf, 4 * hf + 4):
                            g.indirect_dma_start(bufs[4 * q + b // 2][:, b % 2 * D:(b % 2 + 1) * D], None, table,
                                                 bass.IndirectOffsetOnAxis(ap=idx[:, q, b:b + 1], axis=0),
                                                 bounds_check=N - 1, oob_is_err=False).then_inc(arrived[q][hf], 16)

        def layer0_gpsimd(pool):
            pool.wait_ge(look_ready, 1)
            pool.sem_inc(hold, 1)
            gather_rows(pool, feat_table, rows_p2, idx2, lot_ps, rows_arrived)
            pool.wait_ge(den_ready, 1)

            def scale_sums(t):
                row = acc[:, bass.ds(t, 1), 0:D].rearrange("p a (h o) -> p (a h) o", h=H)
                g.tensor_tensor(row, row, maxd[:, bass.ds(t, 1), :].rearrange("p a h -> p (a h)").unsqueeze(2)
                                .broadcast_to([P, H, O]), ALU.mult).then_inc(x_scaled, 1)
            with pool.Fori(0, TILES) as t:
                scale_sums(t)
            pool.wait_ge(sums_cleared, 2)

            def sum_h1(q):
                g.tensor_tensor(hsum, hsum, hout[:, q, :], ALU.add).then_inc(h_summed, 1)
            for q in range(4):
                pool.wait_ge(h1_ready, q + 1)
                if q > 0:
                    pool.wait_ge(h_summed, q)
                sum_h1(q)
            with pool.Fori(1, QUADS) as i:
                for q in range(4):
                    pool.wait_ge(h1_ready, i * 4 + (q + 1))
                    pool.wait_ge(h_summed, i * 4 + q)
                    sum_h1(q)
            pool.wait_ge(h1_ready, TILES)
            pool.wait_ge(h_summed, TILES - 1)
            sum_h1(0)
            layer1_gpsimd(pool)

        def layer0_scalar(act, link, links):
            def put_indices(minor_t, r, q, signal):
                s.copy(idx[:, q, :], minor_t[:, :, bass.ds(r, 1)].rearrange("p b a -> p (b a)")).then_inc(signal, 1)

            def next_indices(minor_t, i, q, arrived, signal):
                for u in range(2):
                    act.wait_ge(arrived[q][u], i * 64 + 64)
                act.sem_inc(hold, 1)
                put_indices(minor_t, i * 2 + (q + 2), q, signal)

            def nodes_onehot(q, signal):
                s.copy(onehot[:, q, :, :].rearrange("p b n -> p (b n)"), onehot_ps).then_inc(signal, 1)

            def weights(q):
                s.activation(wts[:, q, :, :], zbuf[:, 3 * q + 2, :, :], ACT.Exp).then_inc(w_ready, 1)

            act.wait_ge(look_ready, 1)
            act.wait_ge(idx1, 2 + 2 * ROWS)
            put_indices(minorA, 0, 0, idx2)
            put_indices(minorA, 1, 1, idx2)
            act.wait_ge(zstep, 4)
            weights(0)
            act.wait_ge(turned_ps, 1)
            nodes_onehot(0, onehot_ready)
            with act.Fori(0, ROWS // 2) as i:
                for q in range(2):
                    next_indices(minorA, i, q, rows_arrived, idx2)
                    act.wait_ge(zstep, i * 8 + (4 * q + 8))
                    weights(1 - q)
                    act.wait_ge(turned_ps, i * 2 + (q + 2))
                    nodes_onehot(1 - q, onehot_ready)
            act.wait_ge(moments, 1)
            s.activation(stat[:, 2, :], var1, ACT.Sqrt, bias=small[:, 0:1]).then_inc(var1_ready, 1)
            act.wait_ge(rstd1_ready, 1)

            def make_h1(target, t):
                return s.activation(target, acc[:, bass.ds(t, 1), 0:D].rearrange("p a d -> p (a d)"), ACT.Relu,
                                    scale=stat[:, 3, bass.ds(t, 1)], bias=stat[:, 1, bass.ds(t, 1)])
            for q in range(4):
                make_h1(hout[:, q, :], q).then_inc(h1_ready, 1)
            for n in range(NT):
                make_h1(hA[:, n, :], n).then_inc(hA_ready, 1)
            with act.Fori(1, QUADS) as i:
                for q in range(4):
                    act.wait_ge(h_summed, i * 4 + (q - 3))
                    act.wait_ge(squared, i * 4 + (q - 3))
                    act.wait_ge(h1_stored[q], i * 16)
                    act.sem_inc(hold, 1)
                    make_h1(hout[:, q, :], i * 4 + q).then_inc(h1_ready, 1)
            act.wait_ge(h_summed, TILES - 4)
            act.wait_ge(squared, TILES - 4)
            act.wait_ge(h1_stored[0], 16 * QUADS)
            act.sem_inc(hold, 1)
            make_h1(hout[:, 0, :], TILES - 1).then_inc(h1_ready, 1)
            layer1_scalar(act, link, links, put_indices, next_indices)

        def layer0_vector(dve, link, links):
            def make_onehotT(q):
                v.tensor_scalar(onehotT[:, q, :], nodes_all[:, q, :], iota_col[:, 0:1], None,
                                ALU.is_equal).then_inc(onehotT_ready, 1)

            def make_onehot(node_t, r, q, signal):
                v.tensor_tensor(onehot[:, q, :, :], iota_row[:, :].unsqueeze(1).broadcast_to([P, SB, P]),
                                node_t[:, :, bass.ds(r, 1)].broadcast_to([P, SB, P]), ALU.is_equal).then_inc(signal, 1)

            def zops(k, r, q, zbase):
                ps = look_of(q).rearrange("p (b c) -> p b c", c=2 * H)
                z = [zbuf[:, 3 * q + n, :, :] for n in range(3)]
                if k > 0:
                    dve.wait_ge(zstep, zbase + k)
                if k == 0:
                    v.tensor_tensor(z[0], ps[:, :, 0:H],
                                    gathered_ad[:, :, bass.ds(r, 1), :].rearrange("p b a h -> p b (a h)"),
                                    ALU.add).then_inc(zstep, 1)
                elif k == 1:
                    v.scalar_tensor_tensor(z[1], z[0], SLOPE, z[0], ALU.mult, ALU.max).then_inc(zstep, 1)
                elif k == 2:
                    v.tensor_tensor(z[0], z[1], ps[:, :, H:2 * H], ALU.subtract).then_inc(zstep, 1)
                else:
                    v.tensor_scalar(z[2], z[0], 0.0, None, ALU.min).then_inc(zstep, 1)

            def split_weights(k, q, base):
                n = k // 2
                if k > 0:
                    dve.wait_ge(split, base + k)
                if k % 2 == 0:
                    ins = v.tensor_copy(wparts[:, q, :, n, :], wts[:, q, :, :] if n == 0 else wrest[:, :, :])
                else:
                    ins = v.tensor_tensor(wrest[:, :, :], wts[:, q, :, :] if n == 0 else wrest[:, :, :],
                                          wparts[:, q, :, n, :], ALU.subtract)
                ins.then_inc(split, 1)

            def weigh(a, q):
                pair = rows_p2[4 * q + a].rearrange("p (x o) -> p x o", o=O)
                v.tensor_tensor(pair, pair, wts[:, q, 2 * a:2 * a + 2, :].rearrange("p b h -> p (b h)").unsqueeze(2)
                                .broadcast_to([P, 2 * H, O]), ALU.mult).then_inc(weighted, 1)

            def add_lot(a, tile, psum, width):
                d = acc[:, bass.ds(tile, 1), 0:width].rearrange("p a d -> p (a d)")
                v.tensor_tensor(d, d, psum[:, 0:width], ALU.add).then_inc(lot_added, 1)

            dve.sem_inc(lot_added, ADD_CREDIT)
            for q in range(2):
                dve.wait_ge(row_loaded[q], 16)
                make_onehotT(q)
            dve.wait_ge(look_ps, 1)
            for k in range(4):
                zops(k, 0, 0, 0)
            dve.wait_ge(w_ready, 1)
            for k in range(5):
                split_weights(k, 0, 0)
            dve.wait_ge(rows_arrived[0][0], 64)
            weigh(0, 0)
            weigh(1, 0)

            def row(i, q, last=False):
                r1, q1, zb, sp_base = i * 2 + (q + 1), 1 - q, i * 8 + (4 * q + 4), i * 10 + (5 * q + 5)

                def add(a, t):
                    dve.wait_ge(lot_added, i * 8 + (4 * q + a + ADD_CREDIT))
                    dve.wait_ge(lot_ps, i * 8 + (4 * q + a + 1 + LOT_CREDIT))
                    add_lot(a, t, (psA, psB)[a % 2], ACC_W)

                def tile_of(a):
                    return dve.value_load(tileA[0:1, a, bass.ds(i * 2 + q, 1)], min_val=0, max_val=TILES - 1)
                for a in range(2):
                    if a == 0:
                        dve.wait_ge(rows_arrived[q][1], i * 64 + 64)
                    weigh(2 + a, q)
                    add(a, tile_of(a))
                third = tile_of(2)
                dve.wait_ge(look_ps, i * 2 + (q + 2))
                zops(0, r1, q1, zb)
                zops(1, r1, q1, zb)
                zops(2, r1, q1, zb)
                zops(3, r1, q1, zb)
                dve.wait_ge(row_loaded[q], i * 16 + 32)
                make_onehotT(q)
                for a in range(2, LOTS):
                    t = third if a == 2 else tile_of(a)
                    if not last:
                        if a == 2:
                            dve.wait_ge(w_ready, i * 2 + (q + 2))
                            dve.wait_ge(rows_arrived[q1][0], i * 64 + 64 * (q + 1))
                            split_weights(0, q1, sp_base)
                        weigh(a - 2, q1)
                        split_weights(2 * a - 3, q1, sp_base)
                    add(a, t)
                    if not last:
                        split_weights(2 * a - 2, q1, sp_base)
            with dve.Fori(0, ROWS // 2 - 1) as i:
                for q in range(2):
                    row(i, q)
            row(ROWS // 2 - 1, 0)
            row(ROWS // 2 - 1, 1, True)
            dve.wait_ge(lot_added, ADD_CREDIT + ROWS * LOTS)
            v.memset(xlast, 0.0).then_inc(zeroed, 1)
            link(v.tensor_scalar(maxd[:, :, :], acc[:, :, D:ACC_W], 1e-30, None, ALU.max))
            v.reciprocal(maxd[:, :, :], maxd[:, :, :]).then_inc(den_ready, 1)

            def make_x1(t, xt):
                row = acc[:, bass.ds(t, 1), 0:D].rearrange("p a d -> p (a d)")
                dve.wait_ge(x_scaled, t + 1)
                v.scalar_tensor_tensor(row, row, 0.0, xt, ALU.max, ALU.add).then_inc(x1_ready, 1)

            def row_moments(t):
                dve.wait_ge(x1_ready, t + 1)
                dve.sem_inc(hold, 1)
                v.bn_stats(bnst[:, bass.ds(t, 1), :].rearrange("p a c -> p (a c)"),
                           acc[:, bass.ds(t, 1), 0:D].rearrange("p a d -> p (a d)")).then_inc(normed, 1)
            for q in range(4):
                dve.wait_ge(x_in[q], 16)
                make_x1(q, xin[:, q, :])
                if q > 0:
                    row_moments(q - 1)
            with dve.Fori(1, QUADS) as i:
                for q in range(4):
                    dve.wait_ge(x_in[q], i * 16 + 16)
                    make_x1(i * 4 + q, xin[:, q, :])
                    row_moments(i * 4 + (q - 1))
            dve.wait_ge(x_last, 16)
            make_x1(TILES - 1, xlast)
            row_moments(TILES - 2)
            row_moments(TILES - 1)
            dve.wait_ge(normed, TILES)
            link(v.tensor_tensor(mean1, bnst[:, :, 1], bnst[:, :, 4], ALU.add))
            link(v.tensor_tensor(dif1, bnst[:, :, 1], bnst[:, :, 4], ALU.subtract))
            link(v.tensor_tensor(dif1, dif1, dif1, ALU.mult))
            link(v.tensor_tensor(var1, bnst[:, :, 2], bnst[:, :, 5], ALU.add))
            link(v.tensor_scalar(var1, var1, 1.0 / D, None, ALU.mult))
            v.scalar_tensor_tensor(var1, dif1, 0.25, var1, ALU.mult, ALU.add).then_inc(moments, 1)
            dve.wait_ge(var1_ready, 1)
            link(v.reciprocal(stat[:, 3, :], stat[:, 2, :]))
            v.scalar_tensor_tensor(stat[:, 1, :], mean1, -0.5, stat[:, 3, :], ALU.mult, ALU.mult).then_inc(rstd1_ready, 1)
            for total in (hsum, hsqsum):
                v.memset(total, 0.0).then_inc(sums_cleared, 1)

            def square_h1(q):
                v.tensor_tensor(hsq[:, q, :], hout[:, q, :], hout[:, q, :], ALU.mult).then_inc(squared, 1)

            def sum_square(q):
                v.tensor_tensor(hsqsum, hsqsum, hsq[:, q, :], ALU.add).then_inc(sq_summed, 1)
            dve.wait_ge(sums_cleared, 2)
            for q in range(4):
                dve.wait_ge(h1_ready, q + 1)
                square_h1(q)
                if q > 0:
                    dve.wait_ge(squared, q)
                    if q > 1:
                        dve.wait_ge(sq_summed, q - 1)
                    sum_square(q - 1)
            with dve.Fori(1, QUADS) as i:
                for q in range(4):
                    dve.wait_ge(h1_ready, i * 4 + (q + 1))
                    square_h1(q)
                    dve.wait_ge(squared, i * 4 + q)
                    dve.wait_ge(sq_summed, i * 4 + (q - 1))
                    sum_square((q - 1) % 4)
            dve.wait_ge(h1_ready, TILES)
            square_h1(0)
            for t in (TILES - 2, TILES - 1):
                dve.wait_ge(squared, t + 1)
                dve.wait_ge(sq_summed, t)
                sum_square(t % 4)
            layer1_vector(dve, link, links, make_onehot, add_lot)

        def layer0_tensor(pe):
            def tile_of(a, r):
                return pe.value_load(tileA[0:1, a, bass.ds(r, 1)], min_val=0, max_val=TILES - 1)

            def look_up(a, t, q):
                for b in (2 * a, 2 * a + 1):
                    for n in range(3):
                        ins = pet.matmul(look_of(q)[:, b * 2 * H:(b + 1) * 2 * H], onehotT[:, q, b * P:(b + 1) * P],
                                         look[:, bass.ds(t, 1), n, :].rearrange("p a c -> p (a c)"),
                                         start=(n == 0), stop=(n == 2))
                return ins

            def finish_look_up(tiles, q):
                for a in range(2, LOTS):
                    ins = look_up(a, tiles[a], q)
                ins.then_inc(look_ps, 1)
                for b in range(SB):
                    ins = pet.transpose(onehot_ps[:, b * P:(b + 1) * P], onehotT[:, q, b * P:(b + 1) * P], ident_b)
                ins.then_inc(turned_ps, 1)

            def lot(a, q, r, tiles, later):
                psum = (psA, psB)[a % 2]
                for b in (2 * a, 2 * a + 1):
                    pet.matmul(psum[:, 0:D], onehot[:, q, b, :], rows_p2[4 * q + a][:, b % 2 * D:(b % 2 + 1) * D],
                               start=(b % 2 == 0), stop=(b % 2 == 1))
                    if q == 0:
                        (tiles if a < 2 else later).append(tile_of(b % LOTS, r + 1 + b // LOTS))
                    if a == 1:
                        look_up(b - 2, tiles[b - 2], 1 - q)
                if a == 0:
                    pe.wait_ge(split, r * 5 + 5)
                for b in (2 * a, 2 * a + 1):
                    for n in range(3):
                        ins = pet.matmul(psum[:, D:ACC_W], onehot_b[:, q, b, :], wparts[:, q, b, n, :],
                                         start=(b % 2 == 0 and n == 0), stop=(b % 2 == 1 and n == 2))
                ins.then_inc(lot_ps, 1)

            pe.sem_inc(lot_ps, LOT_CREDIT)
            pe.wait_ge(onehotT_ready, 1)
            tiles = [tile_of(a, 0) for a in range(LOTS)]
            for a in range(2):
                look_up(a, tiles[a], 0)
            finish_look_up(tiles, 0)
            with pe.Fori(0, ROWS // 2) as i:
                for q in range(2):
                    pe.wait_ge(onehot_ready, i * 2 + (q + 1))
                    tiles, later = ([], []) if q == 0 else (later, None)
                    for a in range(LOTS):
                        pe.wait_ge(weighted, i * 8 + (4 * q + a + 1))
                        pe.wait_ge(lot_added, i * 8 + (4 * q + a + ADD_CREDIT - 1))
                        lot(a, q, i * 2 + q, tiles, later)
                        if a == 1:
                            finish_look_up(tiles, 1 - q)
            pe.wait_ge(h_summed, TILES)
            pe.wait_ge(sq_summed, TILES)
            for k in range(2 * KD):
                ins = pet.matmul(psD[:, k:k + 1], (hsum, hsqsum)[k // KD][:, (k % KD) * P:(k % KD + 1) * P], ones[:, :],
                                 start=True, stop=True)
            ins.then_inc(colsum_ps, 1)
            layer1_tensor(pe)

        def blocks(flat_view):
            return flat_view.rearrange("p (k d) -> p k d", k=KD)
        Wc_s = blocks(ad_flat[:, 0:KD * D])
        Wq_s = blocks(ad_flat[:, 4 * D:8 * D])
        Wk_s = blocks(ad_flat[:, 8 * D:12 * D])
        Wv_s = blocks(wk[:, :, :].rearrange("p a c -> p (a c)"))
        Wo_s = blocks(keys[:, :, :].rearrange("p a c -> p (a c)"))
        proj_s = rows2_flat[:, 0:2 * MT * DH].rearrange("p (t u d) -> p t u d", t=MT, u=2)
        projT = rows2_flat[:, 256:256 + M]
        ones_mat = lastA[:, :, :].rearrange("p b r -> p (b r)").bitcast(F32)[:, 0:P]
        SCRATCH = 28 * ACC_W
        at = [SCRATCH]

        def scratch(width):
            at[0] += width
            assert at[0] <= TILES * ACC_W
            return acc_flat[:, at[0] - width:at[0]]
        hT = scratch(KD * MAXN).rearrange("p (k n) -> p k n", k=KD)
        qT = scratch(KD * MAXN).rearrange("p (j n) -> p j n", j=KD)
        kT = scratch(KD * MAXN).rearrange("p (j n) -> p j n", j=KD)
        values = scratch(NT * H * (DH + 1)).rearrange("p (t h d) -> p t h d", t=NT, h=H)
        uk = scratch(H * NT * M).rearrange("p (h t m) -> p h t m", h=H, t=NT)
        squares = scratch(2 * KD * MAXN)
        kvs = scratch(2 * MT * (DH + 1)).rearrange("p (q t d) -> p q t d", q=2, t=MT)
        select_last = scratch(P)
        qf = oh_flat[:, 1024:2048].rearrange("p (q t m) -> p q t m", q=2, t=NT)
        qfT = squares[:, 0:2 * MT * MAXN].rearrange("p (q t n) -> p q t n", q=2, t=MT)
        attn = oh_flat[:, 0:NT * D].rearrange("p (t d) -> p t d", t=NT)
        look_f32 = look_flat.bitcast(F32)
        hA = look_f32[:, 0:NT * D].rearrange("p (t d) -> p t d", t=NT)
        hattn = hA
        dg = small[:, 16:48]
        mxk = small[:, 48:56]
        mxq = small[:, 56:72]
        bias_k = stat[:, 0, 0:16]
        bias_q = stat[:, 0, 16:32]
        km8 = stat[:, 2, 0:1]
        kmd = stat[:, 2, 8:16]
        zden = stat[:, 2, 16:20]

        Wqkv_loaded = sem("Wqkv_loaded")
        proj_loaded = sem("proj_loaded")
        Wo_loaded = sem("Wo_loaded")
        Wc_loaded = sem("Wc_loaded")
        vec_loaded = sem("vec_loaded")
        bc_loaded = sem("bc_loaded")
        hs = range(H)
        SPE = Steps(sem("att_pe"), ["hT", "projT", "qT", "kT", "v0", "v1", "diag"] + [f"uk{h}" for h in hs] +
                    ["kmT", "kmB", "uq0", "uq1", "kv0"] +
                    [n for h in hs for n in [f"qfT{h}"] + ([f"uq{h + 2}"] if h < H - 2 else []) +
                     ([f"kv{h + 1}"] if h < H - 1 else []) + [f"at{h}"]] + ["aT", "wo", "last"])
        SACT = Steps(sem("att_act"), ["hT", "projT", "qT", "kT", "sq"] + [f"uk{h}" for h in hs] + [f"ek{h}" for h in hs] +
                     ["eq0", "eq1"] + [n for h in hs for n in [f"qfT{h}"] + ([f"eq{h + 2}"] if h < H - 2 else [])] +
                     ["aT", "wo"])
        SDVE = Steps(sem("att_dve"), ["sums", "sel", "ones_mat", "ones", "v0", "v1", "diag"] + [f"mk{h}" for h in hs] +
                     ["km", "kmd", "bk", "mq0", "bq0", "kf0", "mq1", "bq1", "kv0"] +
                     [n for h in hs for n in [f"qf{h}"] + ([f"kf{h + 1}"] if h < H - 1 else []) +
                      ([f"mq{h + 2}", f"bq{h + 2}"] if h < H - 2 else []) + ([f"kv{h + 1}"] if h < H - 1 else []) +
                      [f"zd{h}", f"zr{h}", f"at{h}"]] + ["hat0", "hat1"])

        colsum = stat[:, 1, 0:8]
        vecs = alphas[:, :, :].rearrange("p t c -> p (t c)")
        g1c, b1c = vecs[:, 0:KD], vecs[:, 4:4 + KD]
        mean_c, var_c, scale_c, shift_c, sd_c = (vecs[:, 8 + 4 * n:12 + 4 * n] for n in range(5))
        shrow = ad_flat[0:1, 4 * D:5 * D]
        bcrow = ad_flat[0:1, 5 * D:6 * D]
        parts1 = rows2_flat[0:1, 512:512 + 3 * D].bitcast(BF16).rearrange("p (n d) -> p n d", n=6)
        bias_rows = keys_flat[0:6, 2 * D:2 * D + D // 2].bitcast(BF16)
        indT = wk1[0:TILES, 0:P // 2].bitcast(BF16)
        ind_rows = ad_flat[0:6, SB * ROWS_G * H - TILES * P // 2:].bitcast(BF16)
        bn1_sd = sem("bn1_sd")
        bn1_step = sem("bn1_step")
        SHIFT_ROW = 8
        bn1_shift = sem("bn1_shift")
        bn1_ps = sem("bn1_ps")
        parts_ready = sem("parts_ready")
        bias_stored = sem("bias_stored")
        acc_cleared = sem("acc_cleared")

        rows_l1 = row_bufs((rows_flat, 4), (ad_flat[:, 6 * D:], 4))
        idx3 = sem("idx3")
        h_arrived = [[sem(f"h_arrived{q}{u}") for u in range(2)] for q in range(2)]
        onehot1_ready = sem("onehot1_ready")
        lot1_ps = sem("lot1_ps")
        lot1_added = sem("lot1_added")

        rowsf = rows_flat
        h_in = rowsf[:, 0:2 * D].rearrange("p (q d) -> p q d", q=2)
        aggn = rowsf[:, 2 * D:4 * D].rearrange("p (q d) -> p q d", q=2)
        aggT = rowsf[:, 4 * D:6 * D].rearrange("p (q d) -> p q d", q=2)
        ybuf = rowsf[:, 6 * D:8 * D].rearrange("p (q d) -> p q d", q=2)
        ysq = oh_flat[:, 0:2 * D].rearrange("p (q d) -> p q d", q=2)
        ysum, ysum2 = oh_flat[:, 2 * D:3 * D], oh_flat[:, 3 * D:4 * D]
        rdeg = stat[:, 3, :]
        indc = stat[:, 1, :]
        deg_ready = sem("deg_ready")
        ind_ps = sem("ind_ps")
        ind_ready = sem("ind_ready")
        ind_spread = sem("ind_spread")
        hc_in = [sem("hc_in0"), sem("hc_in1")]
        aggn_ready = sem("aggn_ready")
        aggT_ps = sem("aggT_ps")
        aggT_ready = sem("aggT_ready")
        conv_ps = sem("conv_ps")
        y_ready = sem("y_ready")
        y_kept = sem("y_kept")
        y_summed = sem("y_summed")
        g2_loaded = sem("g2_loaded")
        total_ps = sem("total_ps")
        bn2_step = sem("bn2_step")
        bn2_sd = sem("bn2_sd")
        bn2_ready = sem("bn2_ready")
        x1_in = [sem(f"x1_in{n}") for n in range(4)]
        shifted = sem("shifted")
        scaled = sem("scaled")
        out_ready = sem("out_ready")
        out_stored = [sem(f"out_stored{n}") for n in range(4)]
        scale2, shift2, mean2, sd2 = (ad_flat[:, (6 + n) * D:(7 + n) * D] for n in range(4))
        g2row, b2row = keys_flat[:, 0:D], keys_flat[:, D:2 * D]
        x1buf = rows2[:, :, :]
        obuf = rowsf[:, 4 * D:8 * D].rearrange("p (q d) -> p q d", q=4)
        tbuf = oh_flat[:, 0:4 * D].rearrange("p (q d) -> p q d", q=4)

        def w_by_block(w):
            return w.rearrange("(k p) d -> p k d", p=P)

        def row_of(vector):
            return vector.rearrange("(u c) -> u c", u=1)

        def wait_h1_stored(engine):
            for q in range(4):
                engine.wait_ge(h1_stored[q], 16 * (QUADS + (q == 0)))

        def load_attention(sp):
            for w, place in ((Wq, Wq_s), (Wk, Wk_s), (Wv, Wv_s)):
                sp.dma_start(place, w_by_block(w)).then_inc(Wqkv_loaded, 16)
            for u in range(2):
                sp.dma_start(proj_s[:, :, u, :], proj.rearrange("(t p) d -> p t d", p=P)).then_inc(proj_loaded, 16)
            for vector, place in ((norm1_g, g1c), (norm1_b, b1c)):
                sp.dma_start(place, vector.rearrange("(k p) -> p k", p=P), allow_slow_non_contiguous=True).then_inc(vec_loaded, 16)

        def layer1_sync(sp):
            sp.wait_ge(rstd1_ready, 1)
            sp.dma_start(Wo_s, w_by_block(Wo)).then_inc(Wo_loaded, 16)
            wait_h1_stored(sp)
            sp.wait_ge(colsum_ps, 1)
            sp.dma_start(Wc_s, w_by_block(W_conv)).then_inc(Wc_loaded, 16)
            SPE.wait(sp, "kT")
            sp.dma_start(bcrow, row_of(b_conv)).then_inc(bc_loaded, 16)
            sp.wait_ge(parts_ready, 1)
            sp.dma_start(bias_table.rearrange("n d -> (n d)").rearrange("(u c) -> u c", u=1),
                         parts1.rearrange("p n d -> p (n d)")).then_inc(bias_stored, 16)
            sp.wait_ge(bias_stored, 16)
            SPE.wait(sp, "wo")
            sp.dma_start(bias_rows, bias_table).then_inc(bias_stored, 16)
            for vector, place in ((norm2_g, g2row), (norm2_b, b2row)):
                sp.dma_start(place, row_of(vector).broadcast_to([P, D])).then_inc(g2_loaded, 16)
            for q in range(4):
                sp.dma_start(x1buf[:, q, :], x1_table[q * P:(q + 1) * P, :]).then_inc(x1_in[q], 16)
            sp.wait_ge(lot1_added, ADD_CREDIT + ROWS * LOTS)
            for q in range(2):
                sp.dma_start(h_in[:, q, :], h1_table[q * P:(q + 1) * P, :]).then_inc(hc_in[q], 16)
            sp.wait_ge(ind_ready, 2)
            sp.dma_start(ind_table, indT).then_inc(ind_spread, 16)
            sp.wait_ge(ind_spread, 16)
            sp.dma_start(ind_rows[0:3, :], row_of(ind_table.rearrange("t n -> (t n)")).broadcast_to([3, TILES * P])
                         ).then_inc(ind_spread, 16)
            with sp.Fori(0, DENSE_PAIRS - 1) as i:
                for q in range(2):
                    sp.wait_ge(y_ready, i * 2 + (q + 1))
                    sp.dma_start(h_in[:, q, :], h1_table[bass.ds(i * (2 * P) + (2 + q) * P, P), :]).then_inc(hc_in[q], 16)
            sp.wait_ge(y_ready, TILES - 2)
            sp.dma_start(h_in[:, 0, :], h1_table[(TILES - 1) * P:TILES * P, :]).then_inc(hc_in[0], 16)
            sp.wait_ge(y_ready, TILES)
            sp.wait_ge(y_kept, 2 * TILES)
            sp.wait_ge(y_summed, 2 * TILES)

            with sp.Fori(0, QUADS - 1) as i:
                for q in range(4):
                    sp.wait_ge(out_ready, i * 4 + (q + 1))
                    sp.dma_start(out[bass.ds(i * (4 * P) + q * P, P), :], obuf[:, q, :]).then_inc(out_stored[q], 16)
                    sp.dma_start(x1buf[:, q, :], x1_table[bass.ds(i * (4 * P) + (4 + q) * P, P), :]).then_inc(x1_in[q], 16)
            for q in range(4):
                t = 4 * (QUADS - 1) + q
                sp.wait_ge(out_ready, t + 1)
                sp.dma_start(out[t * P:(t + 1) * P, :], obuf[:, q, :]).then_inc(out_stored[q], 16)
                if q == 0:
                    sp.dma_start(x1buf[:, 0, :], x1_table[(TILES - 1) * P:TILES * P, :]).then_inc(x1_in[0], 16)
            sp.wait_ge(out_ready, TILES)
            sp.dma_start(out[(TILES - 1) * P:N, :], obuf[0:LAST, 0, :]).then_inc(out_stored[0], 16)
            for q in range(4):
                sp.wait_ge(out_stored[q], 16 * (QUADS + (q == 0)))

        def layer1_gpsimd(pool):
            pool.wait_ge(h1_ready, TILES)
            pool.wait_ge(x1_stored, 16 * TILES)
            g.memset(acc_flat[:, 0:SCRATCH], 0.0).then_inc(acc_cleared, 1)
            wait_h1_stored(pool)
            pool.wait_ge(colsum_ps, 1)
            SPE.wait(pool, "kT")
            pool.sem_inc(hold, 1)
            gather_rows(pool, h1_table, rows_l1, idx3, lot1_ps, h_arrived)
            pool.wait_ge(lot1_added, ADD_CREDIT + ROWS * LOTS)
            g.memset(ysum, 0.0).then_inc(pool_link, 1)
            g.memset(ysum2, 0.0).then_inc(pool_link, 1)
            pool.wait_ge(pool_link, 2)

            def add_y(q, n=P):
                g.tensor_tensor(ysum[0:n, :], ysum[0:n, :], ybuf[0:n, q, :], ALU.add).then_inc(y_summed, 1)
                g.tensor_tensor(ysum2[0:n, :], ysum2[0:n, :], ysq[0:n, q, :], ALU.add).then_inc(y_summed, 1)
            with pool.Fori(0, DENSE_PAIRS) as i:
                for q in range(2):
                    pool.wait_ge(y_kept, i * 4 + (2 * q + 2))
                    pool.sem_inc(hold, 1)
                    add_y(q)
                    pool.wait_ge(y_summed, i * 4 + (2 * q + 2))
                    pool.sem_inc(hold, 1)
            pool.wait_ge(y_kept, 2 * TILES)
            add_y(0, LAST)
            pool.wait_ge(bn2_ready, 1)

            def shift_x1(q, loads):
                pool.wait_ge(x1_in[q], loads)
                pool.sem_inc(hold, 1)
                g.tensor_tensor(x1buf[:, q, :], x1buf[:, q, :], shift2, ALU.add).then_inc(shifted, 1)
            with pool.Fori(0, QUADS) as i:
                for q in range(4):
                    shift_x1(q, i * 16 + 16)
            shift_x1(0, 16 * (QUADS + 1))

        def layer1_scalar(act, link, links, put_indices, next_indices):
            act.wait_ge(idx2, 2 + ROWS)
            put_indices(minorB, 0, 0, idx3)
            put_indices(minorB, 1, 1, idx3)
            done = SACT.done
            SPE.wait(act, "hT")
            act.wait_ge(x1_stored, 16 * TILES)
            done(s.copy(hT.rearrange("p k n -> p (k n)"), psA[:, :]), "hT")
            SPE.wait(act, "projT")
            done(s.copy(projT, psE[:, 0:M]), "projT")
            act.wait_ge(bn1_step, 4)
            s.activation(sd_c, var_c, ACT.Sqrt, bias=small[:, 0:1]).then_inc(bn1_sd, 1)
            SPE.wait(act, "qT")
            done(s.mul(qT.rearrange("p k n -> p (k n)"), psB[:, :], SCALE), "qT")
            SPE.wait(act, "kT")
            done(s.mul(kT.rearrange("p k n -> p (k n)"), psC[:, :], SCALE), "kT")
            SACT.wait(act, "kT")
            s.activation(squares[:, 0:KD * MAXN], qT.rearrange("p k n -> p (k n)"), ACT.Square)
            done(s.activation(squares[:, KD * MAXN:], kT.rearrange("p k n -> p (k n)"), ACT.Square), "sq")
            for h in hs:
                SPE.wait(act, f"uk{h}")
                done(s.copy(uk[:, h, :, :].rearrange("p t m -> p (t m)"), (psA, psB)[h // 2 % 2][:, h % 2 * 512:h % 2 * 512 + 512]), f"uk{h}")
            SDVE.wait(act, "bk")
            SACT.wait(act, f"uk{H - 1}")
            for h in hs:
                for t in range(NT):
                    ins = s.activation(uk[:, h, t, :], uk[:, h, t, :], ACT.Exp, bias=bias_k[:, 2 * h + t:2 * h + t + 1])
                done(ins, f"ek{h}")

            def exp_q(h):
                SDVE.wait(act, f"bq{h}")
                if h >= 2:
                    SPE.wait(act, f"qfT{h - 2}")
                for t in range(NT):
                    ins = s.activation(qf[:, h % 2, t, :], (psA, psB)[h // 2 % 2][:, h % 2 * 512 + t * M:h % 2 * 512 + (t + 1) * M],
                                       ACT.Exp, bias=bias_q[:, 2 * h + t:2 * h + t + 1])
                done(ins, f"eq{h}")
            exp_q(0)
            exp_q(1)
            for h in hs:
                SPE.wait(act, f"qfT{h}")
                if h >= 2:
                    SPE.wait(act, f"at{h - 2}")
                done(s.copy(qfT[:, h % 2, :, :].rearrange("p t n -> p (t n)"), psC[:, h % 2 * 512:h % 2 * 512 + 512]), f"qfT{h}")
                if h < H - 2:
                    exp_q(h + 2)
            SPE.wait(act, "aT")
            done(s.copy(hT.rearrange("p k n -> p (k n)"), psA[:, :]), "aT")
            SPE.wait(act, "wo")
            done(s.copy(hattn.rearrange("p t d -> p (t d)"), psB[:, :]), "wo")
            with act.Fori(0, ROWS // 2) as i:
                for q in range(2):
                    next_indices(minorB, i, q, h_arrived, idx3)

            def turn_out(t, q, first=False):
                act.wait_ge(aggT_ps, t + 1)
                if not first:
                    act.wait_ge(conv_ps, t - 1)
                s.copy(aggT[:, q, :], psC[:, q * 512:(q + 1) * 512]).then_inc(aggT_ready, 1)

            def keep_y(t, q, first=False):
                act.wait_ge(y_ready, t + 1)
                act.sem_inc(hold, 1)
                s.copy(acc[:, bass.ds(t, 1), 0:D].rearrange("p a d -> p (a d)"), ybuf[:, q, :]).then_inc(y_kept, 1)
                if not first:
                    act.wait_ge(y_summed, t * 2 - 2)
                s.activation(ysq[:, q, :], ybuf[:, q, :], ACT.Square).then_inc(y_kept, 1)
            turn_out(0, 0, True)
            turn_out(1, 1, True)
            keep_y(0, 0, True)
            turn_out(2, 0)
            keep_y(1, 1, True)
            with act.Fori(1, DENSE_PAIRS) as i:
                for q in range(2):
                    turn_out(i * 2 + (q + 1), 1 - q)
                    keep_y(i * 2 + q, q)
            keep_y(TILES - 1, 0)
            act.wait_ge(bn2_step, 4)
            s.activation(sd2, scale2, ACT.Sqrt, bias=small[:, 0:1]).then_inc(bn2_sd, 1)

        def layer1_vector(dve, link, links, make_onehot, add_lot):
            done = SDVE.done
            dve.wait_ge(x1_stored, 16 * TILES)
            dve.wait_ge(colsum_ps, 1)
            done(v.tensor_copy(colsum, psD[:, 0:8]), "sums")
            done(v.tensor_copy(select_last, ident[:, P - 1:P].broadcast_to([P, P])), "sel")
            done(v.memset(ones_mat, 1.0), "ones_mat")
            done(v.memset(values, 1.0), "ones")
            dve.wait_ge(vec_loaded, 32)
            SDVE.wait(dve, "sums")
            k = [0]

            def step(ins, wait=True):
                k[0] += 1
                ins.then_inc(bn1_step, 1)
                if wait:
                    dve.wait_ge(bn1_step, k[0])
            step(v.tensor_scalar(mean_c, colsum[:, 0:KD], 1.0 / N, None, ALU.mult))
            step(v.tensor_scalar(var_c, colsum[:, KD:2 * KD], 1.0 / N, None, ALU.mult))
            step(v.tensor_tensor(shift_c, mean_c, mean_c, ALU.mult))
            step(v.tensor_tensor(var_c, var_c, shift_c, ALU.subtract))
            dve.wait_ge(bn1_sd, 1)
            step(v.reciprocal(sd_c, sd_c))
            step(v.tensor_tensor(scale_c, g1c, sd_c, ALU.mult))
            step(v.tensor_tensor(shift_c, mean_c, scale_c, ALU.mult))
            v.tensor_tensor(shift_c, b1c, shift_c, ALU.subtract).then_inc(bn1_shift, 1)
            dve.wait_ge(bn1_ps, 1)
            step(v.tensor_copy(shrow, psE[0:1, :]))
            assert k[0] == SHIFT_ROW
            SDVE.wait(dve, "ones")
            for t, ps in enumerate((psD, psE)):
                SPE.wait(dve, f"v{t}")
                done(v.tensor_copy(values[:, t, :, 0:DH], ps[:, :].rearrange("p (h d) -> p h d", h=H)), f"v{t}")
            SPE.wait(dve, "diag")
            done(v.tensor_copy(dg, psD[:, 0:32]), "diag")
            dve.wait_ge(bc_loaded, 16)
            for n, row in enumerate((shrow, bcrow)):
                for m in range(3):
                    last = n == 1 and m == 2
                    ins = v.tensor_copy(parts1[:, 3 * n + m, :], row)
                    if last:
                        ins.then_inc(parts_ready, 1)
                    else:
                        step(ins)
                    if m < 2:
                        step(v.tensor_tensor(row, row, parts1[:, 3 * n + m, :], ALU.subtract))
            dve.wait_ge(Wc_loaded, 16)
            for kk in range(KD):
                step(v.tensor_scalar(Wc_s[:, kk, :], Wc_s[:, kk, :], scale_c[:, kk:kk + 1], None, ALU.mult))

            def half_bank(h):
                return (psA, psB)[h // 2 % 2][:, h % 2 * 512:h % 2 * 512 + 512]
            for h in hs:
                SACT.wait(dve, f"uk{h}")
                done(v.tensor_reduce(mxk[:, h:h + 1], uk[:, h, :, :].rearrange("p t m -> p (t m)"), AX_X, ALU.max), f"mk{h}")
            SPE.wait(dve, "kmT")
            done(v.tensor_reduce(km8[0:H, :], psC[0:H, 0:P], AX_X, ALU.max), "km")
            SDVE.wait(dve, "km")
            done(v.tensor_scalar(kmd[0:H, :], ident[0:H, 0:H], km8[0:H, :], None, ALU.mult), "kmd")
            SPE.wait(dve, "kmB")
            done(v.scalar_tensor_tensor(bias_k.rearrange("p (h t) -> p h t", t=NT),
                                        psC[:, 512:512 + H].unsqueeze(2).broadcast_to([P, H, NT]), -1.0,
                                        dg[:, 16:32].rearrange("p (h t) -> p h t", t=NT), ALU.mult, ALU.subtract), "bk")

            def max_q(h):
                SPE.wait(dve, f"uq{h}")
                m = mxq[:, 2 * h:2 * h + 2]
                done(v.tensor_reduce(m, half_bank(h).rearrange("p (t m) -> p t m", t=NT), AX_X, ALU.max), f"mq{h}")
                SDVE.wait(dve, f"mq{h}")
                done(v.scalar_tensor_tensor(bias_q[:, 2 * h:2 * h + 2], m, -1.0, dg[:, 2 * h:2 * h + 2],
                                            ALU.mult, ALU.subtract), f"bq{h}")

            def shift_k(h):
                SACT.wait(dve, f"ek{h}")
                done(v.tensor_scalar(uk[:, h, :, :], uk[:, h, :, :], M ** -0.5, KEPS, ALU.mult, ALU.add), f"kf{h}")

            def keep_kv(h):
                SPE.wait(dve, f"kv{h}")
                if h >= 2:
                    SPE.wait(dve, f"at{h - 2}")
                done(v.tensor_copy(kvs[:, h % 2, :, :], psD[:, h % 2 * 256:h % 2 * 256 + MT * (DH + 1)]
                                   .rearrange("p (t d) -> p t d", t=MT)), f"kv{h}")
            max_q(0)
            shift_k(0)
            max_q(1)
            keep_kv(0)
            for h in hs:
                SACT.wait(dve, f"eq{h}")
                done(v.tensor_scalar(qf[:, h % 2, :, :], qf[:, h % 2, :, :], M ** -0.5, KEPS, ALU.mult, ALU.add), f"qf{h}")
                if h < H - 1:
                    shift_k(h + 1)
                if h < H - 2:
                    max_q(h + 2)
                if h < H - 1:
                    keep_kv(h + 1)
                SPE.wait(dve, f"at{h}")
                av = psE[:, h % 2 * 256:h % 2 * 256 + NT * (DH + 1)].rearrange("p (t d) -> p t d", t=NT)
                z = zden[:, 2 * (h % 2):2 * (h % 2) + 2]
                done(v.tensor_scalar(z, av[:, :, DH], KEPS, None, ALU.add), f"zd{h}")
                SDVE.wait(dve, f"zd{h}")
                done(v.reciprocal(z, z), f"zr{h}")
                SDVE.wait(dve, f"zr{h}")
                done(v.tensor_tensor(attn[:, :, h * DH:(h + 1) * DH], av[:, :, 0:DH],
                                     z.unsqueeze(2).broadcast_to([P, NT, DH]), ALU.mult), f"at{h}")
            for t in range(NT):
                if t == 0:
                    SPE.wait(dve, "last")
                    SACT.wait(dve, "wo")
                done(v.tensor_tensor(hattn[:, t, :], hattn[:, t, :], psD[:, :], ALU.subtract), f"hat{t}")
            step(v.memset(acc_flat[:, SCRATCH:], 0.0))
            dve.wait_ge(acc_cleared, 1)
            dve.sem_inc(lot1_added, ADD_CREDIT)
            make_onehot(nodeB, 0, 0, onehot1_ready)
            with dve.Fori(0, ROWS // 2) as i:
                for q in range(2):
                    tiles = [dve.value_load(tileB[0:1, a, bass.ds(i * 2 + q, 1)], min_val=0, max_val=TILES - 1)
                             for a in range(LOTS)]
                    for a in range(LOTS):
                        if a == 1:
                            dve.wait_ge(lot1_ps, i * 8 + (4 * q + LOT_CREDIT))
                            make_onehot(nodeB, i * 2 + (q + 1), 1 - q, onehot1_ready)
                        dve.wait_ge(lot1_added, i * 8 + (4 * q + a + ADD_CREDIT))
                        dve.wait_ge(lot1_ps, i * 8 + (4 * q + a + 1 + LOT_CREDIT))
                        d = acc[:, bass.ds(tiles[a], 1), 0:D + 1].rearrange("p a d -> p (a d)")
                        v.tensor_tensor(d, d, (psA, psB)[a % 2][:, 0:D + 1], ALU.add).then_inc(lot1_added, 1)
            dve.wait_ge(lot1_added, ADD_CREDIT + ROWS * LOTS)
            v.tensor_scalar(indc, acc[:, :, D], 1.0, None, ALU.min).then_inc(deg_ready, 1)
            link(v.tensor_scalar(rdeg, acc[:, :, D], 1.0, None, ALU.max))
            link(v.reciprocal(rdeg, rdeg))
            dve.wait_ge(bias_stored, 32)
            dve.wait_ge(ind_ps, 1)
            v.memset(ind_rows, 1.0).then_inc(ind_ready, 1)
            v.tensor_copy(indT, psD[0:TILES, 0:P]).then_inc(ind_ready, 1)

            def average(t, q, first=False):
                if not first:
                    dve.wait_ge(aggT_ps, t - 1)
                v.tensor_scalar(aggn[:, q, :], acc[:, bass.ds(t, 1), 0:D].rearrange("p a d -> p (a d)"),
                                rdeg[:, bass.ds(t, 1)], None, ALU.mult).then_inc(aggn_ready, 1)

            def make_y(t, q, loads, first=False):
                dve.wait_ge(conv_ps, t + 1)
                dve.wait_ge(hc_in[q], loads)
                if not first:
                    dve.wait_ge(y_kept, t * 2 - 2)
                    dve.wait_ge(y_summed, t * 2 - 2)
                return v.scalar_tensor_tensor(ybuf[:, q, :], psA[:, q * 512:(q + 1) * 512], 0.0, h_in[:, q, :],
                                              ALU.max, ALU.add)
            average(0, 0, True)
            average(1, 1, True)
            for t in range(NT):
                average(t + 2, t)
                link(make_y(t, t, 16, True))
                v.tensor_tensor(ybuf[:, t, :], ybuf[:, t, :], hattn[:, t, :], ALU.add).then_inc(y_ready, 1)
            with dve.Fori(1, DENSE_PAIRS - 1) as i:
                for q in range(2):
                    average(i * 2 + (q + 2), q)
                    make_y(i * 2 + q, q, i * 16 + 16).then_inc(y_ready, 1)
            for q in range(2):
                if q == 0:
                    average(TILES - 1, 0)
                make_y(TILES - 3 + q, q, 16 * DENSE_PAIRS).then_inc(y_ready, 1)
            make_y(TILES - 1, 0, 16 * (DENSE_PAIRS + 1)).then_inc(y_ready, 1)
            dve.wait_ge(g2_loaded, 32)
            dve.wait_ge(total_ps, 1)
            n2 = [0]

            def step2(ins, signal=bn2_step):
                n2[0] += 1
                ins.then_inc(signal, 1)
                dve.wait_ge(signal, n2[0])
            step2(v.tensor_scalar(mean2, psA[:, 0:D], 1.0 / N, None, ALU.mult))
            step2(v.tensor_tensor(shift2, mean2, mean2, ALU.mult))
            step2(v.tensor_scalar(scale2, psA[:, D:2 * D], 1.0 / N, None, ALU.mult))
            step2(v.tensor_tensor(scale2, scale2, shift2, ALU.subtract))
            dve.wait_ge(bn2_sd, 1)
            step2(v.reciprocal(sd2, sd2))
            step2(v.tensor_tensor(scale2, g2row, sd2, ALU.mult))
            step2(v.tensor_tensor(shift2, mean2, scale2, ALU.mult))
            v.tensor_tensor(shift2, b2row, shift2, ALU.subtract).then_inc(bn2_ready, 1)

            def finish(t, q, stores):
                dve.sem_inc(hold, 1)
                v.tensor_tensor(tbuf[:, q, :], acc[:, bass.ds(t, 1), 0:D].rearrange("p a d -> p (a d)"), scale2,
                                ALU.mult).then_inc(scaled, 1)
                dve.wait_ge(scaled, t + 1)
                dve.wait_ge(shifted, t + 1)
                if stores is not None:
                    dve.wait_ge(out_stored[q], stores)
                v.tensor_tensor(obuf[:, q, :], tbuf[:, q, :], x1buf[:, q, :], ALU.add).then_inc(out_ready, 1)
            for q in range(4):
                finish(q, q, None)
            with dve.Fori(1, QUADS) as i:
                for q in range(4):
                    finish(i * 4 + q, q, i * 16)
            finish(TILES - 1, 0, 16 * QUADS)

        def layer1_tensor(pe):
            done = SPE.done
            pe.sem_inc(lot1_ps, LOT_CREDIT)
            pe.wait_ge(hA_ready, NT)
            for k in range(KD):
                for t in range(NT):
                    ins = pet.transpose(psA[:, k * MAXN + t * P:k * MAXN + (t + 1) * P], hA[:, t, k * P:(k + 1) * P], ident[:, :])
            done(ins, "hT")
            pe.wait_ge(proj_loaded, 32)
            for t in range(MT):
                ins = pet.transpose(psE[:, t * P:(t + 1) * P], proj_s[:, t, :, :].rearrange("p u d -> p (u d)"), ident[:, :])
            done(ins, "projT")
            SACT.wait(pe, "hT")
            pe.wait_ge(Wqkv_loaded, 48)
            for w, ps, name in ((Wq_s, psB, "qT"), (Wk_s, psC, "kT")):
                for j in range(KD):
                    for k in range(KD):
                        ins = pet.matmul(ps[:, j * MAXN:(j + 1) * MAXN], w[:, k, j * P:(j + 1) * P], hT[:, k, :],
                                         start=(k == 0), stop=(k == KD - 1))
                done(ins, name)
            SACT.wait(pe, "projT")
            pe.wait_ge(bn1_shift, 1)
            pe.wait_ge(Wc_loaded, 16)
            for k in range(KD):
                ins = pet.matmul(psE[0:1, :], shift_c[:, k:k + 1], Wc_s[:, k, :], start=(k == 0), stop=(k == KD - 1))
            ins.then_inc(bn1_ps, 1)
            SDVE.wait(pe, "sums")
            for t, ps in enumerate((psD, psE)):
                if t == 1:
                    pe.wait_ge(bn1_step, SHIFT_ROW)
                for k in range(KD):
                    ins = pet.matmul(ps[:, :], hT[:, k, t * P:(t + 1) * P], Wv_s[:, k, :], start=(k == 0), stop=(k == KD - 1))
                done(ins, f"v{t}")
            SACT.wait(pe, "sq")
            SDVE.wait(pe, "v0")
            for n in range(2):
                for j in range(KD):
                    for t in range(NT):
                        c = n * 16 + 4 * j + t
                        at = n * KD * MAXN + j * MAXN + t * P
                        ins = pet.matmul(psD[:, c:c + 3:2], squares[:, at:at + P], half[:, :], start=True, stop=True)
            done(ins, "diag")

            def half_bank(h):
                return (psA, psB)[h // 2 % 2][:, h % 2 * 512:h % 2 * 512 + 512]

            def features(tT, h, name):
                j, o = h // 2, DH * (h % 2)
                for t in range(NT):
                    ins = pet.matmul(half_bank(h)[:, t * M:(t + 1) * M], tT[o:o + DH, j, t * P:(t + 1) * P],
                                     projT[o:o + DH, :], start=True, stop=True)
                done(ins, f"{name}{h}")
            SACT.wait(pe, "kT")
            for h in hs:
                if h >= 4:
                    SACT.wait(pe, f"uk{h - 4}")
                features(kT, h, "uk")
            SDVE.wait(pe, f"mk{H - 1}")
            done(pet.transpose(psC[0:H, 0:P], mxk, ident[:, :]), "kmT")
            SDVE.wait(pe, "kmd")
            done(pet.matmul(psC[:, 512:512 + H], ones_mat[0:H, :], kmd[0:H, :], start=True, stop=True), "kmB")
            SACT.wait(pe, f"uk{H - 1}")
            def sum_kv(h):
                SDVE.wait(pe, f"kf{h}")
                SDVE.wait(pe, f"kv{h - 1}" if h >= 1 else "diag")
                for mt in range(MT):
                    c = h % 2 * 256 + mt * (DH + 1)
                    for t in range(NT):
                        ins = pet.matmul(psD[:, c:c + DH + 1], uk[:, h, t, mt * P:(mt + 1) * P], values[:, t, h, :],
                                         start=(t == 0), stop=(t == NT - 1))
                done(ins, f"kv{h}")
            features(qT, 0, "uq")
            features(qT, 1, "uq")
            sum_kv(0)
            for h in hs:
                SDVE.wait(pe, f"qf{h}")
                if h >= 2:
                    SACT.wait(pe, f"qfT{h - 2}")
                else:
                    SDVE.wait(pe, "bk")
                for mt in range(MT):
                    for t in range(NT):
                        c = h % 2 * 512 + mt * MAXN + t * P
                        ins = pet.transpose(psC[:, c:c + P], qf[:, h % 2, t, mt * P:(mt + 1) * P], ident[:, :])
                done(ins, f"qfT{h}")
                if h < H - 2:
                    if h + 2 >= 4:
                        SACT.wait(pe, f"eq{h - 2}")
                    features(qT, h + 2, "uq")
                if h < H - 1:
                    sum_kv(h + 1)
                SACT.wait(pe, f"qfT{h}")
                SDVE.wait(pe, f"kv{h}")
                SDVE.wait(pe, f"at{h - 1}" if h >= 1 else "v1")
                for t in range(NT):
                    c = h % 2 * 256 + t * (DH + 1)
                    for mt in range(MT):
                        ins = pet.matmul(psE[:, c:c + DH + 1], qfT[:, h % 2, mt, t * P:(t + 1) * P], kvs[:, h % 2, mt, :],
                                         start=(mt == 0), stop=(mt == MT - 1))
                done(ins, f"at{h}")
            SDVE.wait(pe, f"at{H - 1}")
            SACT.wait(pe, f"eq{H - 1}")
            for k in range(KD):
                for t in range(NT):
                    ins = pet.transpose(psA[:, k * MAXN + t * P:k * MAXN + (t + 1) * P], attn[:, t, k * P:(k + 1) * P], ident[:, :])
            done(ins, "aT")
            SACT.wait(pe, "aT")
            pe.wait_ge(Wo_loaded, 16)
            for t in range(NT):
                for k in range(KD):
                    ins = pet.matmul(psB[:, t * 512:(t + 1) * 512], hT[:, k, t * P:(t + 1) * P], Wo_s[:, k, :],
                                     start=(k == 0), stop=(k == KD - 1))
            done(ins, "wo")
            SACT.wait(pe, "wo")
            done(pet.matmul(psD[:, :], select_last, hattn[:, NT - 1, :], start=True, stop=True), "last")
            with pe.Fori(0, ROWS // 2) as i:
                for q in range(2):
                    pe.wait_ge(onehot1_ready, i * 2 + (q + 1))
                    for a in range(LOTS):
                        psum = (psA, psB)[a % 2]
                        if a % 2 == 0:
                            pe.wait_ge(h_arrived[q][a // 2], i * 64 + 64)
                        pe.wait_ge(lot1_added, i * 8 + (4 * q + a + ADD_CREDIT - 1))
                        for b in (2 * a, 2 * a + 1):
                            pet.matmul(psum[:, 0:D], onehot[:, q, b, :], rows_l1[4 * q + a][:, b % 2 * D:(b % 2 + 1) * D],
                                       start=(b % 2 == 0), stop=(b % 2 == 1))
                        for b in (2 * a, 2 * a + 1):
                            ins = pet.matmul(psum[:, D:D + 1], onehot_b[:, q, b, :], one_b[:, :],
                                             start=(b % 2 == 0), stop=(b % 2 == 1))
                        ins.then_inc(lot1_ps, 1)
            pe.wait_ge(deg_ready, 1)
            pet.transpose(psD[0:TILES, 0:P], indc, ident[:, :]).then_inc(ind_ps, 1)

            def turn(t, q, first=False):
                pe.wait_ge(aggn_ready, t + 1)
                if not first:
                    pe.wait_ge(aggT_ready, t - 1)
                for k in range(KD):
                    ins = pet.transpose(psC[:, q * 512 + k * P:q * 512 + (k + 1) * P], aggn[:, q, k * P:(k + 1) * P], ident[:, :])
                ins.then_inc(aggT_ps, 1)

            def convolve(t, q, first=False):
                pe.wait_ge(aggT_ready, t + 1)
                if not first:
                    pe.wait_ge(y_ready, t - 1)
                for k in range(KD):
                    pet.matmul(psA[:, q * 512:(q + 1) * 512], aggT[:, q, k * P:(k + 1) * P], Wc_s[:, k, :],
                               start=(k == 0), stop=False)
                if first:
                    pe.wait_ge(ind_spread, 32)
                    pe.wait_ge(bias_stored, 32)
                pet.matmul(psA[:, q * 512:(q + 1) * 512],
                           ind_rows.rearrange("p (t n) -> p t n", n=P)[:, bass.ds(t, 1), :].rearrange("p a n -> p (a n)"),
                           bias_rows, start=False, stop=True).then_inc(conv_ps, 1)
            turn(0, 0, True)
            turn(1, 1, True)
            convolve(0, 0, True)
            turn(2, 0)
            convolve(1, 1, True)
            with pe.Fori(1, DENSE_PAIRS) as i:
                for q in range(2):
                    turn(i * 2 + (q + 1), 1 - q)
                    convolve(i * 2 + q, q)
            convolve(TILES - 1, 0)
            pe.wait_ge(y_summed, 2 * TILES)
            for n, total in enumerate((ysum, ysum2)):
                ins = pet.matmul(psA[:, n * 512:(n + 1) * 512], ones_mat, total, start=True, stop=True)
            ins.then_inc(total_ps, 1)

        N_CONST = 13

        @block.sync
        def _(sp):
            def load_keys(order, signal):
                for edge_end, place in zip(order, (wk1, wk2)):
                    sp.dma_start(place[0:EDGE_ROWS, 0:EDGE_COLS].bitcast(I32),
                                 edge_end.rearrange("(p c) -> p c", c=EDGE_COLS)).then_inc(signal, 16)
            load_keys((src, dst), keys_loaded)
            for k in range(KD):
                sp.dma_start(W4[:, k, :, :], W0[:, k * P:(k + 1) * P, :].rearrange("h p o -> p h o")).then_inc(w0_loaded, 16)
            sp.dma_start(attb.rearrange("p h a o -> p (h a o)"),
                         att_w.rearrange("h a -> (h a)").rearrange("(u c) -> u c", u=1).broadcast_to([P, H * 2 * O])
                         ).then_inc(w0_loaded, 16)
            sp.wait_ge(keys_loaded, 32)
            for a in range(0, TILES - 1, 12):
                sp.dma_start(acc[:, a:a + 12, 0:D],
                             x[a * P:(a + 12) * P, :].rearrange("(t p) d -> p t d", p=P)).then_inc(x_loaded, 16)
            sp.wait_ge(consts, N_CONST)
            sp.dma_start(acc[0:LAST, TILES - 1, 0:D], x[(TILES - 1) * P:N, :]).then_inc(x_loaded, 16)
            with sp.Fori(0, DENSE_PAIRS) as i:
                for q in range(2):
                    sp.wait_ge(feat_ready, i * 2 + (q + 1))
                    sp.dma_start(feat_table[bass.ds(i * (2 * P) + q * P, P), :], fbuf[:, q, :]).then_inc(feat_stored[q], 16)
            sp.wait_ge(feat_ready, TILES)
            sp.dma_start(feat_table[(TILES - 1) * P:TILES * P, :], fbuf[:, 0, :]).then_inc(feat_stored[0], 16)
            sp.dma_start(ad_table.rearrange("(t p) h -> p t h", p=P), alphas[:, :, H:2 * H]).then_inc(ad_stored, 16)
            sp.wait_ge(fields, 1)
            sp.dma_start(slot_nodes, oh_flat.bitcast(BF16)[:, 0:COLS]).then_inc(slots_stored, 16)
            sp.wait_ge(keysB_free, 1)
            load_keys((dst, src), keys_loaded2)
            layer0_sync(sp)


        @block.gpsimd
        def _(pool):
            c = [0]

            def const(ins, wait=False):
                ins.then_inc(consts, 1)
                c[0] += 1
                if wait:
                    pool.wait_ge(consts, c[0])
            const(g.memset(acc[:, TILES - 1, 0:D], 0.0))
            const(g.memset(ident[:, :], 0.0))
            const(g.memset(spread, 0.0), wait=True)
            const(g.affine_select(out=ident[:, :], in_=ident[:, :], compare_op=ALU.not_equal, fill=1.0, base=0,
                                  pattern=[[-1, P]], channel_multiplier=1))
            sp3 = spread.rearrange("p (r h) -> p r h", h=H)
            const(g.affine_select(out=sp3, in_=sp3, compare_op=ALU.not_equal, fill=1.0, base=0,
                                  pattern=[[-1, P], [0, H]], channel_multiplier=1))
            const(g.iota(part[:, 0:1], [[0, 1]], base=0, channel_multiplier=1))
            const(g.iota(iota_pad[:, :], [[1, PAD_COLS]], base=0, channel_multiplier=0,
                         allow_small_or_imprecise_dtypes=True))
            const(g.iota(iota_row[:, :], [[1, P]], base=0, channel_multiplier=0, allow_small_or_imprecise_dtypes=True))
            const(g.iota(iota_col[:, :], [[0, 1]], base=0, channel_multiplier=1, allow_small_or_imprecise_dtypes=True))
            const(g.memset(staged_ad[:, :, :], 0.0))
            const(g.memset(rows2[:, :, :], 0.0))
            const(g.memset(one_b[:, :], 1.0))
            const(g.memset(small[:, 0:1], LN_EPS))
            assert c[0] == N_CONST
            pool.wait_ge(ad_stored, 16)
            for q in range(2):
                pool.wait_ge(feat_stored[q], 16 * (DENSE_PAIRS + 1 - q))
            g.memset(gathered_ad[:, :, ROWS:ROWS_G, :], 0.0).then_inc(ad_padded, 1)
            with pool.Fori(0, ROWS) as r:
                for hf in range(2):
                    pool.wait_ge(idx1, r * 2 + (hf + 1))
                    pool.sem_inc(hold, 1)
                    for b in range(4 * hf, 4 * hf + 4):
                        g.indirect_dma_start(staged_ad[:, b, :], None, ad_table,
                                             bass.IndirectOffsetOnAxis(ap=idx[:, 0, b:b + 1], axis=0),
                                             bounds_check=N - 1, oob_is_err=False).then_inc(ad_arrived[hf], 16)
            layer0_gpsimd(pool)

        @block.scalar
        def _(act):
            links = [0]

            def link(ins):
                links[0] += 1
                ins.then_inc(act_link, 1)
                act.wait_ge(act_link, links[0])
            act.wait_ge(consts, N_CONST)
            act.wait_ge(x_loaded, 16 * 5)
            def statistics(function, column):
                for t in range(TILES):
                    if t >= 2:
                        act.wait_ge(act_link, links[0] - 1)
                    s.activation(junk[:, t % 2, :], acc[:, t, 0:D], function,
                                 accum_out=stat[:, column, t:t + 1]).then_inc(act_link, 1)
                    links[0] += 1
                act.wait_ge(act_link, links[0])
            statistics(ACT.Identity, 0)
            link(s.mul(stat[:, 1, :], stat[:, 0, :], -1.0 / D))
            for t in range(TILES):
                if t >= 2:
                    act.wait_ge(act_link, links[0] - 1)
                s.activation(junk[:, t % 2, :], acc[:, t, 0:D], ACT.Square, bias=stat[:, 1, t:t + 1],
                             accum_out=stat[:, 2, t:t + 1]).then_inc(act_link, 1)
                links[0] += 1
            act.wait_ge(act_link, links[0])
            s.activation(stat[:, 3, :], stat[:, 2, :], ACT.Sqrt, scale=1.0 / D, bias=small[:, 0:1]).then_inc(var_ready, 1)
            act.wait_ge(rstd_ready, 1)

            def make_h(t, q):
                s.activation(hbuf[:, q, :], acc[:, bass.ds(t, 1), 0:D].rearrange("p a d -> p (a d)"), ACT.Relu,
                             scale=stat[:, 3, bass.ds(t, 1)], bias=stat[:, 1, bass.ds(t, 1)]).then_inc(h_ready, 1)

            def copy_hT(t, q, first=False):
                act.wait_ge(hT_ps, t + 1)
                if not first:
                    act.wait_ge(feat_ps, t - 1)
                s.copy(hTbuf[:, q, :], psC[:, q * D:(q + 1) * D]).then_inc(hT_ready, 1)

            def copy_feat(t, q, stores):
                act.wait_ge(feat_ps, t + 1)
                s.copy(alphas[:, bass.ds(t, 1), :], (psD, psE)[q][:, 0:2 * H].rearrange("p (a c) -> p a c", a=1))
                if stores is not None:
                    act.wait_ge(feat_stored[q], stores * 16)
                    act.sem_inc(hold, 1)
                s.copy(fbuf[:, q, :], psB[:, q * D:(q + 1) * D]).then_inc(feat_ready, 1)

            make_h(0, 0)
            make_h(1, 1)
            copy_hT(0, 0, True)
            make_h(2, 0)
            for t in range(2):
                copy_hT(t + 1, 1 - t, t == 0)
                make_h(t + 3, 1 - t)
                copy_feat(t, t, None)
            with act.Fori(1, DENSE_PAIRS - 1) as i:
                for q in range(2):
                    copy_hT(i * 2 + (q + 1), 1 - q)
                    act.sem_inc(hold, 1)
                    make_h(i * 2 + (q + 3), 1 - q)
                    copy_feat(i * 2 + q, q, i)
            for t in range(TILES - 3, TILES):
                if t + 1 < TILES:
                    copy_hT(t + 1, (t + 1) % 2)
                copy_feat(t, t % 2, t // 2)
            act.wait_ge(slotsA, 1)
            act.wait_ge(feat_stored[0], 16 * (DENSE_PAIRS + 1))
            act.wait_ge(feat_stored[1], 16 * DENSE_PAIRS)
            for hf in range(2):
                s.copy(idx[:, 0, 4 * hf:4 * hf + 4], minorA[:, 4 * hf:4 * hf + 4, 0]).then_inc(idx1, 1)
            with act.Fori(0, ROWS) as r:
                for hf in range(2):
                    bs = slice(4 * hf, 4 * hf + 4)
                    act.wait_ge(ad_arrived[hf], r * 64 + 64)
                    act.sem_inc(hold, 1)
                    s.copy(gathered_ad[:, bs, bass.ds(r, 1), :].rearrange("p b a h -> p b (a h)"),
                           staged_ad[:, bs, :]).then_inc(ad_kept, 1)
                    act.wait_ge(ad_kept, r * 2 + (hf + 1))
                    act.sem_inc(hold, 1)
                    s.copy(idx[:, 0, bs], minorA[:, bs, bass.ds(r + 1, 1)].rearrange("p b a -> p (b a)")).then_inc(idx1, 1)
            layer0_scalar(act, link, links)

        @block.vector
        def _(dve):
            links = [0]

            def link(ins):
                links[0] += 1
                ins.then_inc(dve_link, 1)
                dve.wait_ge(dve_link, links[0])

            dve.wait_ge(consts, N_CONST)
            v.memset(ones[:, :], 1.0).then_inc(dve_link, 1)
            v.memset(half[:, :], 0.0).then_inc(dve_link, 1)
            v.tensor_copy(ident_b, ident[:, :]).then_inc(dve_link, 1)
            links[0] += 3
            dve.wait_ge(dve_link, links[0])
            for u in range(2):
                link(v.memset(half[u * DH:(u + 1) * DH, u:u + 1], 0.5))
            link(v.tensor_scalar(part[:, 2:3], part[:, 0:1], 1, None, ALU.logical_shift_right))
            link(v.tensor_scalar(part[:, 3:4], part[:, 0:1], 1, None, ALU.bitwise_and))
            link(v.tensor_tensor(part[:, 1:2], part[:, 0:1], part[:, 2:3], ALU.bitwise_xor))
            link(v.tensor_scalar(signi[:, 0:1], part[:, 0:1], 1, None, ALU.bitwise_and))
            for k in range(ALL_BITS - ROW_BITS):
                link(v.tensor_scalar(signi[:, k + 1:k + 2], part[:, 1:2], k, 1, ALU.logical_shift_right, ALU.bitwise_and))
            link(v.tensor_scalar(signs[:, :], signi[:, :], -2.0, 1.0, ALU.mult, ALU.add))
            link(v.tensor_scalar(padc[:, 0:1], part[:, 3:4], float(PAD_COLS), None, ALU.mult))
            link(v.tensor_scalar(padc[:, 1:2], part[:, 2:3], float(P), float(P - 1 - NO_NODE), ALU.mult, ALU.add))
            link(v.tensor_scalar(iota_pad[:, :], iota_pad[:, :], padc[:, 0:1], None, ALU.add))

            steps = [0]

            def prepare(turn):
                major = wk1[0:EDGE_ROWS, 0:EDGE_COLS].bitcast(I32)
                minor = wk2[0:EDGE_ROWS, 0:EDGE_COLS].bitcast(I32)
                key = keyX.bitcast(I32)
                edge_key = key[0:EDGE_ROWS, 0:EDGE_COLS]
                link(v.tensor_scalar(edge_key, major, P.bit_length() - 1, None, ALU.logical_shift_right))
                link(v.tensor_copy(keyY[0:EDGE_ROWS, 0:EDGE_COLS], edge_key))
                link(v.memset(count[:, :, :], 0.0))
                thrown = keyX.bitcast(BF16).rearrange("p (a c) -> p a c", a=2)
                for j in range(TILES):
                    if j >= 2:
                        dve.wait_ge(dve_link, links[0] - 1)
                    v.tensor_scalar(thrown[0:EDGE_ROWS, j % 2, 0:EDGE_COLS], keyY[0:EDGE_ROWS, 0:EDGE_COLS], float(j),
                                    None, ALU.is_equal, ALU.add,
                                    accum_out=count[0:EDGE_ROWS, j, 0:1]).then_inc(dve_link, 1)
                    links[0] += 1
                dve.wait_ge(dve_link, links[0])
                v.tensor_copy(count[:, :, 1:2], count[:, :, 0:1]).then_inc(counted, 1)
                link(v.memset(key, (NO_NODE << SHIFT) | MINOR_MASK | KEY_BASE))
                link(v.tensor_scalar(edge_key, major, SHIFT, KEY_BASE, ALU.logical_shift_left, ALU.bitwise_or))
                link(v.tensor_tensor(edge_key, edge_key, minor, ALU.bitwise_or))
                dve.wait_ge(pads_known, turn)
                link(v.tensor_scalar(padi[:, 0:1], psD[:, 0:1], -1.0, float(1 << ALL_BITS), ALU.mult, ALU.add))
                link(v.tensor_scalar(padi[:, 1:2], padi[:, 0:1], LOT - 1, None, ALU.bitwise_and))
                link(v.tensor_copy(padc[:, 2:3], padi[:, 1:2]))
                pads = keyY[:, EDGE_COLS:COLS]
                link(v.tensor_scalar(pads, iota_pad[:, :], padc[:, 2:3], padc[:, 1:2], ALU.is_lt, ALU.mult))
                link(v.tensor_scalar(pads.bitcast(I32), pads, float(NO_NODE), None, ALU.add))
                link(v.tensor_scalar(key[:, EDGE_COLS:COLS], pads.bitcast(I32), SHIFT, MINOR_MASK | KEY_BASE,
                                     ALU.logical_shift_left, ALU.bitwise_or))
                v.tensor_scalar(keyY, keyX, signs[:, 0:1], None, ALU.mult).then_inc(sort_step, 1)
                steps[0] += 1

            def stage(j, mirror, source, target):
                dve.wait_ge(sort_step, steps[0])

                def halves(buf):
                    w = buf.rearrange("p (n two h) -> p n two h", two=2, h=1 << j)
                    return w[:, :, 0, :], (w[:, :, 1, ::-1] if mirror else w[:, :, 1, :])
                (a, b), (low, high) = halves(source), halves(target)
                if source is psA_all:
                    copied = wk1[:, 0:COLS // 2].rearrange("p (n h) -> p n h", h=1 << j)
                    v.tensor_copy(copied, a).then_inc(sort_step, 1)
                    steps[0] += 1
                    dve.wait_ge(sort_step, steps[0])
                    a = copied
                v.tensor_tensor(low, a, b, ALU.min).then_inc(sort_step, 1)
                v.tensor_tensor(high, a, b, ALU.max).then_inc(sort_step, 1)
                steps[0] += 2

            psA_all = psA[:, :]

            def sort(turns, plan, between=None):
                bufs, at = (keyX, keyY), 1
                for m in range(1, ROW_BITS + 1):
                    if between and m == ROW_BITS - 2:
                        between()
                    for j in range(m - 1, -1, -1):
                        stage(j, j == m - 1 and j > 0, bufs[at], bufs[at ^ 1])
                        at ^= 1
                n = 0
                for m in range(ROW_BITS + 1, ALL_BITS + 1):
                    dve.wait_ge(sort_step, steps[0])
                    v.tensor_scalar(bufs[at ^ 1], bufs[at], signs[:, m - ROW_BITS:m - ROW_BITS + 1], None,
                                    ALU.mult).then_inc(sort_step, 1)
                    steps[0] += 1
                    at ^= 1
                    for js in (range(m - ROW_BITS - 1, -1, -1), range(ROW_BITS - 1, -1, -1)):
                        assert plan[n] == (steps[0], at), (plan[n], steps[0], at)
                        n += 1
                        dve.wait_ge(turned, turns + n)
                        for i, j in enumerate(js):
                            stage(j, False, psA_all if i == 0 else bufs[at], bufs[at ^ 1])
                            at ^= 1
                dve.wait_ge(sort_step, steps[0])
                return bufs[at], bufs[at ^ 1]

            def wait_rstd():
                dve.wait_ge(var_ready, 1)
                link(v.reciprocal(stat[:, 3, :], stat[:, 3, :]))
                v.tensor_tensor(stat[:, 1, :], stat[:, 1, :], stat[:, 3, :], ALU.mult).then_inc(rstd_ready, 1)

            def slot_fields(sorted_keys, other, minor_t, node_t, tile_t, turns, with_last):
                bits = sorted_keys.bitcast(I32)
                seg = wk1.bitcast(I32)
                link(v.tensor_scalar(seg, bits, SHIFT, None, ALU.logical_shift_right))
                link(v.tensor_scalar(seg, seg, P - 1, None, ALU.bitwise_and))
                link(v.tensor_scalar(other.bitcast(I32), bits, MINOR_MASK, None, ALU.bitwise_and))
                link(v.tensor_scalar(other, other.bitcast(I32), float(MINOR_MASK), OFF, ALU.is_equal, ALU.mult))
                link(v.tensor_tensor(wk2, other, seg, ALU.add))
                if with_last:
                    link(v.memset(same, 0.0))
                    link(v.tensor_tensor(same[:, 1:COLS], wk2[:, 1:COLS], wk2[:, 0:COLS - 1], ALU.is_equal))
                    link(v.memset(same[:, 0:COLS:P], 0.0))
                    dve.wait_ge(Wa_ready, 1)
                    v.tensor_copy(oh_flat.bitcast(BF16)[:, 0:COLS], wk2).then_inc(fields, 1)
                    v.scalar_tensor_tensor(wk1, same[:, 1:COLS + 1], OFF, wk2, ALU.mult, ALU.add).then_inc(fields, 1)
                else:
                    v.tensor_copy(small[:, 1:2], small[:, 0:1]).then_inc(fields, 1)
                dve.wait_ge(fieldsT, turns)
                bitsT = psA[:, :].bitcast(I32)
                link(v.tensor_scalar(seg, bitsT, MINOR_MASK, None, ALU.bitwise_and))
                link(v.tensor_copy(minor_t[:, :, :].rearrange("p b r -> p (b r)"), seg))
                link(v.tensor_scalar(tile_t,
                                     bitsT[0:1, :].rearrange("p (a two r) -> p a two r", two=2, r=P)[:, :, 0, :],
                                     SHIFT + 7, 63, ALU.logical_shift_right, ALU.bitwise_and))
                link(v.tensor_scalar(tile_t, tile_t, float(TILES - 1), None, ALU.min))
                link(v.tensor_copy(node_t[:, :, :].rearrange("p b r -> p (b r)"), psB[:, :]))
                if with_last:
                    link(v.tensor_copy(lastA[:, :, :].rearrange("p b r -> p (b r)"), psC[:, :]))

            dve.wait_ge(keys_loaded, 32)
            prepare(1)
            dve.wait_ge(w0_loaded, 16 * 5)
            for a in range(2):
                link(v.tensor_tensor(Wprod, W4, attb[:, :, a, :].unsqueeze(1).broadcast_to([P, KD, H, O]), ALU.mult))
                ins = v.tensor_reduce(Wa[:, :, a * H:(a + 1) * H], Wprod, AX_X, ALU.add)
                if a == 0:
                    link(ins)
                else:
                    ins.then_inc(Wa_ready, 1)
            kA, other = sort(0, planA, wait_rstd)
            slot_fields(kA, other, minorA, nodeA, tileA, 1, True)
            v.memset(small[:, 2:3], 0.0).then_inc(slotsA, 1)

            dve.wait_ge(slots_stored, 16)
            v.memset(small[:, 3:4], 0.0).then_inc(keysB_free, 1)
            dve.wait_ge(keys_loaded2, 32)
            prepare(2)
            kB, other = sort(CROSSINGS, planB)
            slot_fields(kB, other, minorB, nodeB, tileB, 2, False)
            v.memset(small[:, 4:5], 0.0).then_inc(sortB_done, 1)

            dve.wait_ge(feat_ready, TILES)
            link(v.memset(acc_flat, 0.0))
            maxima = (maxd[:, :, :], keys_flat[:, 0:TILES * H].rearrange("p (t h) -> p t h", h=H))
            for m in maxima:
                link(v.memset(m, -BIG))
            link(v.memset(runmaxE, 1.0))
            slot_ps = [ps[:, 0:SB * (H + 1)].rearrange("p (b h) -> p b h", h=H + 1) for ps in (psD, psE)]
            pen = [small[:, 8 + 8 * q:16 + 8 * q] for q in range(2)]
            both = [zbuf[:, q, :, :] for q in range(2)]
            lotmax = [small[:, 24 + 32 * q:56 + 32 * q].rearrange("p (a h) -> p a h", h=H) for q in range(2)]

            def last_onehot(r, q):
                v.tensor_tensor(onehot[:, q, :, :], iota_row[:, :].unsqueeze(1).broadcast_to([P, SB, P]),
                                lastA[:, :, bass.ds(r, 1)].broadcast_to([P, SB, P]), ALU.is_equal).then_inc(last_ready, 1)
            for q in range(2):
                last_onehot(q, q)
            for gr in range(GROUPS):
                dve.wait_ge(adT, 2 * gr + 2)
                link(v.tensor_scalar(mask, psB[:, :], BIG, -BIG, ALU.mult, ALU.add))
                v.tensor_tensor_scan(runmax, mask, psA[:, :], 0.0, ALU.add, ALU.max).then_inc(scanned, 1)
                dve.wait_ge(scanT, gr + 1)
                v.tensor_copy(runmaxE[:, :, :, 0:H], psC[:, :].rearrange("p (b r h) -> p b r h", b=SB, r=GROUP)
                              ).then_inc(runs_ready, 1)
                with dve.Fori(0, (min(GROUP * (gr + 1), ROWS) - GROUP * gr) // 2) as i:
                    def tile_of(a, q):
                        return dve.value_load(tileA[0:1, a, bass.ds(i * 2 + (gr * GROUP + q), 1)],
                                              min_val=0, max_val=TILES - 1)
                    base = gr * GROUP * 7
                    tiles = [[tile_of(a, 0) for a in range(LOTS)], []]
                    for q in range(2):
                        dve.wait_ge(slotmax, i * 2 + (gr * GROUP + q + 1))
                        v.tensor_scalar(pen[q], slot_ps[q][:, :, H], BIG, -BIG, ALU.mult, ALU.add).then_inc(taken, 1)
                    for q in range(2):
                        dve.wait_ge(taken, i * 14 + (base + q + 1))
                        v.tensor_tensor(both[q], slot_ps[q][:, :, 0:H], pen[q].unsqueeze(2).broadcast_to([P, SB, H]),
                                        ALU.add).then_inc(taken, 1)
                    for q in range(2):
                        dve.wait_ge(taken, i * 14 + (base + q + 3))
                        pair = both[q].rearrange("p (a two) h -> p a two h", two=2)
                        v.tensor_tensor(lotmax[q], pair[:, :, 0, :], pair[:, :, 1, :], ALU.max).then_inc(taken, 1)
                        last_onehot(i * 2 + (gr * GROUP + q + 2), q)
                    for q in range(2):
                        for a in range(LOTS):
                            dve.wait_ge(taken, i * 14 + (base + 4 * q + a + 5))
                            m = maxima[a % 2][:, bass.ds(tiles[q][a], 1), :].rearrange("p a h -> p (a h)")
                            v.tensor_tensor(m, m, lotmax[q][:, a, :], ALU.max).then_inc(taken, 1)
                            if q == 0:
                                tiles[1].append(tile_of(a, 1))
            dve.wait_ge(taken, ROWS * 7)
            link(v.tensor_tensor(maxd[:, :, :], maxima[0], maxima[1], ALU.max))
            c_part = alphas[:, :, H:2 * H]
            link(v.tensor_tensor(maxd[:, :, :], alphas[:, :, 0:H], maxd[:, :, :], ALU.add))
            dve.wait_ge(ad_stored, 16)
            link(v.scalar_tensor_tensor(c_part, maxd[:, :, :], SLOPE, maxd[:, :, :], ALU.mult, ALU.max))
            rest = wk2[:, 0:TILES * 2 * H].rearrange("p (t c) -> p t c", c=2 * H)
            link(v.tensor_copy(look[:, :, 0, :], alphas[:, :, :]))
            link(v.tensor_tensor(rest, alphas[:, :, :], look[:, :, 0, :], ALU.subtract))
            link(v.tensor_copy(look[:, :, 1, :], rest))
            link(v.tensor_tensor(rest, rest, look[:, :, 1, :], ALU.subtract))
            v.tensor_copy(look[:, :, 2, :], rest).then_inc(look_ready, 1)
            layer0_vector(dve, link, links)

        @block.tensor
        def _(pe):
            pe.wait_ge(consts, N_CONST)

            def cross(plan, n):
                step, at = plan[n]
                pe.wait_ge(sort_step, step)
                for b in range(SB):
                    ins = pet.transpose(psA[:, b * P:(b + 1) * P], keys[:, at, b * P:(b + 1) * P], ident[:, :])
                ins.then_inc(turned, 1)

            def count_pads(turn):
                pe.wait_ge(counted, turn)
                pet.matmul(psD[:, 0:1], count[:, :, :].rearrange("p a b -> p (a b)"), ones[:, :],
                           start=True, stop=True).then_inc(pads_known, 1)

            def turn_h(t, q, first=False):
                pe.wait_ge(h_ready, t + 1)
                if not first:
                    pe.wait_ge(hT_ready, t - 1)
                for k in range(KD):
                    ins = pet.transpose(psC[:, q * D + k * P:q * D + (k + 1) * P], hbuf[:, q, k * P:(k + 1) * P],
                                        ident[:, :])
                ins.then_inc(hT_ps, 1)

            def project(t, q, first=False):
                pe.wait_ge(hT_ready, t + 1)
                if not first:
                    pe.wait_ge(feat_ready, t - 1)
                for k in range(KD):
                    pet.matmul(psB[:, q * D:(q + 1) * D], hTbuf[:, q, k * P:(k + 1) * P],
                               W4[:, k, :, :].rearrange("p h o -> p (h o)"), start=(k == 0), stop=(k == KD - 1))
                for k in range(KD):
                    ins = pet.matmul((psD, psE)[q][:, 0:2 * H], hTbuf[:, q, k * P:(k + 1) * P], Wa[:, k, :],
                                     start=(k == 0), stop=(k == KD - 1))
                ins.then_inc(feat_ps, 1)

            count_pads(1)
            pe.wait_ge(Wa_ready, 1)
            turn_h(0, 0, True)
            turn_h(1, 1, True)
            project(0, 0, True)
            turn_h(2, 0)
            project(1, 1, True)
            done_pairs = 1
            for n in range(CROSSINGS):
                with pe.Fori(done_pairs, share[n]) as i:
                    for q in range(2):
                        turn_h(i * 2 + (q + 1), 1 - q)
                        project(i * 2 + q, q)
                done_pairs = share[n]
                cross(planA, n)
            assert done_pairs == DENSE_PAIRS
            project(TILES - 1, 0)

            def turn_fields(at, turn, with_last):
                pe.wait_ge(sort_step, (stepsA, stepsB)[turn - 1])
                pe.wait_ge(fields, (2, 3)[turn - 1])
                if with_last:
                    pe.wait_ge(feat_ready, TILES)
                for source, target in ((keys[:, at, :], psA), (wk2, psB)) + (((wk1, psC),) if with_last else ()):
                    for b in range(SB):
                        ins = pet.transpose(target[:, b * P:(b + 1) * P], source[:, b * P:(b + 1) * P], ident[:, :])
                ins.then_inc(fieldsT, 1)

            turn_fields(atA, 1, True)
            count_pads(2)
            pe.wait_ge(slotsA, 1)
            for n in range(CROSSINGS):
                cross(planB, n)
            turn_fields(atB, 2, False)
            pe.wait_ge(sortB_done, 1)

            for gr in range(GROUPS):
                pe.wait_ge(ad_kept, 2 * min(GROUP * (gr + 1), ROWS))
                if gr == GROUPS - 1:
                    pe.wait_ge(ad_padded, 1)
                for b in range(SB):
                    ins = pet.transpose(psA[:, b * P:(b + 1) * P],
                                        gathered_ad[:, b, gr * GROUP:(gr + 1) * GROUP, :].rearrange("p r h -> p (r h)"),
                                        ident[:, :])
                ins.then_inc(adT, 1)
                for c in range(2):
                    ins = pet.matmul(psB[:, c * 512:(c + 1) * 512], spread[:, gr * P:(gr + 1) * P],
                                     same[:, c * 512:(c + 1) * 512], start=True, stop=True)
                ins.then_inc(adT, 1)
                pe.wait_ge(scanned, gr + 1)
                for b in range(SB):
                    ins = pet.transpose(psC[:, b * P:(b + 1) * P], runmax[:, b * P:(b + 1) * P], ident[:, :])
                ins.then_inc(scanT, 1)
                pe.wait_ge(runs_ready, gr + 1)
                with pe.Fori(0, (min(GROUP * (gr + 1), ROWS) - GROUP * gr) // 2) as i:
                    for q in range(2):
                        pe.wait_ge(last_ready, i * 2 + (gr * GROUP + q + 1))
                        for b in range(SB):
                            ins = pet.matmul((psD, psE)[q][:, b * (H + 1):(b + 1) * (H + 1)], onehot[:, q, b, :],
                                             runmaxE[:, b, bass.ds(i * 2 + q, 1), :].rearrange("p a h -> p (a h)"),
                                             start=True, stop=True)
                        ins.then_inc(slotmax, 1)
            layer0_tensor(pe)



_INS = ['x', 'src', 'dst', 'L0_gnn_W', 'L0_gnn_att_w', 'L1_gnn_norm1_g', 'L1_gnn_norm1_b', 'L1_gnn_norm2_g',
        'L1_gnn_norm2_b', 'L1_gnn_W_conv', 'L1_gnn_b_conv', 'L1_gnn_Wq', 'L1_gnn_Wk', 'L1_gnn_Wv', 'L1_gnn_Wo',
        'L1_gnn_proj']


def kernel(**inputs):
    import numpy as _np
    import concourse.bacc as _bacc
    from concourse import mybir as _mybir
    from concourse.bass_utils import run_bass_kernel_spmd as _run

    nc = _bacc.Bacc("TRN2", target_bir_lowering=False, num_devices=1)
    arrays, args = {}, []
    for name in _INS:
        a = _np.ascontiguousarray(inputs[name])
        arrays[f"in_{name}_dram"] = a
        args.append(nc.dram_tensor(f"in_{name}_dram", a.shape, _mybir.dt.from_np(a.dtype), kind="ExternalInput").ap())
    args.append(nc.dram_tensor("out_0_dram", (N, D), _mybir.dt.float32, kind="ExternalOutput").ap())
    build(nc, *args)
    r = _run(nc, [arrays], core_ids=[0])
    return r.results[0]["out_0_dram"]
```
